# Optimizing a Trainium2 kernel written in Bass

```python
import numpy as np
import jax
import jax.numpy as jnp

def _softmax(x, axis=-1):
    return jax.nn.softmax(x, axis=axis)

def _gelu(x):
    return jax.nn.gelu(x, approximate=True)

def _silu(x):
    return jax.nn.silu(x)

def _sigmoid(x):
    return jax.nn.sigmoid(x)

def _layernorm(x, axis=-1, eps=1e-05):
    m = jnp.mean(x, axis=axis, keepdims=True)
    v = jnp.var(x, axis=axis, keepdims=True)
    return (x - m) / jnp.sqrt(v + eps)

def _scatter_add(tgt, idx, src, axis=0):
    return tgt.at[idx].add(src)

def _segment_sum(src, seg, n):
    return jax.ops.segment_sum(src, seg, n)
kernel_name = 'mk_xattn_ffn_d1_seqx_r2_e429dc'

def setup_inputs(seed: int=0):
    np.random.seed(seed)
    _w = jnp.asarray

    def _rec_inputs():
        import jax
        import jax.numpy as jnp
        _rk = jax.random.key(seed)
        x = -0.0002928 + 1 * jax.random.normal(jax.random.fold_in(_rk, 1), (2, 2048, 512), jnp.float32)
        _lenS = 2048 - jax.random.randint(jax.random.fold_in(_rk, 7), (2,), 0, max(1, 2048 // 4) + 1, jnp.int32)
        _lenS2 = 128 - jax.random.randint(jax.random.fold_in(_rk, 8), (2,), 0, max(1, 128 // 4) + 1, jnp.int32)
        _ctx_1024P = jax.random.normal(jax.random.fold_in(_rk, 11), (2, 16, 512), jnp.float32)
        _ctx_1024c = jax.random.dirichlet(jax.random.fold_in(_rk, 511), 0.3 * jnp.ones((16,), jnp.float32), (2, 128))
        _ctx_1024t = jnp.einsum('bsk,bkd->bsd', _ctx_1024c, _ctx_1024P)
        _ctx_1024t = _ctx_1024t * jax.lax.rsqrt(jnp.mean(jnp.square(_ctx_1024t)) + 1e-12) * 0.953939
        ctx_1024 = -1.39393e-06 + 0.999914 * (_ctx_1024t + 0.3 * jax.random.normal(jax.random.fold_in(_rk, 611), (2, 128, 512), jnp.float32))
        _validS = jnp.arange(2048)[None, :] < _lenS[:, None]
        _validS2 = jnp.arange(128)[None, :] < _lenS2[:, None]
        _causal = jnp.tril(jnp.ones((2048, 2048), dtype=bool))
        mask_Bx1x1xS2_ik0 = jnp.where(jnp.broadcast_to(_validS2[:, None, None, :], (2, 1, 1, 128)), 0, 1).astype(jnp.int32)
        return (x, ctx_1024, mask_Bx1x1xS2_ik0)
    x, ctx_1024, mask_Bx1x1xS2_ik0 = _rec_inputs()

    def _L0_xattn_setup():
        import jax, jax.numpy as jnp
        import numpy as np
        EMB = 512
        HEADS = 16
        HEAD_DIM = EMB // HEADS
        key = jax.random.key(seed)
        k1, k2, k3, k4, k5 = jax.random.split(key, 5)
        N, S = (2, 1024)
        query = jax.random.normal(k1, (N, S, EMB), dtype=jnp.float32)
        key_t = jax.random.normal(k2, (N, S, EMB), dtype=jnp.float32)
        values = jax.random.normal(k3, (N, S, EMB), dtype=jnp.float32)
        mask = jax.random.randint(k4, (N, 1, 1, S), 0, 2, dtype=jnp.int32)
        W_out = jax.random.normal(k5, (EMB, EMB), dtype=jnp.float32) * (1.0 / np.sqrt(EMB))
        return {'query': query, 'key': key_t, 'values': values, 'mask': mask, 'W_out': W_out}
    _L0_xattn_all = _L0_xattn_setup()
    _L0_xattn_in = {k: v for k, v in _L0_xattn_all.items() if k in ('W_out',)}
    del _L0_xattn_all

    def _L0_ffn_setup():
        import jax, jax.numpy as jnp
        import numpy as np
        B, T, D_MODEL = (4, 1024, 512)
        N_EXPERTS, TOP_K, D_EXPERT = (6, 2, 256)
        QUANT_TEMP = 0.3
        _ANCHOR_IDS = [63, 6, 0, 18, 45, 27]

        def _q6_idx_to_vertex(idx):
            bits = [idx >> 5 - b & 1 for b in range(6)]
            return [2.0 * b - 1.0 for b in bits]

        def _anchors():
            return jnp.asarray(np.array([_q6_idx_to_vertex(i) for i in _ANCHOR_IDS], dtype=np.float32))

        def _router(x, proj_w, anchors, routing_temp):
            z = jnp.einsum('btd,ed->bte', x, proj_w)
            q = jnp.tanh(z / QUANT_TEMP)
            dot = jnp.einsum('btd,ed->bte', q, anchors)
            hamming = (6.0 - dot) * 0.5
            logits = -hamming / jnp.clip(routing_temp, 0.1)
            topk_logits, topk_idx = jax.lax.top_k(logits, TOP_K)
            topk_w = jax.nn.softmax(topk_logits, axis=-1)
            onehot = jax.nn.one_hot(topk_idx, N_EXPERTS, dtype=x.dtype)
            expert_weights = jnp.einsum('btke,btk->bte', onehot, topk_w)
            return (expert_weights, q)
        key = jax.random.key(seed)
        k_x, k_p, k_w1, k_w2 = jax.random.split(key, 4)
        x = jax.random.normal(k_x, (B, T, D_MODEL), dtype=jnp.float32)
        proj_w = jax.random.normal(k_p, (6, D_MODEL), dtype=jnp.float32) * 0.02
        anchors = _anchors()
        routing_temp = jnp.array(1.0, dtype=jnp.float32)
        s1 = 1.0 / np.sqrt(D_MODEL)
        s2 = 1.0 / np.sqrt(D_EXPERT)
        w1 = jax.random.uniform(k_w1, (N_EXPERTS, D_MODEL, D_EXPERT), jnp.float32, -s1, s1)
        w2 = jax.random.uniform(k_w2, (N_EXPERTS, D_EXPERT, D_MODEL), jnp.float32, -s2, s2)
        return {'x': x, 'proj_w': proj_w, 'anchors': anchors, 'routing_temp': routing_temp, 'w1': w1, 'w2': w2}
    _L0_ffn_all = _L0_ffn_setup()
    _L0_ffn_in = {k: v for k, v in _L0_ffn_all.items() if k in ('proj_w', 'anchors', 'routing_temp', 'w1', 'w2')}
    del _L0_ffn_all
    return {'x': x, 'ctx_1024': ctx_1024, 'mask_Bx1x1xS2_ik0': mask_Bx1x1xS2_ik0, 'L0_xattn_W_out': _L0_xattn_in['W_out'], 'L0_ffn_proj_w': _L0_ffn_in['proj_w'], 'L0_ffn_anchors': _L0_ffn_in['anchors'], 'L0_ffn_routing_temp': _L0_ffn_in['routing_temp'], 'L0_ffn_w1': _L0_ffn_in['w1'], 'L0_ffn_w2': _L0_ffn_in['w2']}

def reference(x, ctx_1024, mask_Bx1x1xS2_ik0, L0_xattn_W_out, L0_ffn_proj_w, L0_ffn_anchors, L0_ffn_routing_temp, L0_ffn_w1, L0_ffn_w2):
    import jax
    import jax.numpy as jnp

    def _L0_xattn_ref(query, key, values, mask, W_out):
        import jax, jax.numpy as jnp
        import numpy as np
        EMB = 512
        HEADS = 16
        HEAD_DIM = EMB // HEADS
        N, Q, _ = query.shape
        K = key.shape[1]
        q = query.reshape(N, Q, HEADS, HEAD_DIM)
        k = key.reshape(N, K, HEADS, HEAD_DIM)
        v = values.reshape(N, K, HEADS, HEAD_DIM)
        energy = jnp.einsum('nqhd,nkhd->nhqk', q, k)
        energy = jnp.where(mask == 0, jnp.float32(-1e+20), energy)
        attn = jax.nn.softmax(energy / jnp.sqrt(jnp.float32(EMB)), axis=-1)
        out = jnp.einsum('nhqk,nkhd->nqhd', attn, v).reshape(N, Q, EMB)
        return out @ W_out.T

    def _L0_ffn_ref(x, proj_w, anchors, routing_temp, w1, w2):
        import jax, jax.numpy as jnp
        import numpy as np
        B, T, D_MODEL = (4, 1024, 512)
        N_EXPERTS, TOP_K, D_EXPERT = (6, 2, 256)
        QUANT_TEMP = 0.3
        _ANCHOR_IDS = [63, 6, 0, 18, 45, 27]

        def _q6_idx_to_vertex(idx):
            bits = [idx >> 5 - b & 1 for b in range(6)]
            return [2.0 * b - 1.0 for b in bits]

        def _anchors():
            return jnp.asarray(np.array([_q6_idx_to_vertex(i) for i in _ANCHOR_IDS], dtype=np.float32))

        def _router(x, proj_w, anchors, routing_temp):
            z = jnp.einsum('btd,ed->bte', x, proj_w)
            q = jnp.tanh(z / QUANT_TEMP)
            dot = jnp.einsum('btd,ed->bte', q, anchors)
            hamming = (6.0 - dot) * 0.5
            logits = -hamming / jnp.clip(routing_temp, 0.1)
            topk_logits, topk_idx = jax.lax.top_k(logits, TOP_K)
            topk_w = jax.nn.softmax(topk_logits, axis=-1)
            onehot = jax.nn.one_hot(topk_idx, N_EXPERTS, dtype=x.dtype)
            expert_weights = jnp.einsum('btke,btk->bte', onehot, topk_w)
            return (expert_weights, q)
        expert_weights, q = _router(x, proj_w, anchors, routing_temp)
        h = jax.nn.gelu(jnp.einsum('btd,edh->bteh', x, w1))
        out = jnp.einsum('bteh,ehd,bte->btd', h, w2, expert_weights)
        return out
    x = x + _L0_xattn_ref(_layernorm(x, axis=-1), ctx_1024, ctx_1024, mask_Bx1x1xS2_ik0, L0_xattn_W_out)
    x = x + _L0_ffn_ref(_layernorm(x, axis=-1), L0_ffn_proj_w, L0_ffn_anchors, L0_ffn_routing_temp, L0_ffn_w1, L0_ffn_w2)
    return x

_drawn_inputs = setup_inputs


def setup_inputs(seed=0):
    import zlib

    import numpy as np

    out = dict(_drawn_inputs(seed))
    spreads = {}
    factors = {}
    for name, (base, spread) in spreads.items():
        noise = np.random.default_rng([zlib.crc32(name.encode()), seed]).standard_normal(out[name].shape)
        drawn = base * np.exp(spread * noise) if base else spread * noise
        out[name] = jnp.asarray(drawn.astype(out[name].dtype))
    for name, factor in factors.items():
        out[name] = (out[name] * factor).astype(out[name].dtype)
    return out
```

```python
from contextlib import ExitStack

import concourse.bass as bass
from concourse import mybir

ALU = mybir.AluOpType
ACT = mybir.ActivationFunctionType
AX = mybir.AxisListType
F32 = mybir.dt.float32
F32R = mybir.dt.float32r
I32 = mybir.dt.int32

P = 128
HEADS, HD = 16, 32
EXPERTS, HID = 6, 256
LN_EPS = 1e-5
QUANT_TEMP = 0.3
MASKED = 1e20


def xattn_moe(nc, x, ctx_in, mask, w_out, proj_w, anchors, routing_temp, w1, w2, out):
    batches, seq, emb = x.shape
    keys = ctx_in.shape[1]
    kchunks = emb // P
    hpg = P // HD
    blk = 4 * P
    nblk = batches * seq // blk
    ntile = nblk * 4
    blk_per_batch = seq // blk
    scale = float(emb) ** -0.5
    halves = HID // P
    nch = EXPERTS * halves
    R_BIAS = 3 * HD
    R_MAX = R_BIAS + 2
    ROWS = R_MAX + 2

    x_t = x.rearrange("b (n t p) d -> (b n) t p d", t=4, p=P)
    out_t = out.rearrange("b (n t p) d -> (b n) t p d", t=4, p=P)

    def dram(name, shape, dt):
        return nc.dram_tensor(name, shape, dt, kind="Internal").ap()

    qhi_d = dram("qhi_d", [nblk, kchunks, P, blk], F32)
    qlo_d = dram("qlo_d", [nblk, kchunks, P, blk], F32)
    att_d = dram("att_d", [nblk, kchunks, P, 4 * P], F32)
    x2_d = dram("x2_d", [nblk, 4, P, emb], F32)
    x2t_d = dram("x2t_d", [nblk, P, kchunks, blk], F32)
    wt_d = dram("wt_d", [nblk, 4, EXPERTS, P], F32)

    ctx = ExitStack()
    with ctx:
        ctx.enter_context(nc.allow_non_contiguous_dma(reason="one mask value to a partition"))
        base = -(-nc.sbuf_base // 64) * 64
        cursor = [base]

        def size_of(shape):
            n = 4
            for s in shape[1:]:
                n *= s
            return -(-n // 64) * 64

        def sb(name, shape, dt=F32):
            at = cursor[0]
            cursor[0] += size_of(shape)
            return nc.alloc_sbuf_tensor_at(name, shape, dt, offset=at)

        ident = sb("ident", [P, P])
        vals = sb("vals", [P, batches * kchunks, P])
        ones = sb("ones", [P, HD])
        fold = sb("fold", [P, EXPERTS])
        projT = sb("projT", [P, kchunks, HD])
        anc = sb("anc", [P, EXPERTS, 6])
        tri = sb("tri", [P, EXPERTS, EXPERTS])
        temp = sb("temp", [P, 1])
        tclip = sb("tclip", [P, 1])
        tinv = sb("tinv", [P, 1])
        nhalf = sb("nhalf", [P, 4, 1])
        woH = sb("woH", [P, kchunks, emb], F32R)
        woL = sb("woL", [P, kchunks, emb], F32R)
        att_base = cursor[0]
        xin = sb("xin", [P, 4, emb])
        xhi = sb("xhi", [P, 2, emb])
        xlo = sb("xlo", [P, 2, emb])
        xn = sb("xn", [P, 2, emb])
        qth = sb("qth", [P, 2, kchunks, P])
        qtl = sb("qtl", [P, 2, kchunks, P])
        qst = sb("qst", [P, 4, hpg, blk], F32R)
        kst = sb("kst", [P, 4, hpg, keys], F32R)
        val = sb("val", [P, 4, P])
        prob = sb("prob", [P, 2, hpg, blk])
        lnden = sb("lnden", [P, blk])
        rden = sb("rden", [P, 2, blk])
        newton = sb("newton", [P, blk])
        atT = sb("atT", [P, 2, blk])
        mhl = sb("mhl", [2 * hpg, 2, blk])
        st1 = sb("st1", [P, 4, 6])
        mv1 = sb("mv1", [P, 4, 2])
        vare1 = sb("vare1", [P, 4, 1])
        rstd1 = sb("rstd1", [P, 4, 1])
        nmr1 = sb("nmr1", [P, 4, 1])
        nmax = sb("nmax", [P, 2, 4, hpg])
        nmhl = sb("nmhl", [P, 2, 4, 2 * hpg])
        cursor[0] = max(cursor[0], att_base + 4 * 2 * (EXPERTS * kchunks * HID + EXPERTS * halves * emb))
        att_end = cursor[0]
        attf = sb("attf", [P, kchunks, blk])
        atH = sb("atH", [P, kchunks, blk], F32R)
        atL = sb("atL", [P, kchunks, blk], F32R)
        xres = sb("xres", [P, 4, emb])
        mid_base = cursor[0]
        x2 = sb("x2", [P, 4, emb])
        xn2 = sb("xn2", [P, 4, emb])
        x2T = sb("x2T", [P, 4, kchunks, P])
        mid_end = cursor[0]
        wTs = sb("wTs", [4 * EXPERTS, P])
        st2 = sb("st2", [P, 4, 6])
        mv2 = sb("mv2", [P, 4, 2])
        vare2 = sb("vare2", [P, 4, 1])
        rstd2 = sb("rstd2", [P, 4, 1])
        mrs2 = sb("mrs2", [P, 4, 1])
        nmr2 = sb("nmr2", [P, 4, 1])
        zpart = sb("zpart", [P, blk])
        qr = sb("qr", [P, 4, 6])
        qa = sb("qa", [P, 4, EXPERTS, 6])
        dot = sb("dot", [P, 4, EXPERTS])
        lgs = sb("lgs", [P, 4, EXPERTS])
        gt = sb("gt", [P, 4, EXPERTS, EXPERTS])
        eq = sb("eq", [P, 4, EXPERTS, EXPERTS])
        rank = sb("rank", [P, 4, EXPERTS])
        lmax = sb("lmax", [P, 4])
        ldif = sb("ldif", [P, 4, EXPERTS])
        lexp = sb("lexp", [P, 4, EXPERTS])
        wsel = sb("wsel", [P, 4, EXPERTS])
        wsum = sb("wsum", [P, 4])
        winv = sb("winv", [P, 4])
        wgt = sb("wgt", [P, 4, EXPERTS])
        spare = cursor[0]
        maski = sb("maski", [P, batches, 1], I32)
        m01 = sb("m01", [P, batches, 1])
        bias = sb("bias", [P, batches, 1])
        bhi = sb("bhi", [P, batches, 1])
        blo = sb("blo", [P, batches, 1])
        pjraw = sb("pjraw", [EXPERTS, emb])
        cursor[0] = att_end
        ctok = sb("ctok", [P, batches, emb])
        kmask = sb("kmask", [P, batches, emb])
        ktok = sb("ktok", [P, batches, HEADS, P])
        woraw = sb("woraw", [P, kchunks, emb])
        assert cursor[0] <= mid_base
        cursor[0] = mid_base
        kss = sb("kss", [P, batches * kchunks, 6 * keys], F32R)
        assert cursor[0] <= mid_end
        cursor[0] = att_base
        w1H = sb("w1H", [P, EXPERTS, kchunks, HID], F32R)
        w1L = sb("w1L", [P, EXPERTS, kchunks, HID], F32R)
        w2H = sb("w2H", [P, EXPERTS, halves, emb], F32R)
        w2L = sb("w2L", [P, EXPERTS, halves, emb], F32R)
        assert cursor[0] <= att_end
        cursor[0] = spare
        wraw = sb("wraw", [P, 2, kchunks * HID])
        wbc = sb("wbc", [P, EXPERTS, blk])
        assert cursor[0] <= nc.sbuf_usable_end
        cursor[0] = att_end
        xH = sb("xH", [P, kchunks, blk], F32R)
        xL = sb("xL", [P, kchunks, blk], F32R)
        gel = sb("gel", [P, 2, blk])
        hw = sb("hw", [P, 2, blk])
        hH = sb("hH", [P, 4, blk], F32R)
        hL = sb("hL", [P, 4, blk], F32R)
        yres = sb("yres", [P, 4, emb])
        x2tf = sb("x2tf", [P, kchunks, blk])
        assert cursor[0] <= mid_end

        ps = ctx.enter_context(nc.psum_tensor("ps", [P, 8, 512], F32))
        B_TH, B_TL, B_MX, B_SC, B_NUM, B_DEN = 0, 1, 2, 4, 6, 7
        B_OUT, B_T2, B_Z, B_ZP = 0, 4, 6, 7
        WT0 = P
        B_UP, B_Y = 0, 4

        def sem(name):
            return ctx.enter_context(nc.semaphore(name))

        def sems(name, n):
            return [sem(f"{name}{k}") for k in range(n)]

        s_load = sem("s_load")
        s_ident, s_const, s_ktok0, s_row1 = sem("s_ident"), sem("s_const"), sem("s_ktok0"), sem("s_row1")
        s_set = sem("s_set")
        s_ktok = sem("s_ktok")
        s_kT, s_kss, s_vals, s_gap = sem("s_kT"), sem("s_kss"), sem("s_vals"), sem("s_gap")
        s_woT, s_woH, s_woL = sem("s_woT"), sem("s_woH"), sem("s_woL")
        s_pjT, s_pj = sem("s_pjT"), sem("s_pj")
        s_pool, s_dve, s_sync = sem("s_pool"), sem("s_dve"), sem("s_sync")
        x_in = sems("x_in", 4)
        st_done, mv_done = sem("st_done"), sem("mv_done")
        rstd_done, nmr_done = sem("rstd_done"), sem("nmr_done")
        xhi_done, xn_done, xlo_done = sem("xhi_done"), sem("xn_done"), sem("xlo_done")
        th_ready, tl_ready = sem("th_ready"), sem("tl_ready")
        qth_done, qtl_done = sem("qth_done"), sem("qtl_done")
        q_out = sems("q_out", 4)
        q_in = sems("q_in", 4)
        kv_in = sems("kv_in", 4)
        mx_ready, mx_done = sem("mx_ready"), sem("mx_done")
        nmh_done, nml_done = sem("nmh_done"), sem("nml_done")
        mt_ready, mt_done = sem("mt_ready"), sem("mt_done")
        m_in = sems("m_in", 4)
        sc_ready, exp_done = sem("sc_ready"), sem("exp_done")
        pv_done, sums_ready, den_done, rec_done, newton_done, at_done = (
            sem("pv_done"), sem("sums_ready"), sem("den_done"), sem("rec_done"), sem("newton_done"), sem("at_done"))
        at_out = sems("at_out", 4)
        att_in = sems("att_in", 4)
        xr_in, atH_done, atL_done = sem("xr_in"), sem("atH_done"), sem("atL_done")
        wo_done, out_ready, add_done = sem("wo_done"), sem("out_ready"), sem("add_done")
        st2_done, mv2_done, rs2_done, xn2_done = sem("st2_done"), sem("mv2_done"), sem("rs2_done"), sem("xn2_done")
        nmr2_done, zp_ready, zp_done = sem("nmr2_done"), sem("zp_ready"), sem("zp_done")
        t2_ready, t2_done = sem("t2_ready"), sem("t2_done")
        x2_out, x2t_out = sem("x2_out"), sems("x2t_out", 4)
        z_ready, q_done, rt, rw, ldif_done, lexp_done, w_done = (
            sem("z_ready"), sem("q_done"), sem("rt"), sem("rw"), sem("ldif_done"), sem("lexp_done"), sem("w_done"))
        wt_ready, wt_done, wt_out = sem("wt_ready"), sem("wt_done"), sem("wt_out")
        wr_in, wH_done, wL_done = sem("wr_in"), sem("wH_done"), sem("wL_done")
        xt_in, xH_done, xL_done = sem("xt_in"), sem("xH_done"), sem("xL_done")
        wb_in = sems("wb_in", EXPERTS)
        up_ready, gel_done, hw_done = sem("up_ready"), sem("gel_done"), sem("hw_done")
        hH_done, hL_done, dn_done = sem("hH_done"), sem("hL_done"), sem("dn_done")
        yr_in, y_ready, y_done, y_out = sem("yr_in"), sem("y_ready"), sem("y_done"), sem("y_out")

        block = ctx.enter_context(nc.Block())

        def after(eng, semaphore, count):
            if not isinstance(count, int) or count > 0:
                eng.wait_ge(semaphore, count)

        def apart(eng, tick):
            eng.sem_inc(tick, 1)

        def live(v, n):
            return not isinstance(v, int) or 0 <= v < n

        def at(i, s, lag):
            return 4 * i + (s - lag), i + (s - lag) // 4, (s - lag) % 4

        L_LOAD, L_STAT, L_NORM, L_TR = -2, 0, 1, 2
        L_UNIT, L_KV, L_MAX, L_MT, L_SC, L_PV, L_DIV, L_STORE = 6, 8, 8, 9, 10, 11, 12, 13
        SP_AHEAD = 2

        def attention_loop(eng, step, last):
            def iteration(i):
                for s in range(4):
                    step(i, s)
            for i in range(4):
                iteration(i)
            with eng.Fori(4, nblk) as i:
                iteration(i)
            for i in range(nblk, nblk + -(-last // 4) + 1):
                iteration(i)

        def middle_loop(eng, body):
            for i in range(3):
                body(i)
            with eng.Fori(3, nblk - 1) as i:
                body(i)
            for i in range(nblk - 1, nblk + 2):
                body(i)

        def expert_loop(eng, body):
            body(0)
            with eng.Fori(1, nblk - 1) as i:
                body(i)
            body(nblk - 1)

        N_SETUP_LOADS = 1 + batches + 4

        @block.sync
        def _(sp):
            sp.dma_start(ctok[:], ctx_in.rearrange("b k d -> k b d")).then_inc(s_load, 16)
            for b in range(batches):
                sp.dma_start(maski[:, b, :], mask[b, 0, :, :].rearrange("a k -> k a")).then_inc(s_load, 16)
            sp.dma_start(woraw[:], w_out.rearrange("(c p) d -> p c d", p=P)).then_inc(s_load, 16)
            sp.dma_start(pjraw[:], proj_w).then_inc(s_load, 16)
            sp.dma_start(anc[:], anchors.partition_broadcast(P)).then_inc(s_load, 16)
            sp.dma_start(temp[:], routing_temp.partition_broadcast(P)).then_inc(s_load, 16)

            def step(i, s):
                w, n, t = at(i, s, 0)
                if live(w, ntile):
                    after(sp, xhi_done, w - 3)
                    after(sp, xn_done, w - 3)
                    sp.dma_start(xin[:, t, :], x_t[n, t, :, :]).then_inc(x_in[t], 16)
                m, n, g = at(i, s, L_MT + SP_AHEAD)
                if live(m, ntile):
                    sp.wait_ge(mt_done, m + 1)
                    sp.dma_start(qst[R_MAX:R_MAX + 2, g, :, :].bitcast(F32), mhl[:, g % 2, :]).then_inc(m_in[g], 16)
                u, n, g = at(i, s, L_KV + SP_AHEAD)
                if live(u, ntile):
                    stack = (n // blk_per_batch) * kchunks + g
                    if isinstance(u, int) and u == 0:
                        sp.wait_ge(s_kss, batches * kchunks)
                        sp.wait_ge(s_vals, 1)
                    after(sp, pv_done, u - 3)
                    for a in range(2):
                        pair = kss[:, stack, 3 * keys * a:3 * keys * (a + 1)].rearrange("p (c k) -> p c k", c=3)
                        sp.dma_start(kst[:, g, 2 * a:2 * a + 2, :].bitcast(F32), pair[:, 0:3:2, :].bitcast(F32))\
                          .then_inc(kv_in[g], 16)
                    sp.dma_start(val[:, g, :], vals[:, stack, :]).then_inc(kv_in[g], 16)
                v, n, g = at(i, s, L_STORE + SP_AHEAD)
                if live(v, ntile):
                    sp.wait_ge(at_done, v + 1)
                    sp.dma_start(att_d[n, g, :, :], atT[:, g % 2, :]).then_inc(at_out[g], 16)
                u, n, g = at(i, s, L_UNIT + SP_AHEAD)
                if live(u, ntile):
                    if isinstance(u, int) and u == 0:
                        sp.wait_ge(s_row1, 1)
                    for k in range(4):
                        sp.wait_ge(q_out[k], 32 * (n + 1))
                    apart(sp, s_sync)
                    after(sp, sc_ready, hpg * (u - 3))
                    q3 = qhi_d[n, g, :, :].rearrange("(h r) t -> r h t", r=HD)
                    sp.dma_start(qst[0:HD, g, :, :].bitcast(F32), q3).then_inc(q_in[g], 16)
                    sp.dma_start(qst[2 * HD:3 * HD, g, :, :].bitcast(F32), q3).then_inc(q_in[g], 16)
                    sp.dma_start(qst[HD:2 * HD, g, :, :].bitcast(F32),
                                 qlo_d[n, g, :, :].rearrange("(h r) t -> r h t", r=HD)).then_inc(q_in[g], 16)
                w, n, t = at(i, s, L_TR + SP_AHEAD)
                if live(w, ntile):
                    sp.wait_ge(qth_done, w + 1)
                    sp.dma_start(qhi_d[n, :, :, t * P:(t + 1) * P].rearrange("k p t -> p k t"), qth[:, t % 2, :, :])\
                      .then_inc(q_out[t], 16)
                    sp.wait_ge(qtl_done, w + 1)
                    sp.dma_start(qlo_d[n, :, :, t * P:(t + 1) * P].rearrange("k p t -> p k t"), qtl[:, t % 2, :, :])\
                      .then_inc(q_out[t], 16)

            attention_loop(sp, step, L_STORE + SP_AHEAD)

            for g in range(4):
                sp.wait_ge(at_out[g], 16 * nblk)

            def middle(i):
                if live(i, nblk):
                    for g in range(4):
                        after(sp, atL_done, 4 * (i - 1) + g + 1)
                        sp.dma_start(attf[:, g, :], att_d[i, g, :, :]).then_inc(att_in[g], 16)
                    after(sp, add_done, 4 * i)
                    sp.dma_start(xres[:], x_t[i, :, :, :].rearrange("t p d -> p t d")).then_inc(xr_in, 16)
                if not isinstance(i, int) or 1 <= i <= EXPERTS:
                    e = i - 1
                    sp.wait_ge(add_done, 4)
                    after(sp, wL_done, 2 * e)
                    sp.dma_start(wraw[:, 0, :].rearrange("p (k h) -> p k h", k=kchunks),
                                 w1[e, :, :].rearrange("(k p) h -> p k h", p=P)).then_inc(wr_in, 16)
                    sp.dma_start(wraw[:, 1, :].rearrange("p (j d) -> p j d", j=halves),
                                 w2[e, :, :].rearrange("(j p) d -> p j d", p=P)).then_inc(wr_in, 16)
                n = i - 1
                if live(n, nblk):
                    sp.wait_ge(add_done, 4 * n + 4)
                    sp.dma_start(x2_d[n, :, :, :].rearrange("t p d -> p t d"), x2[:]).then_inc(x2_out, 16)

            middle_loop(sp, middle)

            sp.wait_ge(x2_out, 16 * nblk)
            for t in range(4):
                sp.wait_ge(x2t_out[t], 16 * nblk)
            sp.wait_ge(wt_out, 16 * nblk)

            def load_rows(i):
                after(sp, xL_done, 2 * i)
                sp.dma_start(x2tf[:], x2t_d[i, :, :, :]).then_inc(xt_in, 16)

            def load_weights(i):
                for e in range(EXPERTS):
                    after(sp, hw_done, nch * (i - 1) + halves * (e + 1))
                    sp.dma_start(wbc[:, e, :].rearrange("p (t k) -> p t k", t=4), wt_d[i, :, e, :].partition_broadcast(P)).then_inc(wb_in[e], 16)

            def experts(i):
                after(sp, y_out, 64 * i)
                sp.dma_start(yres[:], x2_d[i, :, :, :].rearrange("t p d -> p t d")).then_inc(yr_in, 16)
                if not isinstance(i, int) or i < nblk - 1:
                    load_rows(i + 1)
                    load_weights(i + 1)
                for t in range(4):
                    sp.wait_ge(y_done, 4 * i + t + 1)
                    sp.dma_start(out_t[i, t, :, :], yres[:, t, :]).then_inc(y_out, 16)

            load_rows(0)
            load_weights(0)
            expert_loop(sp, experts)
            sp.wait_ge(y_out, 64 * nblk)

        @block.gpsimd
        def _(pool):
            nc.gpsimd.memset(ident[:], 0.0).then_inc(s_ident, 1)
            pool.wait_ge(s_ident, 1)
            nc.gpsimd.affine_select(out=ident[:], in_=ident[:], compare_op=ALU.not_equal, fill=1.0, base=0,
                                    pattern=[[-1, P]], channel_multiplier=1).then_inc(s_ident, 1)
            nc.gpsimd.memset(ktok[:], 0.0).then_inc(s_ktok0, 1)
            nc.gpsimd.memset(kss[:].rearrange("p s (a c k) -> p s a c k", a=2, c=3)[:, :, :, 1, :].bitcast(F32), 0.0)\
              .then_inc(s_gap, 1)
            nc.gpsimd.memset(ones[:], 1.0).then_inc(s_gap, 1)
            nc.gpsimd.memset(projT[:], 0.0).then_inc(s_gap, 1)
            nc.gpsimd.memset(fold[:], 0.0).then_inc(s_gap, 1)
            pool.wait_ge(s_gap, 4)
            for c in range(kchunks):
                nc.gpsimd.affine_select(out=fold[:], in_=fold[:], compare_op=ALU.not_equal, fill=1.0, base=-HD * c,
                                        pattern=[[-1, EXPERTS]], channel_multiplier=1).then_inc(s_gap, 1)
                pool.wait_ge(s_gap, 5 + c)
            nc.gpsimd.memset(nhalf[:], -0.5).then_inc(s_const, 1)
            nc.gpsimd.memset(tri[:], 0.0).then_inc(s_const, 1)
            pool.wait_ge(s_const, 2)
            nc.gpsimd.affine_select(out=tri[:], in_=tri[:], compare_op=ALU.is_ge, fill=1.0, base=0,
                                    pattern=[[-1, EXPERTS], [1, EXPERTS]], channel_multiplier=0).then_inc(s_const, 1)
            pool.wait_ge(s_ktok0, 1)
            nc.gpsimd.memset(ktok[:, :, :, R_MAX:R_MAX + 2], 1.0).then_inc(s_ktok0, 1)
            pool.wait_ge(s_ktok0, 2)
            nc.gpsimd.memset(qst[R_BIAS:R_BIAS + 2, :, :, :].bitcast(F32), 1.0).then_inc(s_row1, 1)
            pool.wait_ge(s_row1, 1)

            def step(i, s):
                w, n, t = at(i, s, L_STAT)
                if live(w, ntile):
                    pool.wait_ge(mv_done, w + 1)
                    after(pool, xhi_done, w - 3)
                    apart(pool, s_pool)
                    nc.gpsimd.tensor_scalar(vare1[:, t, :], mv1[:, t, 1:2], LN_EPS, None, ALU.add).then_inc(rstd_done, 1)
                    pool.wait_ge(rstd_done, 2 * w + 1)
                    nc.gpsimd.tensor_tensor(rstd1[:, t, :], vare1[:, t, :], nhalf[:, 0, :], ALU.pow).then_inc(rstd_done, 1)
                    pool.wait_ge(rstd_done, 2 * w + 2)
                    apart(pool, s_pool)
                    nc.gpsimd.tensor_scalar(nmr1[:, t, :], mv1[:, t, 0:1], rstd1[:, t, :], -1.0, ALU.mult, ALU.mult)\
                      .then_inc(nmr_done, 1)
                v, n, g = at(i, s, L_MAX)
                if live(v, ntile):
                    pool.wait_ge(mx_done, 4 * v + 4)
                    after(pool, mt_ready, v - 1)
                    apart(pool, s_pool)
                    nc.gpsimd.tensor_scalar(nmhl[:, g % 2, :, 0:hpg].bitcast(F32R), nmax[:, g % 2, :, :], 1.0, None,
                                            ALU.mult).then_inc(nmh_done, 1)
                    pool.wait_ge(nmh_done, v + 1)
                    nc.gpsimd.tensor_tensor(nmhl[:, g % 2, :, hpg:2 * hpg].bitcast(F32R), nmax[:, g % 2, :, :],
                                            nmhl[:, g % 2, :, 0:hpg], ALU.subtract).then_inc(nml_done, 1)
                w, n, t = at(i, s, L_NORM)
                if live(w, ntile):
                    pool.wait_ge(xn_done, w + 1)
                    pool.wait_ge(xhi_done, w + 1)
                    after(pool, tl_ready, w - 1)
                    nc.gpsimd.tensor_tensor(xlo[:, t % 2, :].bitcast(F32R), xn[:, t % 2, :], xhi[:, t % 2, :], ALU.subtract)\
                      .then_inc(xlo_done, 1)

            attention_loop(pool, step, L_MAX)

            def middle(i):
                n = i - 1
                if live(n, nblk):
                    pool.wait_ge(mv2_done, 4 * n + 4)
                    after(pool, xn2_done, 4 * n)
                    apart(pool, s_pool)
                    nc.gpsimd.tensor_scalar(vare2[:], mv2[:, :, 1:2], LN_EPS, None, ALU.add).then_inc(rs2_done, 1)
                    pool.wait_ge(rs2_done, 3 * n + 1)
                    nc.gpsimd.tensor_tensor(rstd2[:], vare2[:], nhalf[:], ALU.pow).then_inc(rs2_done, 1)
                    pool.wait_ge(rs2_done, 3 * n + 2)
                    nc.gpsimd.tensor_tensor(mrs2[:], mv2[:, :, 0:1], rstd2[:], ALU.mult).then_inc(rs2_done, 1)
                    pool.wait_ge(rs2_done, 3 * n + 3)
                    apart(pool, s_pool)
                    nc.gpsimd.tensor_scalar(nmr2[:], mrs2[:], -1.0, None, ALU.mult).then_inc(nmr2_done, 1)
                if not isinstance(i, int) or 1 <= i <= EXPERTS:
                    e = i - 1
                    pool.wait_ge(wH_done, 2 * e + 1)
                    apart(pool, s_pool)
                    nc.gpsimd.tensor_tensor(w1L[:, e, :, :], wraw[:, 0, :].rearrange("p (k h) -> p k h", k=kchunks),
                                            w1H[:, e, :, :], ALU.subtract).then_inc(wL_done, 1)
                    pool.wait_ge(wH_done, 2 * e + 2)
                    apart(pool, s_pool)
                    nc.gpsimd.tensor_tensor(w2L[:, e, :, :], wraw[:, 1, :].rearrange("p (j d) -> p j d", j=halves),
                                            w2H[:, e, :, :], ALU.subtract).then_inc(wL_done, 1)

            middle_loop(pool, middle)

        @block.scalar
        def _(act):
            for k in range(batches * kchunks):
                act.wait_ge(s_kT, k + 1)
                nc.scalar.activation(kss[:, k, :].rearrange("p (a c k) -> p a c k", a=2, c=3)[:, :, 0:3:2, :],
                                     ps[:, k, :].rearrange("p (a h k) -> p a h k", a=2, h=2), ACT.Copy).then_inc(s_kss, 1)
            for c in range(kchunks):
                act.wait_ge(s_woT, c + 1)
                nc.scalar.activation(woH[:, c, :], ps[:, c, :], ACT.Copy).then_inc(s_woH, 1)
            act.wait_ge(s_pjT, 1)
            act.wait_ge(s_gap, 3)
            nc.scalar.activation(projT[:, :, 0:EXPERTS], ps[:, 4, 0:kchunks * EXPERTS].rearrange("p (k e) -> p k e", k=kchunks),
                                 ACT.Copy).then_inc(s_pj, 1)

            def exps(v, g, heads):
                for h in heads:
                    act.wait_ge(sc_ready, hpg * v + h + 1)
                    after(act, pv_done, v - 1)
                    nc.scalar.activation(prob[:, g % 2, h, :], ps[:, B_SC + h % 2, :], ACT.Exp, scale=scale)\
                      .then_inc(exp_done, 1)

            def step(i, s):
                v, n, g = at(i, s, L_SC)
                if live(v, ntile):
                    exps(v, g, (0, 1))
                m, mn, mg = at(i, s, L_MT)
                if live(m, ntile):
                    _, pn, pg = at(i, s, L_MT + 2)
                    act.wait_ge(mt_ready, m + 1)
                    after(act, m_in[pg], 16 * (pn + 1))
                    nc.scalar.activation(mhl[:, mg % 2, :], ps[0:2 * hpg, B_TL, :], ACT.Copy).then_inc(mt_done, 1)
                if live(v, ntile):
                    exps(v, g, (2, 3))
                f, fn, ft = at(i, s, L_NORM)
                if live(f, ntile):
                    act.wait_ge(nmr_done, f + 1)
                    act.wait_ge(x_in[ft], 16 * (fn + 1))
                    after(act, th_ready, f - 1)
                    after(act, xlo_done, f - 1)
                    nc.scalar.activation(xhi[:, ft % 2, :].bitcast(F32R), xin[:, ft, :], ACT.Identity,
                                         bias=nmr1[:, ft, :], scale=rstd1[:, ft, :]).then_inc(xhi_done, 1)
                w, wn, wt = at(i, s, L_TR)
                if live(w, ntile):
                    _, pn, pt = at(i, s, L_TR + 2)
                    act.wait_ge(th_ready, w + 1)
                    after(act, q_out[pt], 32 * (pn + 1))
                    nc.scalar.activation(qth[:, wt % 2, :, :], ps[:, B_TH, :].rearrange("p (k t) -> p k t", k=kchunks),
                                         ACT.Copy).then_inc(qth_done, 1)
                    act.wait_ge(tl_ready, w + 1)
                    nc.scalar.activation(qtl[:, wt % 2, :, :], ps[:, B_TL, :].rearrange("p (k t) -> p k t", k=kchunks),
                                         ACT.Copy).then_inc(qtl_done, 1)
                d, dn, dg = at(i, s, L_PV)
                if live(d, ntile):
                    act.wait_ge(sums_ready, d + 1)
                    after(act, rec_done, d)
                    nc.scalar.activation(lnden[:], ps[:, B_DEN, :], ACT.Ln).then_inc(den_done, 1)
                    act.wait_ge(den_done, d + 1)
                    after(act, newton_done, 2 * (d - 1))
                    nc.scalar.activation(rden[:, dg % 2, :], lnden[:], ACT.Exp, scale=-1.0).then_inc(rec_done, 1)

            nc.scalar.preload_act_table_set("natural_log_exp_and_others")
            attention_loop(act, step, L_PV)

            def split(i, g):
                if live(i, nblk):
                    act.wait_ge(att_in[g], 16 * (i + 1))
                    if g < 3:
                        after(act, wo_done, 3 * (i - 1) + g + 1)
                    else:
                        after(act, out_ready, 4 * i)
                    nc.scalar.activation(atH[:, g, :], attf[:, g, :], ACT.Copy).then_inc(atH_done, 1)

            def normalise(n, t):
                if live(n, nblk):
                    act.wait_ge(nmr2_done, n + 1)
                    after(act, t2_ready, 4 * (n - 1) + t + 1)
                    nc.scalar.activation(xn2[:, t, :], x2[:, t, :], ACT.Identity, bias=nmr2[:, t, :], scale=rstd2[:, t, :])\
                      .then_inc(xn2_done, 1)

            def rows_out(n, t):
                if live(n, nblk):
                    act.wait_ge(t2_ready, 4 * n + t + 1)
                    after(act, zp_ready, n)
                    after(act, x2t_out[t], 16 * n)
                    nc.scalar.activation(x2T[:, t, :, :],
                                         ps[:, B_T2 + t % 2, :].rearrange("p (k t) -> p k t", k=kchunks), ACT.Copy)\
                      .then_inc(t2_done, 1)
                    act.wait_ge(t2_done, 4 * n + t + 1)
                    act.dma_start(x2t_d[n, :, :, t * P:(t + 1) * P], x2T[:, t, :, :]).then_inc(x2t_out[t], 16)

            def middle(i):
                n = i - 2
                if live(n, nblk):
                    act.wait_ge(zp_ready, n + 1)
                    after(act, z_ready, n)
                    nc.scalar.activation(zpart[:], ps[:, B_ZP, :], ACT.Copy).then_inc(zp_done, 1)
                    act.wait_ge(z_ready, n + 1)
                    after(act, w_done, n)
                    nc.scalar.activation(qr[:], ps[:, B_Z, 0:4 * 6].rearrange("p (t d) -> p t d", t=4), ACT.Tanh,
                                         scale=1.0 / QUANT_TEMP).then_inc(q_done, 1)
                split(i + 1, 0)
                if live(n, nblk):
                    act.wait_ge(ldif_done, n + 1)
                    nc.scalar.activation(lexp[:], ldif[:], ACT.Exp).then_inc(lexp_done, 1)
                if not isinstance(i, int) or 1 <= i <= EXPERTS:
                    e = i - 1
                    act.wait_ge(wr_in, 32 * e + 32)
                    nc.scalar.activation(w1H[:, e, :, :], wraw[:, 0, :].rearrange("p (k h) -> p k h", k=kchunks), ACT.Copy)\
                      .then_inc(wH_done, 1)
                    nc.scalar.activation(w2H[:, e, :, :], wraw[:, 1, :].rearrange("p (j d) -> p j d", j=halves), ACT.Copy)\
                      .then_inc(wH_done, 1)
                normalise(i - 1, 0)
                normalise(i - 1, 1)
                split(i + 1, 1)
                rows_out(i - 1, 0)
                normalise(i - 1, 2)
                rows_out(i - 1, 1)
                normalise(i - 1, 3)
                split(i + 1, 2)
                rows_out(i - 1, 2)
                rows_out(i - 1, 3)
                if live(n, nblk):
                    act.wait_ge(wt_ready, n + 1)
                    after(act, wt_out, 16 * n)
                    nc.scalar.activation(wTs[:], ps[0:4 * EXPERTS, B_Z, WT0:WT0 + P], ACT.Copy).then_inc(wt_done, 1)
                    act.wait_ge(wt_done, n + 1)
                    act.dma_start(wt_d[n, :, :, :].rearrange("t e p -> (t e) p"), wTs[:]).then_inc(wt_out, 16)
                split(i + 1, 3)

            for g in range(4):
                split(0, g)
            middle_loop(act, middle)

            def split_rows(i):
                act.wait_ge(xt_in, 16 * (i + 1))
                after(act, up_ready, nch * i)
                for c in range(0, kchunks, 2):
                    nc.scalar.activation(xH[:, c:c + 2, :], x2tf[:, c:c + 2, :], ACT.Copy).then_inc(xH_done, 1)

            def experts(i):
                def gelu(c):
                    act.wait_ge(up_ready, nch * i + c + 1)
                    after(act, hw_done, nch * i + c - 1)
                    nc.scalar.activation(gel[:, c % 2, :], ps[:, B_UP + c % 4, :], ACT.Gelu_apprx_tanh).then_inc(gel_done, 1)

                def high(c):
                    act.wait_ge(hw_done, nch * i + c + 1)
                    if c >= 4:
                        act.wait_ge(dn_done, (nch - 1) * i + c - 3)
                    elif c < 3:
                        after(act, dn_done, (nch - 1) * (i - 1) + c + 9)
                    else:
                        after(act, y_ready, 4 * i)
                    nc.scalar.activation(hH[:, c % 4, :], hw[:, c % 2, :], ACT.Copy).then_inc(hH_done, 1)

                for c in range(nch):
                    gelu(c)
                    if c >= 1:
                        high(c - 1)
                high(nch - 1)
                if not isinstance(i, int) or i < nblk - 1:
                    split_rows(i + 1)

            split_rows(0)
            expert_loop(act, experts)

        @block.vector
        def _(dve):
            dve.wait_ge(s_load, 16 * N_SETUP_LOADS)
            chain = [0]

            def link(ins):
                chain[0] += 1
                ins.then_inc(s_set, 1)
                dve.wait_ge(s_set, chain[0])

            link(nc.vector.tensor_scalar(m01[:], maski[:], 0.0, None, ALU.not_equal))
            link(nc.vector.tensor_scalar(bias[:], m01[:], -1.0, MASKED, ALU.add, ALU.mult))
            link(nc.vector.tensor_copy(bhi[:].bitcast(F32R), bias[:]))
            link(nc.vector.tensor_tensor(blo[:].bitcast(F32R), bias[:], bhi[:], ALU.subtract))
            dve.wait_ge(s_ktok0, 2)
            for b in range(batches):
                link(nc.vector.tensor_scalar(kmask[:, b, :], ctok[:, b, :], m01[:, b, :], None, ALU.mult))
                km = kmask[:, b, :].rearrange("k (h d) -> k h d", h=HEADS)
                nc.vector.tensor_copy(ktok[:, b, :, HD:2 * HD].bitcast(F32R), km).then_inc(s_ktok, 1)
                link(nc.vector.tensor_copy(ktok[:, b, :, 0:HD].bitcast(F32R), km))
                nc.vector.tensor_tensor(ktok[:, b, :, 2 * HD:3 * HD].bitcast(F32R), km, ktok[:, b, :, 0:HD], ALU.subtract)\
                  .then_inc(s_ktok, 1)
                nc.vector.tensor_copy(ktok[:, b, :, R_BIAS:R_BIAS + 1], bhi[:, b, :].unsqueeze(1).to_broadcast([P, HEADS, 1]))\
                  .then_inc(s_ktok, 1)
                nc.vector.tensor_copy(ktok[:, b, :, R_BIAS + 1:R_BIAS + 2],
                                      blo[:, b, :].unsqueeze(1).to_broadcast([P, HEADS, 1])).then_inc(s_ktok, 1)
            nc.vector.tensor_copy(vals[:], ctok[:].rearrange("k b (g c) -> k (b g) c", g=kchunks)).then_inc(s_vals, 1)
            link(nc.vector.tensor_scalar(tclip[:], temp[:], 0.1, None, ALU.max))
            link(nc.vector.reciprocal(tinv[:], tclip[:]))
            for c in range(kchunks):
                dve.wait_ge(s_woH, c + 1)
                nc.vector.tensor_tensor(woL[:, c, :], ps[:, c, :], woH[:, c, :], ALU.subtract).then_inc(s_woL, 1)

            def maxima(v, g, tiles):
                for t in tiles:
                    dve.wait_ge(mx_ready, 4 * v + t + 1)
                    after(dve, nml_done, v - 1)
                    nc.vector.tensor_reduce(nmax[:, g % 2, t, :],
                                            ps[:, B_MX + t % 2, :].rearrange("p (h k) -> p h k", h=hpg),
                                            axis=AX.X, op=ALU.max, negate=True).then_inc(mx_done, 1)

            def step(i, s):
                d, dn, dg = at(i, s, L_DIV)
                v, n, g = at(i, s, L_MAX)
                if live(d, ntile):
                    dve.wait_ge(rec_done, d + 1)
                    after(dve, at_done, d)
                    nc.vector.tensor_tensor(newton[:], ps[:, B_DEN, :], rden[:, dg % 2, :], ALU.mult).then_inc(newton_done, 1)
                    dve.wait_ge(newton_done, 2 * d + 1)
                    nc.vector.scalar_tensor_tensor(newton[:], newton[:], 2.0, rden[:, dg % 2, :], ALU.subtract, ALU.mult)\
                      .then_inc(newton_done, 1)
                if live(v, ntile):
                    maxima(v, g, (0,))
                if live(d, ntile):
                    _, pn, pg = at(i, s, L_DIV + 2)
                    dve.wait_ge(newton_done, 2 * d + 2)
                    dve.wait_ge(pv_done, d + 1)
                    after(dve, at_out[pg], 16 * (pn + 1))
                    nc.vector.scalar_tensor_tensor(atT[:, dg % 2, :], ps[:, B_NUM, :], -1.0, newton[:], ALU.mult, ALU.mult)\
                      .then_inc(at_done, 1)
                if live(v, ntile):
                    maxima(v, g, (1,))
                w, wn, t = at(i, s, L_STAT)
                if live(w, ntile):
                    dve.wait_ge(x_in[t], 16 * (wn + 1))
                    after(dve, mv_done, w - 3)
                    nc.vector.bn_stats(st1[:, t, :], xin[:, t, :]).then_inc(st_done, 1)
                f, fn, ft = at(i, s, L_NORM)
                if live(f, ntile):
                    dve.wait_ge(rstd_done, 2 * f + 2)
                    after(dve, xlo_done, f - 1)
                    nc.vector.tensor_scalar(xn[:, ft % 2, :], xin[:, ft, :], mv1[:, ft, 0:1], rstd1[:, ft, :],
                                            ALU.subtract, ALU.mult).then_inc(xn_done, 1)
                if live(w, ntile):
                    dve.wait_ge(st_done, w + 1)
                    after(dve, xn_done, w - 3)
                    apart(dve, s_dve)
                    nc.vector.bn_aggr(mv1[:, t, :], st1[:, t, :]).then_inc(mv_done, 1)
                if live(v, ntile):
                    maxima(v, g, (2, 3))

            attention_loop(dve, step, L_DIV)

            RT = 9

            def router_logits(n):
                def link(ins, k):
                    ins.then_inc(rt, 1)
                    dve.wait_ge(rt, RT * n + k)
                dve.wait_ge(q_done, n + 1)
                after(dve, w_done, n)
                link(nc.vector.tensor_tensor(qa[:], qr[:].unsqueeze(2).to_broadcast([P, 4, EXPERTS, 6]),
                                             anc[:].unsqueeze(1).to_broadcast([P, 4, EXPERTS, 6]), ALU.mult), 1)
                link(nc.vector.tensor_reduce(dot[:], qa[:], axis=AX.X, op=ALU.add), 2)
                link(nc.vector.tensor_scalar(dot[:], dot[:], 6.0, 0.5, ALU.subtract, ALU.mult), 3)
                link(nc.vector.tensor_scalar(lgs[:], dot[:], tinv[:], None, ALU.mult), 4)
                link(nc.vector.tensor_reduce(lmax[:], lgs[:], axis=AX.X, op=ALU.max), 5)
                after(dve, lexp_done, n)
                nc.vector.tensor_tensor(ldif[:], lgs[:], lmax[:].unsqueeze(2).to_broadcast([P, 4, EXPERTS]),
                                        ALU.subtract).then_inc(ldif_done, 1)
                mine = lgs[:].unsqueeze(3).to_broadcast([P, 4, EXPERTS, EXPERTS])
                other = lgs[:].unsqueeze(2).to_broadcast([P, 4, EXPERTS, EXPERTS])
                nc.vector.tensor_tensor(gt[:], other, mine, ALU.is_gt).then_inc(rt, 1)
                link(nc.vector.tensor_tensor(eq[:], other, mine, ALU.is_equal), 7)
                link(nc.vector.tensor_tensor(eq[:], eq[:], tri[:].unsqueeze(1).to_broadcast([P, 4, EXPERTS, EXPERTS]),
                                             ALU.mult), 8)
                link(nc.vector.tensor_tensor(gt[:], gt[:], eq[:], ALU.add), 9)

            RW = 4

            def router_weights(n):
                def link(ins, k):
                    ins.then_inc(rw, 1)
                    dve.wait_ge(rw, RW * n + k)
                link(nc.vector.tensor_reduce(rank[:], gt[:], axis=AX.X, op=ALU.add), 1)
                dve.wait_ge(lexp_done, n + 1)
                link(nc.vector.scalar_tensor_tensor(wsel[:], rank[:], 2.0, lexp[:], ALU.is_lt, ALU.mult), 2)
                link(nc.vector.tensor_reduce(wsum[:], wsel[:], axis=AX.X, op=ALU.add), 3)
                link(nc.vector.reciprocal(winv[:], wsum[:]), 4)
                after(dve, wt_ready, n)
                nc.vector.tensor_tensor(wgt[:], wsel[:], winv[:].unsqueeze(2).to_broadcast([P, 4, EXPERTS]), ALU.mult)\
                  .then_inc(w_done, 1)

            def split(i, g):
                if live(i, nblk):
                    dve.wait_ge(atH_done, 4 * i + g + 1)
                    nc.vector.tensor_tensor(atL[:, g, :], attf[:, g, :], atH[:, g, :], ALU.subtract).then_inc(atL_done, 1)

            def middle(i):
                n = i - 2
                if live(n, nblk):
                    router_logits(n)
                split(i + 1, 0)
                if live(n, nblk):
                    router_weights(n)
                split(i + 1, 1)
                split(i + 1, 2)
                n = i
                if live(n, nblk):
                    dve.wait_ge(xr_in, 16 * (n + 1))
                    after(dve, x2_out, 16 * n)
                    after(dve, xn2_done, 4 * n)
                    for t in range(4):
                        dve.wait_ge(out_ready, 4 * n + t + 1)
                        nc.vector.tensor_tensor(x2[:, t, :], ps[:, B_OUT + t, :], xres[:, t, :], ALU.add).then_inc(add_done, 1)
                    for t in range(4):
                        dve.wait_ge(add_done, 4 * n + t + 1)
                        after(dve, mv2_done, 4 * n)
                        nc.vector.bn_stats(st2[:, t, :], x2[:, t, :]).then_inc(st2_done, 1)
                    for t in range(4):
                        dve.wait_ge(st2_done, 4 * n + t + 1)
                        apart(dve, s_dve)
                        nc.vector.bn_aggr(mv2[:, t, :], st2[:, t, :]).then_inc(mv2_done, 1)
                split(i + 1, 3)

            for g in range(4):
                split(0, g)
            middle_loop(dve, middle)

            def split_rows(i):
                for c in range(0, kchunks, 2):
                    dve.wait_ge(xH_done, 2 * i + c // 2 + 1)
                    nc.vector.tensor_tensor(xL[:, c:c + 2, :], x2tf[:, c:c + 2, :], xH[:, c:c + 2, :], ALU.subtract)\
                      .then_inc(xL_done, 1)

            def experts(i):
                def weigh(c):
                    e = c // halves
                    dve.wait_ge(gel_done, nch * i + c + 1)
                    dve.wait_ge(wb_in[e], 16 * (i + 1))
                    after(dve, hL_done, nch * i + c - 1)
                    nc.vector.tensor_tensor(hw[:, c % 2, :], gel[:, c % 2, :], wbc[:, e, :], ALU.mult).then_inc(hw_done, 1)

                def low(c):
                    dve.wait_ge(hH_done, nch * i + c + 1)
                    nc.vector.tensor_tensor(hL[:, c % 4, :], hw[:, c % 2, :], hH[:, c % 4, :], ALU.subtract).then_inc(hL_done, 1)

                for c in range(nch):
                    weigh(c)
                    if c >= 1:
                        low(c - 1)
                low(nch - 1)
                if not isinstance(i, int) or i < nblk - 1:
                    split_rows(i + 1)
                dve.wait_ge(yr_in, 16 * (i + 1))
                for t in range(4):
                    dve.wait_ge(y_ready, 4 * i + t + 1)
                    nc.vector.tensor_tensor(yres[:, t, :], ps[:, B_Y + t, :], yres[:, t, :], ALU.add).then_inc(y_done, 1)

            split_rows(0)
            expert_loop(dve, experts)

        @block.tensor
        def _(pe):
            mm = nc.tensor.matmul
            pe.wait_ge(s_ident, 2)
            pe.wait_ge(s_ktok, 4 * batches)
            pe.wait_ge(s_set, 4 + 2 * batches)
            for k in range(batches * kchunks):
                for h in range(hpg):
                    last = nc.tensor.transpose(ps[:, k, h * keys:(h + 1) * keys],
                                               ktok[:, k // kchunks, (k % kchunks) * hpg + h, :], ident[:])
                last.then_inc(s_kT, 1)
            for c in range(kchunks):
                pe.wait_ge(s_kss, c + 1)
                for r in range(kchunks):
                    last = nc.tensor.transpose(ps[:, c, r * P:(r + 1) * P], woraw[:, r, c * P:(c + 1) * P], ident[:])
                last.then_inc(s_woT, 1)
            pe.wait_ge(s_kss, batches * kchunks)
            for c in range(kchunks):
                last = nc.tensor.transpose(ps[:, 4, c * EXPERTS:(c + 1) * EXPERTS], pjraw[:, c * P:(c + 1) * P],
                                           ident[0:EXPERTS, 0:EXPERTS])
            last.then_inc(s_pjT, 1)
            pe.wait_ge(s_woL, kchunks)
            pe.wait_ge(s_pj, 1)
            pe.wait_ge(s_const, 3)
            pe.wait_ge(s_gap, 4 + kchunks)

            def scores_by_token(v, n, g, tiles):
                stack = (n // blk_per_batch) * kchunks + g
                for t in tiles:
                    after(pe, mx_done, 4 * v + t - 1)
                    for h in range(hpg):
                        o, c = h // 2 * 2 * keys, (h // 2 * 3 + h % 2) * keys
                        last = mm(ps[:, B_MX + t % 2, o:o + 2 * keys], qst[0:R_MAX, g, h, t * P:(t + 1) * P],
                                  kss[0:R_MAX, stack, c:c + 2 * keys], start=(h % 2 == 0), stop=(h % 2 == 1))
                    last.then_inc(mx_ready, 1)

            def scores_by_key(v, g, heads):
                for h in heads:
                    after(pe, exp_done, hpg * v + h - 1)
                    mm(ps[:, B_SC + h % 2, :], kst[0:ROWS, g, h, :], qst[0:ROWS, g, h, :], start=True, stop=True)\
                        .then_inc(sc_ready, 1)

            def step(i, s):
                v, n, g = at(i, s, L_SC)
                if live(v, ntile):
                    pe.wait_ge(kv_in[g], 48 * (n + 1))
                    pe.wait_ge(m_in[g], 16 * (n + 1))
                    scores_by_key(v, g, (0, 1))
                a, an, ag = at(i, s, L_MAX)
                if live(a, ntile):
                    pe.wait_ge(q_in[ag], 48 * (an + 1))
                    scores_by_token(a, an, ag, (0, 1))
                m, mn, mg = at(i, s, L_MT)
                if live(m, ntile):
                    w = at(i, s, L_TR + 1)[0]
                    pe.wait_ge(nml_done, m + 1)
                    pe.wait_ge(qtl_done, min(w + 1, ntile) if isinstance(w, int) else w + 1)
                    for t in range(4):
                        last = nc.tensor.transpose(ps[0:2 * hpg, B_TL, t * P:(t + 1) * P], nmhl[:, mg % 2, t, :], ident[:])
                    last.then_inc(mt_ready, 1)
                if live(v, ntile):
                    scores_by_key(v, g, (2, 3))
                w, n, t = at(i, s, L_TR)
                if live(w, ntile):
                    pe.wait_ge(xhi_done, w + 1)
                    after(pe, qth_done, w)
                    for c in range(kchunks):
                        last = nc.tensor.transpose(ps[:, B_TH, c * P:(c + 1) * P], xhi[:, t % 2, c * P:(c + 1) * P], ident[:])
                    last.then_inc(th_ready, 1)
                    pe.wait_ge(xlo_done, w + 1)
                    after(pe, qtl_done, w)
                    if live(m, ntile):
                        pe.wait_ge(mt_done, m + 1)
                    for c in range(kchunks):
                        last = nc.tensor.transpose(ps[:, B_TL, c * P:(c + 1) * P], xlo[:, t % 2, c * P:(c + 1) * P], ident[:])
                    last.then_inc(tl_ready, 1)
                if live(a, ntile):
                    scores_by_token(a, an, ag, (2, 3))
                v, n, g = at(i, s, L_PV)
                if live(v, ntile):
                    pe.wait_ge(exp_done, hpg * v + hpg)
                    after(pe, newton_done, 2 * v - 1)
                    for h in range(hpg):
                        last = mm(ps[h * HD:(h + 1) * HD, B_DEN, :], ones[:], prob[:, g % 2, h, :], start=True, stop=True)
                    last.then_inc(sums_ready, 1)
                    after(pe, at_done, v)
                    for h in range(hpg):
                        last = mm(ps[h * HD:(h + 1) * HD, B_NUM, :], val[:, g, h * HD:(h + 1) * HD], prob[:, g % 2, h, :],
                                  start=True, stop=True)
                    last.then_inc(pv_done, 1)

            attention_loop(pe, step, L_PV)

            def project(n, g):
                if live(n, nblk):
                    pe.wait_ge(atH_done, 4 * n + g + 1)
                    pe.wait_ge(atL_done, 4 * n + g + 1)
                    for t in range(4):
                        if g == 0:
                            after(pe, add_done, 4 * (n - 1) + t + 1)
                        o = ps[:, B_OUT + t, :]
                        mm(o, atH[:, g, t * P:(t + 1) * P], woH[:, g, :], start=(g == 0), stop=False)
                        mm(o, atH[:, g, t * P:(t + 1) * P], woL[:, g, :], start=False, stop=False)
                        last = mm(o, atL[:, g, t * P:(t + 1) * P], woH[:, g, :], start=False, stop=(g == 3))
                        if g == 3:
                            last.then_inc(out_ready, 1)
                    if g < 3:
                        last.then_inc(wo_done, 1)

            def rows_transposed(n, tiles):
                if live(n, nblk):
                    for t in tiles:
                        pe.wait_ge(xn2_done, 4 * n + t + 1)
                        after(pe, t2_done, 4 * n + t - 1)
                        for c in range(kchunks):
                            last = nc.tensor.transpose(ps[:, B_T2 + t % 2, c * P:(c + 1) * P], xn2[:, t, c * P:(c + 1) * P],
                                                       ident[:])
                        last.then_inc(t2_ready, 1)

            def middle(i):
                project(i, 0)
                n = i - 2
                if live(n, nblk):
                    pe.wait_ge(t2_done, 4 * n + 4)
                    after(pe, zp_done, n)
                    for c in range(kchunks):
                        last = mm(ps[c * HD:(c + 1) * HD, B_ZP, :], projT[:, c, :], x2T[:, :, c, :], start=True, stop=True)
                    last.then_inc(zp_ready, 1)
                project(i, 1)
                if live(n, nblk):
                    pe.wait_ge(zp_done, n + 1)
                    after(pe, wt_done, n)
                    for t in range(4):
                        last = mm(ps[:, B_Z, t * EXPERTS:(t + 1) * EXPERTS], zpart[:, t * P:(t + 1) * P], fold[:],
                                  start=True, stop=True)
                    last.then_inc(z_ready, 1)
                project(i, 2)
                rows_transposed(i - 1, (0, 1))
                project(i, 3)
                rows_transposed(i - 1, (2, 3))
                if live(n, nblk):
                    pe.wait_ge(w_done, n + 1)
                    last = nc.tensor.transpose(ps[0:4 * EXPERTS, B_Z, WT0:WT0 + P],
                                               wgt[:].rearrange("p t e -> p (t e)"), ident[:])
                    last.then_inc(wt_ready, 1)
            middle_loop(pe, middle)

            pe.wait_ge(wL_done, 2 * EXPERTS)

            def experts(i):
                def up(c):
                    e, j = c // halves, c % halves
                    after(pe, gel_done, nch * i + c - 3)
                    for k in range(kchunks):
                        o, cols = ps[:, B_UP + c % 4, :], slice(j * P, (j + 1) * P)
                        mm(o, w1H[:, e, k, cols], xH[:, k, :], start=(k == 0), stop=False)
                        mm(o, w1H[:, e, k, cols], xL[:, k, :], start=False, stop=False)
                        last = mm(o, w1L[:, e, k, cols], xH[:, k, :], start=False, stop=(k == kchunks - 1))
                    last.then_inc(up_ready, 1)

                def down(c):
                    e, j = c // halves, c % halves
                    pe.wait_ge(hL_done, nch * i + c + 1)
                    for t in range(4):
                        if c == 0:
                            after(pe, y_done, 4 * (i - 1) + t + 1)
                        o, rows = ps[:, B_Y + t, :], slice(t * P, (t + 1) * P)
                        mm(o, hH[:, c % 4, rows], w2H[:, e, j, :], start=(c == 0), stop=False)
                        mm(o, hH[:, c % 4, rows], w2L[:, e, j, :], start=False, stop=False)
                        last = mm(o, hL[:, c % 4, rows], w2H[:, e, j, :], start=False, stop=(c == nch - 1))
                        if c == nch - 1:
                            last.then_inc(y_ready, 1)
                    if c < nch - 1:
                        last.then_inc(dn_done, 1)

                pe.wait_ge(xL_done, 2 * i + 2)
                for c in range(nch):
                    up(c)
                    if c >= 2:
                        down(c - 2)
                down(nch - 2)
                down(nch - 1)

            expert_loop(pe, experts)


_INS = ["x", "ctx_1024", "mask_Bx1x1xS2_ik0", "L0_xattn_W_out", "L0_ffn_proj_w", "L0_ffn_anchors",
        "L0_ffn_routing_temp", "L0_ffn_w1", "L0_ffn_w2"]


def kernel(**inputs):
    import numpy as np
    import concourse.bacc as bacc
    from concourse.bass_utils import run_bass_kernel_spmd

    nc = bacc.Bacc("TRN2", target_bir_lowering=False, num_devices=1)
    arrays, args = {}, []
    for name in _INS:
        a = np.ascontiguousarray(inputs[name])
        arrays[f"in_{name}"] = a
        args.append(nc.dram_tensor(f"in_{name}", a.shape, mybir.dt.from_np(a.dtype), kind="ExternalInput").ap())
    shape = arrays["in_x"].shape
    args.append(nc.dram_tensor("out_x", shape, F32, kind="ExternalOutput").ap())
    xattn_moe(nc, *args)
    r = run_bass_kernel_spmd(nc, [arrays], core_ids=[0])
    return r.results[0]["out_x"]
```

```python
from contextlib import ExitStack

import concourse.bass as bass
from concourse import mybir

ALU = mybir.AluOpType
ACT = mybir.ActivationFunctionType
AX = mybir.AxisListType
F32 = mybir.dt.float32
F32R = mybir.dt.float32r
U32 = mybir.dt.uint32
I32 = mybir.dt.int32

P = 128
HEADS, HD = 16, 32
EXPERTS, HID = 6, 256
LN_EPS = 1e-5
QUANT_TEMP = 0.3
MASKED = 1e20


def xattn_moe(nc, x, ctx_in, mask, w_out, proj_w, anchors, routing_temp, w1, w2, out):
    batches, seq, emb = x.shape
    keys = ctx_in.shape[1]
    kchunks = emb // P
    hpg = P // HD
    blk = 4 * P
    nblk = batches * seq // blk
    ntile = nblk * 4
    blk_per_batch = seq // blk
    scale = float(emb) ** -0.5
    halves = HID // P
    btiles = seq // P
    region = batches * seq
    NT = (2 * seq + EXPERTS * (P - 1)) // P
    NT += NT % 2
    TPI = 4
    CPI = 2
    TAIL = 4
    rows = (EXPERTS - 1) * region + seq + NT * P
    wexp = kchunks * HID
    L_T, L_UP, L_HT, L_DN, L_YW = 2, 3, 4, 5, 6
    tiles = batches * NT
    n_iter = -(-(tiles + L_YW) // TPI)
    NCOL = (n_iter - 1) * TPI + L_DN + 1
    assert tiles % TPI == 0 and (NT + L_YW) % TPI == 0 and NCOL >= L_DN + tiles
    R_BIAS = 3 * HD
    R_MAX = R_BIAS + 2
    ROWS = R_MAX + 2

    x_t = x.rearrange("b (n t p) d -> (b n) t p d", t=4, p=P)
    out_rows = out.rearrange("b (n p) d -> (b n) p d", p=P)

    def dram(name, shape, dt):
        return nc.dram_tensor(name, shape, dt, kind="Internal").ap()

    qhi_d = dram("qhi_d", [nblk, kchunks, P, blk], F32)
    qlo_d = dram("qlo_d", [nblk, kchunks, P, blk], F32)
    att_d = dram("att_d", [nblk, kchunks, P, 4 * P], F32)
    x2_d = dram("x2_d", [nblk, 4, P, emb], F32)
    xn_d = dram("xn_d", [batches * seq, emb], F32)
    perm_d = dram("perm_d", [rows, 1], I32)
    xn_t = xn_d.rearrange("(n t p) d -> n t p d", t=4, p=P)
    x2_rows = x2_d.rearrange("n t p d -> (n t) p d")
    y_d = [dram(f"y{b}_d", [NT * P, emb], F32) for b in range(batches)]

    ctx = ExitStack()
    with ctx:
        ctx.enter_context(nc.allow_non_contiguous_dma(reason="one mask value to a partition"))
        base = -(-nc.sbuf_base // 64) * 64
        cursor = [base]

        def size_of(shape):
            n = 4
            for s in shape[1:]:
                n *= s
            return -(-n // 64) * 64

        def sb(name, shape, dt=F32):
            at = cursor[0]
            cursor[0] += size_of(shape)
            return nc.alloc_sbuf_tensor_at(name, shape, dt, offset=at)

        ident = sb("ident", [P, P])
        vals = sb("vals", [P, batches * kchunks, P])
        ones = sb("ones", [P, HD])
        fold = sb("fold", [P, EXPERTS])
        projT = sb("projT", [P, kchunks, HD])
        anc = sb("anc", [P, EXPERTS, 6])
        tri = sb("tri", [P, EXPERTS, EXPERTS])
        earlier = sb("earlier", [P, P])
        allones = sb("allones", [P, P])
        steps = sb("steps", [P, btiles])
        tileno = sb("tileno", [P, NT])
        expno = sb("expno", [P, EXPERTS])
        rank01 = sb("rank01", [P, 2])
        before = sb("before", [P, 5, 4])
        token = sb("token", [P, 4])
        used = sb("used", [P, nblk + 1, EXPERTS])
        place = sb("place", [P, nblk * 4, 2])
        out_row = sb("out_row", [P, nblk * 4, 2], U32)
        share = sb("share", [P, nblk * 4, 2])
        tab_row = sb("tab_row", [P, batches * NT], I32)
        tab_col = sb("tab_col", [P, NCOL], I32)
        temp = sb("temp", [P, 1])
        tclip = sb("tclip", [P, 1])
        tinv = sb("tinv", [P, 1])
        nhalf = sb("nhalf", [P, 4, 1])
        att_base = cursor[0]
        xin = sb("xin", [P, 4, emb])
        xhi = sb("xhi", [P, 2, emb])
        xlo = sb("xlo", [P, 2, emb])
        xn = sb("xn", [P, 2, emb])
        qth = sb("qth", [P, 2, kchunks, P])
        qtl = sb("qtl", [P, 2, kchunks, P])
        qst = sb("qst", [P, 4, hpg, blk], F32R)
        kst = sb("kst", [P, 4, hpg, keys], F32R)
        val = sb("val", [P, 4, P])
        prob = sb("prob", [P, 2, hpg, blk])
        lnden = sb("lnden", [P, blk])
        rden = sb("rden", [P, 2, blk])
        newton = sb("newton", [P, blk])
        atT = sb("atT", [P, 2, blk])
        mhl = sb("mhl", [2 * hpg, 2, blk])
        st1 = sb("st1", [P, 4, 6])
        mv1 = sb("mv1", [P, 4, 2])
        vare1 = sb("vare1", [P, 4, 1])
        rstd1 = sb("rstd1", [P, 4, 1])
        nmr1 = sb("nmr1", [P, 4, 1])
        nmax = sb("nmax", [P, 2, 4, hpg])
        nmhl = sb("nmhl", [P, 2, 4, 2 * hpg])
        cursor[0] = max(cursor[0], att_base + 4 * 2 * (EXPERTS * kchunks * HID + EXPERTS * halves * emb))
        att_end = cursor[0]
        attf = sb("attf", [P, kchunks, blk])
        atH = sb("atH", [P, kchunks, blk], F32R)
        atL = sb("atL", [P, kchunks, blk], F32R)
        xres = sb("xres", [P, 4, emb])
        mid_base = cursor[0]
        x2 = sb("x2", [P, 4, emb])
        xn2 = sb("xn2", [P, 4, emb])
        x2T = sb("x2T", [P, 4, kchunks, P])
        mid_end = cursor[0]
        woH = sb("woH", [P, kchunks, emb], F32R)
        woL = sb("woL", [P, kchunks, emb], F32R)
        wraw = sb("wraw", [P, 2, kchunks * HID])
        exp_end = cursor[0]
        st2 = sb("st2", [P, 4, 6])
        mv2 = sb("mv2", [P, 4, 2])
        vare2 = sb("vare2", [P, 4, 1])
        rstd2 = sb("rstd2", [P, 4, 1])
        mrs2 = sb("mrs2", [P, 4, 1])
        nmr2 = sb("nmr2", [P, 4, 1])
        zpart = sb("zpart", [P, blk])
        qr = sb("qr", [P, 4, 6])
        qa = sb("qa", [P, 4, EXPERTS, 6])
        dot = sb("dot", [P, 4, EXPERTS])
        lgs = sb("lgs", [P, 4, EXPERTS])
        gt = sb("gt", [P, 4, EXPERTS, EXPERTS])
        eq = sb("eq", [P, 4, EXPERTS, EXPERTS])
        rank = sb("rank", [P, 4, EXPERTS])
        lmax = sb("lmax", [P, 4])
        ldif = sb("ldif", [P, 4, EXPERTS])
        lexp = sb("lexp", [P, 4, EXPERTS])
        wsel = sb("wsel", [P, 4, EXPERTS])
        wsum = sb("wsum", [P, 4])
        winv = sb("winv", [P, 4])
        wgt = sb("wgt", [P, 4, EXPERTS])
        sel = sb("sel", [P, 4, EXPERTS])
        pick = sb("pick", [P, 2, 4, EXPERTS])
        selb = sb("selb", [P, 5, EXPERTS, 4])
        selc = sb("selc", [P, 5, EXPERTS])
        slot = sb("slot", [P, 4, EXPERTS])
        pslot = sb("pslot", [P, 2, 4, EXPERTS])
        pwgt = sb("pwgt", [P, 2, 4, EXPERTS])
        slot01 = sb("slot01", [P, 2, 4])
        place_now = sb("place_now", [P, 2, 4], U32)
        token_now = sb("token_now", [P, 4], I32)
        spare = cursor[0]
        maski = sb("maski", [P, batches, 1], I32)
        m01 = sb("m01", [P, batches, 1])
        bias = sb("bias", [P, batches, 1])
        bhi = sb("bhi", [P, batches, 1])
        blo = sb("blo", [P, batches, 1])
        pjraw = sb("pjraw", [EXPERTS, emb])
        zeros = sb("zeros", [P, rows // P])
        cursor[0] = att_end
        ctok = sb("ctok", [P, batches, emb])
        kmask = sb("kmask", [P, batches, emb])
        ktok = sb("ktok", [P, batches, HEADS, P])
        woraw = sb("woraw", [P, kchunks, emb])
        assert cursor[0] <= mid_base
        cursor[0] = mid_base
        kss = sb("kss", [P, batches * kchunks, 6 * keys], F32R)
        assert cursor[0] <= mid_end
        cursor[0] = att_base
        w1H = sb("w1H", [P, EXPERTS, kchunks, HID], F32R)
        w1L = sb("w1L", [P, EXPERTS, kchunks, HID], F32R)
        w2H = sb("w2H", [P, EXPERTS, halves, emb], F32R)
        w2L = sb("w2L", [P, EXPERTS, halves, emb], F32R)
        assert cursor[0] <= att_end
        cursor[0] = spare
        cnt = sb("cnt", [P, batches, EXPERTS])
        ncmp = sb("ncmp", [P, batches, EXPERTS, btiles])
        ntil = sb("ntil", [P, batches, EXPERTS])
        nbef = sb("nbef", [P, batches, EXPERTS, EXPERTS])
        first = sb("first", [P, batches, EXPERTS])
        tcmp = sb("tcmp", [P, batches, NT, EXPERTS])
        tsel = sb("tsel", [P, batches, NT, EXPERTS])
        texp = sb("texp", [P, batches, NT])
        tfirst = sb("tfirst", [P, batches, NT])
        trow = sb("trow", [P, batches, NT])
        shift = sb("shift", [P, batches, EXPERTS])
        bounds = sb("bounds", [P, EXPERTS])
        within = sb("within", [P, 2 * btiles, EXPERTS])
        moved = sb("moved", [P, 2 * btiles])
        assert cursor[0] <= nc.sbuf_usable_end
        cursor[0] = att_end
        pidx = sb("pidx", [P, 4, 1], U32)
        xg = sb("xg", [P, 4, emb])
        sidx = sb("sidx", [P, TAIL, 2], U32)
        wst = sb("wst", [P, TAIL, 2])
        xgH = sb("xgH", [P, 2, kchunks, P], F32R)
        xgL = sb("xgL", [P, 2, kchunks, P], F32R)
        gel = sb("gel", [P, 2, HID])
        hH = sb("hH", [P, 2, halves, P], F32R)
        hL = sb("hL", [P, 2, halves, P], F32R)
        ysb = sb("ysb", [P, 2, emb])
        yg = sb("yg", [P, TAIL, 2, emb])
        x2c = sb("x2c", [P, CPI, emb])
        x2t = sb("x2t", [P, btiles, emb])
        assert cursor[0] <= exp_end

        ps = ctx.enter_context(nc.psum_tensor("ps", [P, 8, 512], F32))
        B_TH, B_TL, B_MX, B_SC, B_NUM, B_DEN = 0, 1, 2, 4, 6, 7
        B_OUT, B_T2, B_Z, B_ZP = 0, 4, 6, 7
        PL0 = P
        B_X, B_UP, B_H, B_Y = 0, 2, 4, 6

        def sem(name):
            return ctx.enter_context(nc.semaphore(name))

        def sems(name, n):
            return [sem(f"{name}{k}") for k in range(n)]

        s_load = sem("s_load")
        s_ident, s_const, s_ktok0, s_row1 = sem("s_ident"), sem("s_const"), sem("s_ktok0"), sem("s_row1")
        s_set = sem("s_set")
        s_ktok = sem("s_ktok")
        s_kT, s_kss, s_vals, s_gap = sem("s_kT"), sem("s_kss"), sem("s_vals"), sem("s_gap")
        s_woT, s_woH, s_woL = sem("s_woT"), sem("s_woH"), sem("s_woL")
        s_pjT, s_pj = sem("s_pjT"), sem("s_pj")
        s_pool, s_dve, s_sync = sem("s_pool"), sem("s_dve"), sem("s_sync")
        x_in = sems("x_in", 4)
        st_done, mv_done = sem("st_done"), sem("mv_done")
        rstd_done, nmr_done = sem("rstd_done"), sem("nmr_done")
        xhi_done, xn_done, xlo_done = sem("xhi_done"), sem("xn_done"), sem("xlo_done")
        th_ready, tl_ready = sem("th_ready"), sem("tl_ready")
        qth_done, qtl_done = sem("qth_done"), sem("qtl_done")
        q_out = sems("q_out", 4)
        q_in = sems("q_in", 4)
        kv_in = sems("kv_in", 4)
        mx_ready, mx_done = sem("mx_ready"), sem("mx_done")
        nmh_done, nml_done = sem("nmh_done"), sem("nml_done")
        mt_ready, mt_done = sem("mt_ready"), sem("mt_done")
        m_in = sems("m_in", 4)
        sc_ready, exp_done = sem("sc_ready"), sem("exp_done")
        pv_done, sums_ready, den_done, rec_done, newton_done, at_done = (
            sem("pv_done"), sem("sums_ready"), sem("den_done"), sem("rec_done"), sem("newton_done"), sem("at_done"))
        at_out = sems("at_out", 4)
        att_in = sems("att_in", 4)
        xr_in, atH_done, atL_done = sem("xr_in"), sem("atH_done"), sem("atL_done")
        wo_done, out_ready, add_done = sem("wo_done"), sem("out_ready"), sem("add_done")
        st2_done, mv2_done, rs2_done, xn2_done = sem("st2_done"), sem("mv2_done"), sem("rs2_done"), sem("xn2_done")
        nmr2_done, zp_ready, zp_done = sem("nmr2_done"), sem("zp_ready"), sem("zp_done")
        t2_ready, t2_done = sem("t2_ready"), sem("t2_done")
        x2_out, xn_out = sem("x2_out"), sem("xn_out")
        z_ready, q_done, rt, rw, ldif_done, lexp_done, w_done = (
            sem("z_ready"), sem("q_done"), sem("rt"), sem("rw"), sem("ldif_done"), sem("lexp_done"), sem("w_done"))
        sel_done, pl, pl_ready, used_done, place_done, share_done, token_done, scattered, s_token = (
            sem("sel_done"), sem("pl"), sem("pl_ready"), sem("used_done"), sem("place_done"), sem("share_done"),
            sem("token_done"), sem("scattered"), sem("s_token"))
        s_zero, perm_zero, s_pos, tb, tab_done = sem("s_zero"), sem("perm_zero"), sem("s_pos"), sem("tb"), sem("tab_done")
        wr_in, wH_done, wL_done = sem("wr_in"), sem("wH_done"), sem("wL_done")
        s_pe = sem("s_pe")
        pidx_in, xg_in = sems("pidx_in", 4), sems("xg_in", 4)
        xt_ready, xh_done, xl_done = sem("xt_ready"), sem("xh_done"), sem("xl_done")
        up_ready, gel_done, ht_ready, hh_done, hl_done = (
            sem("up_ready"), sem("gel_done"), sem("ht_ready"), sem("hh_done"), sem("hl_done"))
        y_ready, yc_done, y_out = sem("y_ready"), sem("yc_done"), sems("y_out", 2)
        sidx_done, yg_in = sems("sidx_done", TAIL), sems("yg_in", TAIL)
        x2c_in, x2t_in = sems("x2c_in", CPI), sem("x2t_in")
        half_done, cmb_done, o_out, o2_out = sems("half_done", TAIL), sems("cmb_done", TAIL), sems("o_out", CPI), sem("o2_out")

        block = ctx.enter_context(nc.Block())

        def after(eng, semaphore, count):
            if not isinstance(count, int) or count > 0:
                eng.wait_ge(semaphore, count)

        def apart(eng, tick):
            eng.sem_inc(tick, 1)

        def live(v, n):
            return not isinstance(v, int) or 0 <= v < n

        def at(i, s, lag):
            return 4 * i + (s - lag), i + (s - lag) // 4, (s - lag) % 4

        L_LOAD, L_STAT, L_NORM, L_TR = -2, 0, 1, 2
        L_UNIT, L_KV, L_MAX, L_MT, L_SC, L_PV, L_DIV, L_STORE = 6, 8, 8, 9, 10, 11, 12, 13
        SP_AHEAD = 2

        def attention_loop(eng, step, last):
            def iteration(i):
                for s in range(4):
                    step(i, s)
            for i in range(4):
                iteration(i)
            with eng.Fori(4, nblk) as i:
                iteration(i)
            for i in range(nblk, nblk + -(-last // 4) + 1):
                iteration(i)

        def middle_loop(eng, body):
            for i in range(3):
                body(i)
            with eng.Fori(3, nblk - 1) as i:
                body(i)
            for i in range(nblk - 1, nblk + 3):
                body(i)

        def tl(i, k, lag, places=2):
            w = TPI * i + (k - lag)
            return w, (k - lag) % places, (TPI // places) * i + (k - lag) // places

        def at1(v):
            return slice(v, v + 1) if isinstance(v, int) else bass.ds(v, 1)

        C0 = (NT + L_YW) // TPI
        C1 = C0 + btiles // CPI
        assert C1 <= n_iter - 1

        def expert_loop(eng, body):
            for i in range(2):
                body(i)
            with eng.Fori(2, C0) as i:
                body(i, combine=False)
            for i in range(C0, C0 + 2):
                body(i)
            with eng.Fori(C0 + 2, tiles // TPI) as i:
                body(i)
            for i in range(tiles // TPI, n_iter):
                body(i)

        combined = [btiles // CPI if k < CPI else 0 for k in range(TAIL)]

        def combine_loop(eng, body):
            body(0)
            with eng.Fori(1, btiles // TAIL) as j:
                body(j)
            body(btiles // TAIL)

        N_SETUP_LOADS = 1 + batches + 4

        @block.sync
        def _(sp):
            sp.dma_start(ctok[:], ctx_in.rearrange("b k d -> k b d")).then_inc(s_load, 16)
            for b in range(batches):
                sp.dma_start(maski[:, b, :], mask[b, 0, :, :].rearrange("a k -> k a")).then_inc(s_load, 16)
            sp.dma_start(woraw[:], w_out.rearrange("(c p) d -> p c d", p=P)).then_inc(s_load, 16)
            sp.dma_start(pjraw[:], proj_w).then_inc(s_load, 16)
            sp.dma_start(anc[:], anchors.partition_broadcast(P)).then_inc(s_load, 16)
            sp.dma_start(temp[:], routing_temp.partition_broadcast(P)).then_inc(s_load, 16)

            sp.wait_ge(s_zero, 1)
            sp.dma_start(perm_d.rearrange("(p a) c -> p (a c)", p=P), zeros[:].bitcast(I32)).then_inc(perm_zero, 16)

            def step(i, s):
                w, n, t = at(i, s, 0)
                if live(w, ntile):
                    after(sp, xhi_done, w - 3)
                    after(sp, xn_done, w - 3)
                    sp.dma_start(xin[:, t, :], x_t[n, t, :, :]).then_inc(x_in[t], 16)
                m, n, g = at(i, s, L_MT + SP_AHEAD)
                if live(m, ntile):
                    sp.wait_ge(mt_done, m + 1)
                    sp.dma_start(qst[R_MAX:R_MAX + 2, g, :, :].bitcast(F32), mhl[:, g % 2, :]).then_inc(m_in[g], 16)
                u, n, g = at(i, s, L_KV + SP_AHEAD)
                if live(u, ntile):
                    stack = (n // blk_per_batch) * kchunks + g
                    if isinstance(u, int) and u == 0:
                        sp.wait_ge(s_kss, batches * kchunks)
                        sp.wait_ge(s_vals, 1)
                    after(sp, pv_done, u - 3)
                    for a in range(2):
                        pair = kss[:, stack, 3 * keys * a:3 * keys * (a + 1)].rearrange("p (c k) -> p c k", c=3)
                        sp.dma_start(kst[:, g, 2 * a:2 * a + 2, :].bitcast(F32), pair[:, 0:3:2, :].bitcast(F32))\
                          .then_inc(kv_in[g], 16)
                    sp.dma_start(val[:, g, :], vals[:, stack, :]).then_inc(kv_in[g], 16)
                v, n, g = at(i, s, L_STORE + SP_AHEAD)
                if live(v, ntile):
                    sp.wait_ge(at_done, v + 1)
                    sp.dma_start(att_d[n, g, :, :], atT[:, g % 2, :]).then_inc(at_out[g], 16)
                u, n, g = at(i, s, L_UNIT + SP_AHEAD)
                if live(u, ntile):
                    if isinstance(u, int) and u == 0:
                        sp.wait_ge(s_row1, 1)
                    for k in range(4):
                        sp.wait_ge(q_out[k], 32 * (n + 1))
                    apart(sp, s_sync)
                    after(sp, sc_ready, hpg * (u - 3))
                    q3 = qhi_d[n, g, :, :].rearrange("(h r) t -> r h t", r=HD)
                    sp.dma_start(qst[0:HD, g, :, :].bitcast(F32), q3).then_inc(q_in[g], 16)
                    sp.dma_start(qst[2 * HD:3 * HD, g, :, :].bitcast(F32), q3).then_inc(q_in[g], 16)
                    sp.dma_start(qst[HD:2 * HD, g, :, :].bitcast(F32),
                                 qlo_d[n, g, :, :].rearrange("(h r) t -> r h t", r=HD)).then_inc(q_in[g], 16)
                w, n, t = at(i, s, L_TR + SP_AHEAD)
                if live(w, ntile):
                    sp.wait_ge(qth_done, w + 1)
                    sp.dma_start(qhi_d[n, :, :, t * P:(t + 1) * P].rearrange("k p t -> p k t"), qth[:, t % 2, :, :])\
                      .then_inc(q_out[t], 16)
                    sp.wait_ge(qtl_done, w + 1)
                    sp.dma_start(qlo_d[n, :, :, t * P:(t + 1) * P].rearrange("k p t -> p k t"), qtl[:, t % 2, :, :])\
                      .then_inc(q_out[t], 16)

            attention_loop(sp, step, L_STORE + SP_AHEAD)

            for g in range(4):
                sp.wait_ge(at_out[g], 16 * nblk)

            def load_attention(i, groups):
                if live(i, nblk):
                    for g in groups:
                        after(sp, atL_done, 4 * (i - 1) + g + 1)
                        sp.dma_start(attf[:, g, :], att_d[i, g, :, :]).then_inc(att_in[g], 16)

            def middle(i):
                load_attention(i + 1, (0, 1, 2))
                n = i - 2
                if live(n, nblk):
                    sp.wait_ge(xn2_done, 4 * n + 4)
                    sp.dma_start(xn_t[n, :, :, :].rearrange("t p d -> p t d"), xn2[:]).then_inc(xn_out, 16)
                if live(i, nblk):
                    after(sp, add_done, 4 * i)
                    sp.dma_start(xres[:], x_t[i, :, :, :].rearrange("t p d -> p t d")).then_inc(xr_in, 16)
                n = i - 1
                if live(n, nblk):
                    sp.wait_ge(add_done, 4 * n + 4)
                    sp.dma_start(x2_d[n, :, :, :].rearrange("t p d -> p t d"), x2[:]).then_inc(x2_out, 16)
                load_attention(i + 1, (3,))
                if not isinstance(i, int) or 1 <= i <= EXPERTS:
                    e = i - 1
                    sp.wait_ge(add_done, 4)
                    after(sp, wL_done, 2 * e)
                    sp.dma_start(wraw[:, 0, :].rearrange("p (k h) -> p k h", k=kchunks),
                                 w1[e, :, :].rearrange("(k p) h -> p k h", p=P)).then_inc(wr_in, 16)
                    sp.dma_start(wraw[:, 1, :].rearrange("p (j d) -> p j d", j=halves),
                                 w2[e, :, :].rearrange("(j p) d -> p j d", p=P)).then_inc(wr_in, 16)

            sp.wait_ge(perm_zero, 16)
            load_attention(0, range(4))
            middle_loop(sp, middle)

            sp.wait_ge(x2_out, 16 * nblk)
            sp.wait_ge(xn_out, 16 * nblk)
            sp.wait_ge(scattered, 16 * 8 * nblk)
            sp.wait_ge(tab_done, 2)

            sp.dma_start(x2t[:], x2_rows[btiles:2 * btiles, :, :].rearrange("c p d -> p c d")).then_inc(x2t_in, 16)
            row_regs = [sp.alloc_register(f"row{k}") for k in range(TPI)]

            def experts(i, combine=True):
                if live(TPI * i, tiles):
                    sp.load(row_regs, tab_row[0:1, TPI * i:TPI * (i + 1)] if isinstance(i, int) else
                            tab_row[0:1, bass.ds(TPI * i, TPI)])
                    row = [sp.snap(r, min_val=0, max_val=rows - P) for r in row_regs]
                for k in range(TPI):
                    w, p, n = tl(i, k, 0, 4)
                    if live(w, tiles):
                        after(sp, xg_in[p], 16 * n)
                        apart(sp, s_sync)
                        sp.dma_start(pidx[:, p, :].bitcast(I32), perm_d[bass.ds(row[k], P), :]).then_inc(pidx_in[p], 16)
                    w, p, n = tl(i, k, L_YW)
                    if live(w, tiles):
                        sp.wait_ge(yc_done, w + 1)
                        if isinstance(w, int):
                            y = y_d[w // NT].rearrange("(t p) d -> t p d", p=P)[w % NT, :, :]
                        else:
                            y = y_d[int(combine)].rearrange("(t p) d -> t p d", p=P)[w - NT * int(combine), :, :]
                        sp.dma_start(y, ysb[:, p, :]).then_inc(y_out[p], 16)
                    j = i - C0 - 1
                    q = k - (TPI - CPI)
                    if combine and q >= 0 and live(j, btiles // CPI):
                        sp.wait_ge(cmb_done[q], j + 1)
                        sp.dma_start(out_rows[CPI * j + q, :, :], x2c[:, q, :]).then_inc(o_out[q], 16)
                if combine:
                    j = i - C0
                    if live(j, btiles // CPI):
                        for q in range(CPI):
                            after(sp, o_out[q], 16 * j)
                            sp.dma_start(x2c[:, q, :], x2_rows[CPI * j + q, :, :]).then_inc(x2c_in[q], 16)

            expert_loop(sp, experts)

            def put_together(j):
                for k in range(TAIL):
                    if live(j - 1, btiles // TAIL):
                        c = TAIL * (j - 1) + k
                        sp.wait_ge(cmb_done[k], combined[k] + j)
                        sp.dma_start(out_rows[btiles + c, :, :], x2t[:, at1(c), :].squeeze(1)).then_inc(o2_out, 16)

            combine_loop(sp, put_together)
            for q in range(CPI):
                sp.wait_ge(o_out[q], 16 * (btiles // CPI))
            sp.wait_ge(o2_out, 16 * btiles)

        @block.gpsimd
        def _(pool):
            nc.gpsimd.memset(ident[:], 0.0).then_inc(s_ident, 1)
            pool.wait_ge(s_ident, 1)
            nc.gpsimd.affine_select(out=ident[:], in_=ident[:], compare_op=ALU.not_equal, fill=1.0, base=0,
                                    pattern=[[-1, P]], channel_multiplier=1).then_inc(s_ident, 1)
            nc.gpsimd.memset(ktok[:], 0.0).then_inc(s_ktok0, 1)
            nc.gpsimd.memset(kss[:].rearrange("p s (a c k) -> p s a c k", a=2, c=3)[:, :, :, 1, :].bitcast(F32), 0.0)\
              .then_inc(s_gap, 1)
            nc.gpsimd.memset(ones[:], 1.0).then_inc(s_gap, 1)
            nc.gpsimd.memset(projT[:], 0.0).then_inc(s_gap, 1)
            nc.gpsimd.memset(fold[:], 0.0).then_inc(s_gap, 1)
            pool.wait_ge(s_gap, 4)
            for c in range(kchunks):
                nc.gpsimd.affine_select(out=fold[:], in_=fold[:], compare_op=ALU.not_equal, fill=1.0, base=-HD * c,
                                        pattern=[[-1, EXPERTS]], channel_multiplier=1).then_inc(s_gap, 1)
                pool.wait_ge(s_gap, 5 + c)
            nc.gpsimd.memset(nhalf[:], -0.5).then_inc(s_const, 1)
            nc.gpsimd.memset(tri[:], 0.0).then_inc(s_const, 1)
            pool.wait_ge(s_const, 2)
            nc.gpsimd.affine_select(out=tri[:], in_=tri[:], compare_op=ALU.is_ge, fill=1.0, base=0,
                                    pattern=[[-1, EXPERTS], [1, EXPERTS]], channel_multiplier=0).then_inc(s_const, 1)
            nc.gpsimd.memset(zeros[:], 0.0).then_inc(s_zero, 1)
            nc.gpsimd.memset(allones[:], 1.0).then_inc(s_pos, 1)
            nc.gpsimd.memset(earlier[:], 1.0).then_inc(s_pos, 1)
            nc.gpsimd.memset(before[:], 1.0).then_inc(s_pos, 1)
            nc.gpsimd.iota(steps[:], pattern=[[P, btiles]], base=0, channel_multiplier=0,
                           allow_small_or_imprecise_dtypes=True).then_inc(s_pos, 1)
            nc.gpsimd.iota(tileno[:], pattern=[[1, NT]], base=0, channel_multiplier=0,
                           allow_small_or_imprecise_dtypes=True).then_inc(s_pos, 1)
            nc.gpsimd.iota(expno[:], pattern=[[1, EXPERTS]], base=0, channel_multiplier=0,
                           allow_small_or_imprecise_dtypes=True).then_inc(s_pos, 1)
            nc.gpsimd.iota(rank01[:], pattern=[[1, 2]], base=0, channel_multiplier=0,
                           allow_small_or_imprecise_dtypes=True).then_inc(s_pos, 1)
            nc.gpsimd.iota(token[:], pattern=[[P, 4]], base=0, channel_multiplier=1,
                           allow_small_or_imprecise_dtypes=True).then_inc(s_pos, 1)
            nc.gpsimd.iota(used[:, 0, :], pattern=[[region, EXPERTS]], base=0, channel_multiplier=0,
                           allow_small_or_imprecise_dtypes=True).then_inc(s_pos, 1)
            pool.wait_ge(s_pos, 9)
            nc.gpsimd.affine_select(out=earlier[:], in_=earlier[:], compare_op=ALU.is_gt, fill=0.0, base=0,
                                    pattern=[[1, P]], channel_multiplier=-1).then_inc(s_pos, 1)
            nc.gpsimd.affine_select(out=before[:], in_=before[:], compare_op=ALU.is_gt, fill=0.0, base=0,
                                    pattern=[[1, 5], [-1, 4]], channel_multiplier=0).then_inc(s_pos, 1)
            pool.wait_ge(s_ktok0, 1)
            nc.gpsimd.memset(ktok[:, :, :, R_MAX:R_MAX + 2], 1.0).then_inc(s_ktok0, 1)
            pool.wait_ge(s_ktok0, 2)
            nc.gpsimd.memset(qst[R_BIAS:R_BIAS + 2, :, :, :].bitcast(F32), 1.0).then_inc(s_row1, 1)
            pool.wait_ge(s_row1, 1)

            def step(i, s):
                w, n, t = at(i, s, L_STAT)
                if live(w, ntile):
                    pool.wait_ge(mv_done, w + 1)
                    after(pool, xhi_done, w - 3)
                    apart(pool, s_pool)
                    nc.gpsimd.tensor_scalar(vare1[:, t, :], mv1[:, t, 1:2], LN_EPS, None, ALU.add).then_inc(rstd_done, 1)
                    pool.wait_ge(rstd_done, 2 * w + 1)
                    nc.gpsimd.tensor_tensor(rstd1[:, t, :], vare1[:, t, :], nhalf[:, 0, :], ALU.pow).then_inc(rstd_done, 1)
                    pool.wait_ge(rstd_done, 2 * w + 2)
                    apart(pool, s_pool)
                    nc.gpsimd.tensor_scalar(nmr1[:, t, :], mv1[:, t, 0:1], rstd1[:, t, :], -1.0, ALU.mult, ALU.mult)\
                      .then_inc(nmr_done, 1)
                v, n, g = at(i, s, L_MAX)
                if live(v, ntile):
                    pool.wait_ge(mx_done, 4 * v + 4)
                    after(pool, mt_ready, v - 1)
                    apart(pool, s_pool)
                    nc.gpsimd.tensor_scalar(nmhl[:, g % 2, :, 0:hpg].bitcast(F32R), nmax[:, g % 2, :, :], 1.0, None,
                                            ALU.mult).then_inc(nmh_done, 1)
                    pool.wait_ge(nmh_done, v + 1)
                    nc.gpsimd.tensor_tensor(nmhl[:, g % 2, :, hpg:2 * hpg].bitcast(F32R), nmax[:, g % 2, :, :],
                                            nmhl[:, g % 2, :, 0:hpg], ALU.subtract).then_inc(nml_done, 1)
                w, n, t = at(i, s, L_NORM)
                if live(w, ntile):
                    pool.wait_ge(xn_done, w + 1)
                    pool.wait_ge(xhi_done, w + 1)
                    after(pool, tl_ready, w - 1)
                    nc.gpsimd.tensor_tensor(xlo[:, t % 2, :].bitcast(F32R), xn[:, t % 2, :], xhi[:, t % 2, :], ALU.subtract)\
                      .then_inc(xlo_done, 1)

            attention_loop(pool, step, L_MAX)

            def middle(i):
                n = i - 1
                if live(n, nblk):
                    pool.wait_ge(mv2_done, 4 * n + 4)
                    after(pool, xn2_done, 4 * n)
                    apart(pool, s_pool)
                    nc.gpsimd.tensor_scalar(vare2[:], mv2[:, :, 1:2], LN_EPS, None, ALU.add).then_inc(rs2_done, 1)
                    pool.wait_ge(rs2_done, 3 * n + 1)
                    nc.gpsimd.tensor_tensor(rstd2[:], vare2[:], nhalf[:], ALU.pow).then_inc(rs2_done, 1)
                    pool.wait_ge(rs2_done, 3 * n + 2)
                    nc.gpsimd.tensor_tensor(mrs2[:], mv2[:, :, 0:1], rstd2[:], ALU.mult).then_inc(rs2_done, 1)
                    pool.wait_ge(rs2_done, 3 * n + 3)
                    apart(pool, s_pool)
                    nc.gpsimd.tensor_scalar(nmr2[:], mrs2[:], -1.0, None, ALU.mult).then_inc(nmr2_done, 1)
                n = i - 3
                if live(n, nblk):
                    pool.wait_ge(token_done, n + 1)
                    pool.wait_ge(place_done, 2 * n + 1)
                    if isinstance(n, int) and n == 0:
                        pool.wait_ge(perm_zero, 16)
                    apart(pool, s_pool)
                    for k in range(2):
                        for t in range(4):
                            nc.gpsimd.indirect_dma_start(
                                perm_d, bass.IndirectOffsetOnAxis(ap=place_now[:, k, t:t + 1], axis=0),
                                token_now[:, t:t + 1], None).then_inc(scattered, 16)
                if not isinstance(i, int) or 2 <= i <= EXPERTS + 1:
                    e = i - 2
                    pool.wait_ge(wH_done, 2 * e + 1)
                    apart(pool, s_pool)
                    nc.gpsimd.tensor_tensor(w1L[:, e, :, :], wraw[:, 0, :].rearrange("p (k h) -> p k h", k=kchunks),
                                            w1H[:, e, :, :], ALU.subtract).then_inc(wL_done, 1)
                    pool.wait_ge(wH_done, 2 * e + 2)
                    apart(pool, s_pool)
                    nc.gpsimd.tensor_tensor(w2L[:, e, :, :], wraw[:, 1, :].rearrange("p (j d) -> p j d", j=halves),
                                            w2H[:, e, :, :], ALU.subtract).then_inc(wL_done, 1)

            middle_loop(pool, middle)

            def fetch_outputs(b, q):
                k, n = q
                pool.wait_ge(sidx_done[k], 2 * n + 2)
                after(pool, cmb_done[k], n)
                apart(pool, s_pool)
                for z in range(2):
                    nc.gpsimd.indirect_dma_start(yg[:, k, z, :], None, y_d[b],
                                                 bass.IndirectOffsetOnAxis(ap=sidx[:, k, z:z + 1], axis=0))\
                        .then_inc(yg_in[k], 16)

            def experts(i, combine=True):
                for k in range(TPI):
                    w, p, n = tl(i, k, 0, 4)
                    if live(w, tiles):
                        pool.wait_ge(pidx_in[p], 16 * (n + 1))
                        after(pool, xt_ready, w - 3)
                        apart(pool, s_pool)
                        nc.gpsimd.indirect_dma_start(xg[:, p, :], None, xn_d,
                                                     bass.IndirectOffsetOnAxis(ap=pidx[:, p, :], axis=0)).then_inc(xg_in[p], 16)
                if combine:
                    j = i - C0
                    if live(j, btiles // CPI):
                        if isinstance(j, int) and j == 0:
                            for p in range(2):
                                pool.wait_ge(y_out[p], 16 * (NT // 2))
                        for q in range(CPI):
                            fetch_outputs(0, (q, j))

            expert_loop(pool, experts)
            for p in range(2):
                pool.wait_ge(y_out[p], 16 * (tiles // 2))

            def put_together(j):
                for k in range(TAIL):
                    if live(j, btiles // TAIL):
                        fetch_outputs(1, (k, combined[k] + j))

            combine_loop(pool, put_together)

        @block.scalar
        def _(act):
            for k in range(batches * kchunks):
                act.wait_ge(s_kT, k + 1)
                nc.scalar.activation(kss[:, k, :].rearrange("p (a c k) -> p a c k", a=2, c=3)[:, :, 0:3:2, :],
                                     ps[:, k, :].rearrange("p (a h k) -> p a h k", a=2, h=2), ACT.Copy).then_inc(s_kss, 1)
            for c in range(kchunks):
                act.wait_ge(s_woT, c + 1)
                nc.scalar.activation(woH[:, c, :], ps[:, c, :], ACT.Copy).then_inc(s_woH, 1)
            act.wait_ge(s_pjT, 1)
            act.wait_ge(s_gap, 3)
            nc.scalar.activation(projT[:, :, 0:EXPERTS], ps[:, 4, 0:kchunks * EXPERTS].rearrange("p (k e) -> p k e", k=kchunks),
                                 ACT.Copy).then_inc(s_pj, 1)

            def exps(v, g, heads):
                for h in heads:
                    act.wait_ge(sc_ready, hpg * v + h + 1)
                    after(act, pv_done, v - 1)
                    nc.scalar.activation(prob[:, g % 2, h, :], ps[:, B_SC + h % 2, :], ACT.Exp, scale=scale)\
                      .then_inc(exp_done, 1)

            def step(i, s):
                v, n, g = at(i, s, L_SC)
                if live(v, ntile):
                    exps(v, g, (0, 1))
                m, mn, mg = at(i, s, L_MT)
                if live(m, ntile):
                    _, pn, pg = at(i, s, L_MT + 2)
                    act.wait_ge(mt_ready, m + 1)
                    after(act, m_in[pg], 16 * (pn + 1))
                    nc.scalar.activation(mhl[:, mg % 2, :], ps[0:2 * hpg, B_TL, :], ACT.Copy).then_inc(mt_done, 1)
                if live(v, ntile):
                    exps(v, g, (2, 3))
                f, fn, ft = at(i, s, L_NORM)
                if live(f, ntile):
                    act.wait_ge(nmr_done, f + 1)
                    act.wait_ge(x_in[ft], 16 * (fn + 1))
                    after(act, th_ready, f - 1)
                    after(act, xlo_done, f - 1)
                    nc.scalar.activation(xhi[:, ft % 2, :].bitcast(F32R), xin[:, ft, :], ACT.Identity,
                                         bias=nmr1[:, ft, :], scale=rstd1[:, ft, :]).then_inc(xhi_done, 1)
                w, wn, wt = at(i, s, L_TR)
                if live(w, ntile):
                    _, pn, pt = at(i, s, L_TR + 2)
                    act.wait_ge(th_ready, w + 1)
                    after(act, q_out[pt], 32 * (pn + 1))
                    nc.scalar.activation(qth[:, wt % 2, :, :], ps[:, B_TH, :].rearrange("p (k t) -> p k t", k=kchunks),
                                         ACT.Copy).then_inc(qth_done, 1)
                    act.wait_ge(tl_ready, w + 1)
                    nc.scalar.activation(qtl[:, wt % 2, :, :], ps[:, B_TL, :].rearrange("p (k t) -> p k t", k=kchunks),
                                         ACT.Copy).then_inc(qtl_done, 1)
                d, dn, dg = at(i, s, L_PV)
                if live(d, ntile):
                    act.wait_ge(sums_ready, d + 1)
                    after(act, rec_done, d)
                    nc.scalar.activation(lnden[:], ps[:, B_DEN, :], ACT.Ln).then_inc(den_done, 1)
                    act.wait_ge(den_done, d + 1)
                    after(act, newton_done, 2 * (d - 1))
                    nc.scalar.activation(rden[:, dg % 2, :], lnden[:], ACT.Exp, scale=-1.0).then_inc(rec_done, 1)

            nc.scalar.preload_act_table_set("natural_log_exp_and_others")
            attention_loop(act, step, L_PV)

            def split(i, g):
                if live(i, nblk):
                    act.wait_ge(att_in[g], 16 * (i + 1))
                    if g < 3:
                        after(act, wo_done, 3 * (i - 1) + g + 1)
                    else:
                        after(act, out_ready, 4 * i)
                    nc.scalar.activation(atH[:, g, :], attf[:, g, :], ACT.Copy).then_inc(atH_done, 1)

            def normalise(n, t):
                if live(n, nblk):
                    act.wait_ge(nmr2_done, n + 1)
                    after(act, t2_ready, 4 * (n - 1) + t + 1)
                    after(act, xn_out, 16 * n)
                    nc.scalar.activation(xn2[:, t, :], x2[:, t, :], ACT.Identity, bias=nmr2[:, t, :], scale=rstd2[:, t, :])\
                      .then_inc(xn2_done, 1)

            def rows_out(n, t):
                if live(n, nblk):
                    act.wait_ge(t2_ready, 4 * n + t + 1)
                    after(act, zp_ready, n)
                    nc.scalar.activation(x2T[:, t, :, :],
                                         ps[:, B_T2 + t % 2, :].rearrange("p (k t) -> p k t", k=kchunks), ACT.Copy)\
                      .then_inc(t2_done, 1)

            def middle(i):
                n = i - 2
                if live(n, nblk):
                    act.wait_ge(zp_ready, n + 1)
                    after(act, z_ready, n)
                    nc.scalar.activation(zpart[:], ps[:, B_ZP, :], ACT.Copy).then_inc(zp_done, 1)
                    act.wait_ge(z_ready, n + 1)
                    after(act, w_done, n)
                    nc.scalar.activation(qr[:], ps[:, B_Z, 0:4 * 6].rearrange("p (t d) -> p t d", t=4), ACT.Tanh,
                                         scale=1.0 / QUANT_TEMP).then_inc(q_done, 1)
                split(i + 1, 0)
                if live(n, nblk):
                    act.wait_ge(ldif_done, n + 1)
                    nc.scalar.activation(lexp[:], ldif[:], ACT.Exp).then_inc(lexp_done, 1)
                if not isinstance(i, int) or 2 <= i <= EXPERTS + 1:
                    e = i - 2
                    act.wait_ge(wr_in, 32 * e + 32)
                    nc.scalar.activation(w1H[:, e, :, :], wraw[:, 0, :].rearrange("p (k h) -> p k h", k=kchunks), ACT.Copy)\
                      .then_inc(wH_done, 1)
                    nc.scalar.activation(w2H[:, e, :, :], wraw[:, 1, :].rearrange("p (j d) -> p j d", j=halves), ACT.Copy)\
                      .then_inc(wH_done, 1)
                normalise(i - 1, 0)
                normalise(i - 1, 1)
                split(i + 1, 1)
                rows_out(i - 1, 0)
                normalise(i - 1, 2)
                rows_out(i - 1, 1)
                normalise(i - 1, 3)
                split(i + 1, 2)
                rows_out(i - 1, 2)
                rows_out(i - 1, 3)
                split(i + 1, 3)

            for g in range(4):
                split(0, g)
            middle_loop(act, middle)

            def experts(i, combine=True):
                for k in range(TPI):
                    w, p, n = tl(i, k, L_T)
                    if live(w, tiles):
                        act.wait_ge(xt_ready, w + 1)
                        after(act, up_ready, w - 1)
                        nc.scalar.activation(xgH[:, p, :, :], ps[:, B_X + p, :].rearrange("p (k t) -> p k t", k=kchunks),
                                             ACT.Copy).then_inc(xh_done, 1)
                    w, p, n = tl(i, k, L_UP)
                    if live(w, tiles):
                        act.wait_ge(up_ready, w + 1)
                        after(act, ht_ready, w - 1)
                        nc.scalar.activation(gel[:, p, :], ps[:, B_UP + p, 0:HID], ACT.Gelu_apprx_tanh).then_inc(gel_done, 1)
                    w, p, n = tl(i, k, L_HT)
                    if live(w, tiles):
                        act.wait_ge(ht_ready, w + 1)
                        after(act, y_ready, w - 1)
                        nc.scalar.activation(hH[:, p, :, :], ps[:, B_H + p, 0:HID].rearrange("p (j t) -> p j t", j=halves),
                                             ACT.Copy).then_inc(hh_done, 1)

            expert_loop(act, experts)

        @block.vector
        def _(dve):
            dve.wait_ge(s_load, 16 * N_SETUP_LOADS)
            chain = [0]

            def link(ins):
                chain[0] += 1
                ins.then_inc(s_set, 1)
                dve.wait_ge(s_set, chain[0])

            link(nc.vector.tensor_scalar(m01[:], maski[:], 0.0, None, ALU.not_equal))
            link(nc.vector.tensor_scalar(bias[:], m01[:], -1.0, MASKED, ALU.add, ALU.mult))
            link(nc.vector.tensor_copy(bhi[:].bitcast(F32R), bias[:]))
            link(nc.vector.tensor_tensor(blo[:].bitcast(F32R), bias[:], bhi[:], ALU.subtract))
            dve.wait_ge(s_ktok0, 2)
            for b in range(batches):
                link(nc.vector.tensor_scalar(kmask[:, b, :], ctok[:, b, :], m01[:, b, :], None, ALU.mult))
                km = kmask[:, b, :].rearrange("k (h d) -> k h d", h=HEADS)
                nc.vector.tensor_copy(ktok[:, b, :, HD:2 * HD].bitcast(F32R), km).then_inc(s_ktok, 1)
                link(nc.vector.tensor_copy(ktok[:, b, :, 0:HD].bitcast(F32R), km))
                nc.vector.tensor_tensor(ktok[:, b, :, 2 * HD:3 * HD].bitcast(F32R), km, ktok[:, b, :, 0:HD], ALU.subtract)\
                  .then_inc(s_ktok, 1)
                nc.vector.tensor_copy(ktok[:, b, :, R_BIAS:R_BIAS + 1], bhi[:, b, :].unsqueeze(1).to_broadcast([P, HEADS, 1]))\
                  .then_inc(s_ktok, 1)
                nc.vector.tensor_copy(ktok[:, b, :, R_BIAS + 1:R_BIAS + 2],
                                      blo[:, b, :].unsqueeze(1).to_broadcast([P, HEADS, 1])).then_inc(s_ktok, 1)
            nc.vector.tensor_copy(vals[:], ctok[:].rearrange("k b (g c) -> k (b g) c", g=kchunks)).then_inc(s_vals, 1)
            link(nc.vector.tensor_scalar(tclip[:], temp[:], 0.1, None, ALU.max))
            link(nc.vector.reciprocal(tinv[:], tclip[:]))
            for c in range(kchunks):
                dve.wait_ge(s_woH, c + 1)
                nc.vector.tensor_tensor(woL[:, c, :], ps[:, c, :], woH[:, c, :], ALU.subtract).then_inc(s_woL, 1)

            def maxima(v, g, tiles):
                for t in tiles:
                    dve.wait_ge(mx_ready, 4 * v + t + 1)
                    after(dve, nml_done, v - 1)
                    nc.vector.tensor_reduce(nmax[:, g % 2, t, :],
                                            ps[:, B_MX + t % 2, :].rearrange("p (h k) -> p h k", h=hpg),
                                            axis=AX.X, op=ALU.max, negate=True).then_inc(mx_done, 1)

            def step(i, s):
                d, dn, dg = at(i, s, L_DIV)
                v, n, g = at(i, s, L_MAX)
                if live(d, ntile):
                    dve.wait_ge(rec_done, d + 1)
                    after(dve, at_done, d)
                    nc.vector.tensor_tensor(newton[:], ps[:, B_DEN, :], rden[:, dg % 2, :], ALU.mult).then_inc(newton_done, 1)
                    dve.wait_ge(newton_done, 2 * d + 1)
                    nc.vector.scalar_tensor_tensor(newton[:], newton[:], 2.0, rden[:, dg % 2, :], ALU.subtract, ALU.mult)\
                      .then_inc(newton_done, 1)
                if live(v, ntile):
                    maxima(v, g, (0,))
                if live(d, ntile):
                    _, pn, pg = at(i, s, L_DIV + 2)
                    dve.wait_ge(newton_done, 2 * d + 2)
                    dve.wait_ge(pv_done, d + 1)
                    after(dve, at_out[pg], 16 * (pn + 1))
                    nc.vector.scalar_tensor_tensor(atT[:, dg % 2, :], ps[:, B_NUM, :], -1.0, newton[:], ALU.mult, ALU.mult)\
                      .then_inc(at_done, 1)
                if live(v, ntile):
                    maxima(v, g, (1,))
                w, wn, t = at(i, s, L_STAT)
                if live(w, ntile):
                    dve.wait_ge(x_in[t], 16 * (wn + 1))
                    after(dve, mv_done, w - 3)
                    nc.vector.bn_stats(st1[:, t, :], xin[:, t, :]).then_inc(st_done, 1)
                f, fn, ft = at(i, s, L_NORM)
                if live(f, ntile):
                    dve.wait_ge(rstd_done, 2 * f + 2)
                    after(dve, xlo_done, f - 1)
                    nc.vector.tensor_scalar(xn[:, ft % 2, :], xin[:, ft, :], mv1[:, ft, 0:1], rstd1[:, ft, :],
                                            ALU.subtract, ALU.mult).then_inc(xn_done, 1)
                if live(w, ntile):
                    dve.wait_ge(st_done, w + 1)
                    after(dve, xn_done, w - 3)
                    apart(dve, s_dve)
                    nc.vector.bn_aggr(mv1[:, t, :], st1[:, t, :]).then_inc(mv_done, 1)
                if live(v, ntile):
                    maxima(v, g, (2, 3))

            attention_loop(dve, step, L_DIV)

            RT = 9

            def router_logits(n):
                def link(ins, k):
                    ins.then_inc(rt, 1)
                    dve.wait_ge(rt, RT * n + k)
                dve.wait_ge(q_done, n + 1)
                after(dve, share_done, n)
                link(nc.vector.tensor_tensor(qa[:], qr[:].unsqueeze(2).to_broadcast([P, 4, EXPERTS, 6]),
                                             anc[:].unsqueeze(1).to_broadcast([P, 4, EXPERTS, 6]), ALU.mult), 1)
                link(nc.vector.tensor_reduce(dot[:], qa[:], axis=AX.X, op=ALU.add), 2)
                link(nc.vector.tensor_scalar(dot[:], dot[:], 6.0, 0.5, ALU.subtract, ALU.mult), 3)
                link(nc.vector.tensor_scalar(lgs[:], dot[:], tinv[:], None, ALU.mult), 4)
                link(nc.vector.tensor_reduce(lmax[:], lgs[:], axis=AX.X, op=ALU.max), 5)
                after(dve, lexp_done, n)
                nc.vector.tensor_tensor(ldif[:], lgs[:], lmax[:].unsqueeze(2).to_broadcast([P, 4, EXPERTS]),
                                        ALU.subtract).then_inc(ldif_done, 1)
                mine = lgs[:].unsqueeze(3).to_broadcast([P, 4, EXPERTS, EXPERTS])
                other = lgs[:].unsqueeze(2).to_broadcast([P, 4, EXPERTS, EXPERTS])
                nc.vector.tensor_tensor(gt[:], other, mine, ALU.is_gt).then_inc(rt, 1)
                link(nc.vector.tensor_tensor(eq[:], other, mine, ALU.is_equal), 7)
                link(nc.vector.tensor_tensor(eq[:], eq[:], tri[:].unsqueeze(1).to_broadcast([P, 4, EXPERTS, EXPERTS]),
                                             ALU.mult), 8)
                link(nc.vector.tensor_tensor(gt[:], gt[:], eq[:], ALU.add), 9)

            RW = 4

            def router_weights(n):
                def link(ins, k):
                    ins.then_inc(rw, 1)
                    dve.wait_ge(rw, RW * n + k)
                link(nc.vector.tensor_reduce(rank[:], gt[:], axis=AX.X, op=ALU.add), 1)
                dve.wait_ge(lexp_done, n + 1)
                link(nc.vector.scalar_tensor_tensor(wsel[:], rank[:], 2.0, lexp[:], ALU.is_lt, ALU.mult), 2)
                link(nc.vector.tensor_reduce(wsum[:], wsel[:], axis=AX.X, op=ALU.add), 3)
                link(nc.vector.reciprocal(winv[:], wsum[:]), 4)
                nc.vector.tensor_tensor(wgt[:], wsel[:], winv[:].unsqueeze(2).to_broadcast([P, 4, EXPERTS]), ALU.mult)\
                  .then_inc(w_done, 1)

                link2(nc.vector.tensor_scalar(sel[:], rank[:], 2.0, None, ALU.is_lt), n, 1)
                nc.vector.tensor_tensor(pick[:], rank[:].unsqueeze(1).to_broadcast([P, 2, 4, EXPERTS]),
                                        rank01[:].unsqueeze(2).unsqueeze(3).to_broadcast([P, 2, 4, EXPERTS]),
                                        ALU.is_equal).then_inc(pl, 1)
                link2(nc.vector.tensor_tensor(selb[:], sel[:].rearrange("p t e -> p e t").unsqueeze(1)
                                              .to_broadcast([P, 5, EXPERTS, 4]),
                                              before[:].unsqueeze(2).to_broadcast([P, 5, EXPERTS, 4]), ALU.mult), n, 3)
                nc.vector.tensor_reduce(selc[:], selb[:], axis=AX.X, op=ALU.add).then_inc(sel_done, 1)

            RP = 7

            def link2(ins, n, k):
                ins.then_inc(pl, 1)
                dve.wait_ge(pl, RP * n + k)

            def places(n):
                dve.wait_ge(pl_ready, n + 1)
                apart(dve, s_dve)
                link2(nc.vector.tensor_tensor(slot[:], ps[:, B_Z, PL0:PL0 + 4 * EXPERTS].rearrange("p (t e) -> p t e", t=4),
                                              used[:, at1(n), :].to_broadcast([P, 4, EXPERTS]), ALU.add), n, 4)
                apart(dve, s_dve)
                nc.vector.tensor_tensor(used[:, at1(n + 1), :],
                                        ps[:, B_Z, PL0 + 4 * EXPERTS:PL0 + 5 * EXPERTS].unsqueeze(1),
                                        used[:, at1(n), :], ALU.add).then_inc(used_done, 1)
                link2(nc.vector.tensor_tensor(pslot[:], pick[:], slot[:].unsqueeze(1).to_broadcast([P, 2, 4, EXPERTS]),
                                              ALU.mult), n, 5)
                link2(nc.vector.tensor_reduce(slot01[:], pslot[:], axis=AX.X, op=ALU.add), n, 6)
                after(dve, scattered, 16 * 8 * n)
                nc.vector.tensor_scalar(place_now[:], slot01[:], 0.0, float(rows - 1), ALU.max, ALU.min).then_inc(place_done, 1)
                after(dve, s_token, n)
                nc.vector.tensor_copy(token_now[:], token[:]).then_inc(token_done, 1)
                dve.wait_ge(token_done, n + 1)
                nc.vector.tensor_scalar(token[:], token[:], float(blk), None, ALU.add).then_inc(s_token, 1)
                nc.vector.tensor_tensor(pwgt[:], pick[:], wgt[:].unsqueeze(1).to_broadcast([P, 2, 4, EXPERTS]), ALU.mult)\
                  .then_inc(pl, 1)
                apart(dve, s_dve)
                nc.vector.tensor_copy(place[:, bass.ds(4 * n, 4), :] if not isinstance(n, int) else place[:, 4 * n:4 * n + 4, :],
                                      slot01[:].rearrange("p k t -> p t k")).then_inc(place_done, 1)
                dve.wait_ge(pl, RP * n + 7)
                apart(dve, s_dve)
                nc.vector.tensor_reduce(share[:, bass.ds(4 * n, 4), :] if not isinstance(n, int) else share[:, 4 * n:4 * n + 4, :],
                                        pwgt[:].rearrange("p k t e -> p t k e"), axis=AX.X, op=ALU.add).then_inc(share_done, 1)

            def split(i, g):
                if live(i, nblk):
                    dve.wait_ge(atH_done, 4 * i + g + 1)
                    nc.vector.tensor_tensor(atL[:, g, :], attf[:, g, :], atH[:, g, :], ALU.subtract).then_inc(atL_done, 1)

            def middle(i):
                n = i - 2
                if live(n, nblk):
                    router_logits(n)
                split(i + 1, 0)
                if live(n, nblk):
                    router_weights(n)
                split(i + 1, 1)
                split(i + 1, 2)
                n = i
                if live(n, nblk):
                    dve.wait_ge(xr_in, 16 * (n + 1))
                    after(dve, x2_out, 16 * n)
                    after(dve, xn2_done, 4 * n)
                    for t in range(4):
                        dve.wait_ge(out_ready, 4 * n + t + 1)
                        nc.vector.tensor_tensor(x2[:, t, :], ps[:, B_OUT + t, :], xres[:, t, :], ALU.add).then_inc(add_done, 1)
                    for t in range(4):
                        dve.wait_ge(add_done, 4 * n + t + 1)
                        after(dve, mv2_done, 4 * n)
                        nc.vector.bn_stats(st2[:, t, :], x2[:, t, :]).then_inc(st2_done, 1)
                    for t in range(4):
                        dve.wait_ge(st2_done, 4 * n + t + 1)
                        apart(dve, s_dve)
                        nc.vector.bn_aggr(mv2[:, t, :], st2[:, t, :]).then_inc(mv2_done, 1)
                split(i + 1, 3)
                n = i - 2
                if live(n, nblk):
                    places(n)

            for g in range(4):
                split(0, g)
            middle_loop(dve, middle)

            tabs = [0]

            def link(ins):
                tabs[0] += 1
                ins.then_inc(tb, 1)
                dve.wait_ge(tb, tabs[0])

            starts = used[:, 0:nblk:blk_per_batch, :]
            ends = used[:, blk_per_batch:nblk + 1:blk_per_batch, :]
            full = [P, batches, NT, EXPERTS]
            dve.wait_ge(used_done, nblk)
            link(nc.vector.tensor_tensor(cnt[:], ends, starts, ALU.subtract))
            link(nc.vector.tensor_tensor(ncmp[:], cnt[:].unsqueeze(3).to_broadcast([P, batches, EXPERTS, btiles]),
                                         steps[:].unsqueeze(1).unsqueeze(2).to_broadcast([P, batches, EXPERTS, btiles]), ALU.is_gt))
            link(nc.vector.tensor_reduce(ntil[:], ncmp[:], axis=AX.X, op=ALU.add))
            link(nc.vector.tensor_tensor(nbef[:], ntil[:].unsqueeze(2).to_broadcast([P, batches, EXPERTS, EXPERTS]),
                                         tri[:].unsqueeze(1).to_broadcast([P, batches, EXPERTS, EXPERTS]), ALU.mult))
            link(nc.vector.tensor_reduce(first[:], nbef[:], axis=AX.X, op=ALU.add))
            firsts = first[:].unsqueeze(2).to_broadcast(full)
            link(nc.vector.tensor_tensor(tcmp[:], firsts, tileno[:].unsqueeze(1).unsqueeze(3).to_broadcast(full), ALU.is_le))
            link(nc.vector.tensor_reduce(texp[:], tcmp[:], axis=AX.X, op=ALU.add))
            link(nc.vector.tensor_tensor(tsel[:], tcmp[:], firsts, ALU.mult))
            link(nc.vector.tensor_reduce(tfirst[:], tsel[:], axis=AX.X, op=ALU.max))
            link(nc.vector.tensor_scalar(texp[:], texp[:], 1.0, None, ALU.subtract))
            link(nc.vector.tensor_tensor(tcmp[:], expno[:].unsqueeze(1).unsqueeze(2).to_broadcast(full),
                                         texp[:].unsqueeze(3).to_broadcast(full), ALU.is_equal))
            link(nc.vector.tensor_tensor(tsel[:], tcmp[:], starts.unsqueeze(2).to_broadcast(full), ALU.mult))
            link(nc.vector.tensor_reduce(trow[:], tsel[:], axis=AX.X, op=ALU.add))
            link(nc.vector.tensor_tensor(tfirst[:], tileno[:].unsqueeze(1).to_broadcast([P, batches, NT]), tfirst[:], ALU.subtract))
            link(nc.vector.scalar_tensor_tensor(trow[:], tfirst[:], float(P), trow[:], ALU.mult, ALU.add))
            nc.vector.tensor_copy(tab_row[:], trow[:].rearrange("p b i -> p (b i)")).then_inc(tab_done, 1)
            link(nc.vector.memset(tab_col[:].bitcast(F32), 0.0))
            nc.vector.tensor_scalar(tab_col[:, L_DN:L_DN + tiles], texp[:].rearrange("p b i -> p (b i)"), float(wexp), None,
                                    ALU.mult).then_inc(tab_done, 1)

            link(nc.vector.scalar_tensor_tensor(first[:], first[:], float(P), starts, ALU.mult, ALU.subtract))
            nc.vector.tensor_copy(shift[:, :, 0:1], first[:, :, 0:1]).then_inc(tb, 1)
            tabs[0] += 1
            link(nc.vector.tensor_tensor(shift[:, :, 1:EXPERTS], first[:, :, 1:EXPERTS], first[:, :, 0:EXPERTS - 1], ALU.subtract))
            link(nc.vector.tensor_scalar(bounds[:], expno[:], float(region), None, ALU.mult))
            for b in range(batches):
                mine = place[:, b * btiles:(b + 1) * btiles, :].rearrange("p t k -> p (t k)")
                each = [P, 2 * btiles, EXPERTS]
                link(nc.vector.tensor_tensor(within[:], mine.unsqueeze(2).to_broadcast(each),
                                             bounds[:].unsqueeze(1).to_broadcast(each), ALU.is_ge))
                link(nc.vector.tensor_tensor(within[:], within[:], shift[:, b, :].unsqueeze(1).to_broadcast(each), ALU.mult))
                link(nc.vector.tensor_reduce(moved[:], within[:], axis=AX.X, op=ALU.add))
                link(nc.vector.tensor_tensor(out_row[:, b * btiles:(b + 1) * btiles, :].rearrange("p t k -> p (t k)"),
                                             mine, moved[:], ALU.add))

            def stage(c, q):
                k, n = q
                after(dve, yg_in[k], 32 * n)
                apart(dve, s_dve)
                nc.vector.tensor_copy(sidx[:, k, :], out_row[:, at1(c), :].squeeze(1)).then_inc(sidx_done[k], 1)
                after(dve, cmb_done[k], n)
                apart(dve, s_dve)
                nc.vector.tensor_copy(wst[:, k, :], share[:, at1(c), :].squeeze(1)).then_inc(sidx_done[k], 1)

            def add(x, q):
                k, n = q
                dve.wait_ge(yg_in[k], 32 * (n + 1))
                dve.wait_ge(sidx_done[k], 2 * n + 2)
                apart(dve, s_dve)
                nc.vector.scalar_tensor_tensor(x, yg[:, k, 0, :], wst[:, k, 0:1], x, ALU.mult, ALU.add)\
                  .then_inc(half_done[k], 1)
                dve.wait_ge(half_done[k], n + 1)
                apart(dve, s_dve)
                nc.vector.scalar_tensor_tensor(x, yg[:, k, 1, :], wst[:, k, 1:2], x, ALU.mult, ALU.add)\
                  .then_inc(cmb_done[k], 1)

            def experts(i, combine=True):
                for k in range(TPI):
                    w, p, n = tl(i, k, L_T)
                    if live(w, tiles):
                        dve.wait_ge(xh_done, w + 1)
                        nc.vector.tensor_tensor(xgL[:, p, :, :], ps[:, B_X + p, :].rearrange("p (k t) -> p k t", k=kchunks),
                                                xgH[:, p, :, :], ALU.subtract).then_inc(xl_done, 1)
                    w, p, n = tl(i, k, L_HT)
                    if live(w, tiles):
                        dve.wait_ge(hh_done, w + 1)
                        nc.vector.tensor_tensor(hL[:, p, :, :], ps[:, B_H + p, 0:HID].rearrange("p (j t) -> p j t", j=halves),
                                                hH[:, p, :, :], ALU.subtract).then_inc(hl_done, 1)
                    w, p, n = tl(i, k, L_DN)
                    if live(w, tiles):
                        dve.wait_ge(y_ready, w + 1)
                        after(dve, y_out[p], 16 * n)
                        nc.vector.tensor_copy(ysb[:, p, :], ps[:, B_Y + p, :]).then_inc(yc_done, 1)
                    if combine and k < CPI:
                        j = i - C0 - 1
                        if live(j, btiles // CPI):
                            dve.wait_ge(x2c_in[k], 16 * (j + 1))
                            add(x2c[:, k, :], (k, j))
                        j = i - C0
                        if live(j, btiles // CPI):
                            stage(CPI * j + k, (k, j))

            expert_loop(dve, experts)

            dve.wait_ge(x2t_in, 16)

            def put_together(j):
                for k in range(TAIL):
                    c = TAIL * (j - 1) + k
                    if live(j - 1, btiles // TAIL):
                        add(x2t[:, at1(c), :].squeeze(1), (k, combined[k] + j - 1))
                    c = TAIL * j + k
                    if live(j, btiles // TAIL):
                        stage(btiles + c, (k, combined[k] + j))

            combine_loop(dve, put_together)

        @block.tensor
        def _(pe):
            mm = nc.tensor.matmul
            pe.wait_ge(s_ident, 2)
            pe.wait_ge(s_ktok, 4 * batches)
            pe.wait_ge(s_set, 4 + 2 * batches)
            for k in range(batches * kchunks):
                for h in range(hpg):
                    last = nc.tensor.transpose(ps[:, k, h * keys:(h + 1) * keys],
                                               ktok[:, k // kchunks, (k % kchunks) * hpg + h, :], ident[:])
                last.then_inc(s_kT, 1)
            for c in range(kchunks):
                pe.wait_ge(s_kss, c + 1)
                for r in range(kchunks):
                    last = nc.tensor.transpose(ps[:, c, r * P:(r + 1) * P], woraw[:, r, c * P:(c + 1) * P], ident[:])
                last.then_inc(s_woT, 1)
            pe.wait_ge(s_kss, batches * kchunks)
            for c in range(kchunks):
                last = nc.tensor.transpose(ps[:, 4, c * EXPERTS:(c + 1) * EXPERTS], pjraw[:, c * P:(c + 1) * P],
                                           ident[0:EXPERTS, 0:EXPERTS])
            last.then_inc(s_pjT, 1)
            pe.wait_ge(s_woL, kchunks)
            pe.wait_ge(s_pj, 1)
            pe.wait_ge(s_const, 3)
            pe.wait_ge(s_pos, 11)
            pe.wait_ge(s_gap, 4 + kchunks)

            def scores_by_token(v, n, g, tiles):
                stack = (n // blk_per_batch) * kchunks + g
                for t in tiles:
                    after(pe, mx_done, 4 * v + t - 1)
                    for h in range(hpg):
                        o, c = h // 2 * 2 * keys, (h // 2 * 3 + h % 2) * keys
                        last = mm(ps[:, B_MX + t % 2, o:o + 2 * keys], qst[0:R_MAX, g, h, t * P:(t + 1) * P],
                                  kss[0:R_MAX, stack, c:c + 2 * keys], start=(h % 2 == 0), stop=(h % 2 == 1))
                    last.then_inc(mx_ready, 1)

            def scores_by_key(v, g, heads):
                for h in heads:
                    after(pe, exp_done, hpg * v + h - 1)
                    mm(ps[:, B_SC + h % 2, :], kst[0:ROWS, g, h, :], qst[0:ROWS, g, h, :], start=True, stop=True)\
                        .then_inc(sc_ready, 1)

            def step(i, s):
                v, n, g = at(i, s, L_SC)
                if live(v, ntile):
                    pe.wait_ge(kv_in[g], 48 * (n + 1))
                    pe.wait_ge(m_in[g], 16 * (n + 1))
                    scores_by_key(v, g, (0, 1))
                a, an, ag = at(i, s, L_MAX)
                if live(a, ntile):
                    pe.wait_ge(q_in[ag], 48 * (an + 1))
                    scores_by_token(a, an, ag, (0, 1))
                m, mn, mg = at(i, s, L_MT)
                if live(m, ntile):
                    w = at(i, s, L_TR + 1)[0]
                    pe.wait_ge(nml_done, m + 1)
                    pe.wait_ge(qtl_done, min(w + 1, ntile) if isinstance(w, int) else w + 1)
                    for t in range(4):
                        last = nc.tensor.transpose(ps[0:2 * hpg, B_TL, t * P:(t + 1) * P], nmhl[:, mg % 2, t, :], ident[:])
                    last.then_inc(mt_ready, 1)
                if live(v, ntile):
                    scores_by_key(v, g, (2, 3))
                w, n, t = at(i, s, L_TR)
                if live(w, ntile):
                    pe.wait_ge(xhi_done, w + 1)
                    after(pe, qth_done, w)
                    for c in range(kchunks):
                        last = nc.tensor.transpose(ps[:, B_TH, c * P:(c + 1) * P], xhi[:, t % 2, c * P:(c + 1) * P], ident[:])
                    last.then_inc(th_ready, 1)
                    pe.wait_ge(xlo_done, w + 1)
                    after(pe, qtl_done, w)
                    if live(m, ntile):
                        pe.wait_ge(mt_done, m + 1)
                    for c in range(kchunks):
                        last = nc.tensor.transpose(ps[:, B_TL, c * P:(c + 1) * P], xlo[:, t % 2, c * P:(c + 1) * P], ident[:])
                    last.then_inc(tl_ready, 1)
                if live(a, ntile):
                    scores_by_token(a, an, ag, (2, 3))
                v, n, g = at(i, s, L_PV)
                if live(v, ntile):
                    pe.wait_ge(exp_done, hpg * v + hpg)
                    after(pe, newton_done, 2 * v - 1)
                    for h in range(hpg):
                        last = mm(ps[h * HD:(h + 1) * HD, B_DEN, :], ones[:], prob[:, g % 2, h, :], start=True, stop=True)
                    last.then_inc(sums_ready, 1)
                    after(pe, at_done, v)
                    for h in range(hpg):
                        last = mm(ps[h * HD:(h + 1) * HD, B_NUM, :], val[:, g, h * HD:(h + 1) * HD], prob[:, g % 2, h, :],
                                  start=True, stop=True)
                    last.then_inc(pv_done, 1)

            attention_loop(pe, step, L_PV)

            def project(n, g):
                if live(n, nblk):
                    pe.wait_ge(atH_done, 4 * n + g + 1)
                    pe.wait_ge(atL_done, 4 * n + g + 1)
                    for t in range(4):
                        if g == 0:
                            after(pe, add_done, 4 * (n - 1) + t + 1)
                        o = ps[:, B_OUT + t, :]
                        mm(o, atH[:, g, t * P:(t + 1) * P], woH[:, g, :], start=(g == 0), stop=False)
                        mm(o, atH[:, g, t * P:(t + 1) * P], woL[:, g, :], start=False, stop=False)
                        last = mm(o, atL[:, g, t * P:(t + 1) * P], woH[:, g, :], start=False, stop=(g == 3))
                        if g == 3:
                            last.then_inc(out_ready, 1)
                    if g < 3:
                        last.then_inc(wo_done, 1)

            def rows_transposed(n, tiles):
                if live(n, nblk):
                    for t in tiles:
                        pe.wait_ge(xn2_done, 4 * n + t + 1)
                        after(pe, t2_done, 4 * n + t - 1)
                        for c in range(kchunks):
                            last = nc.tensor.transpose(ps[:, B_T2 + t % 2, c * P:(c + 1) * P], xn2[:, t, c * P:(c + 1) * P],
                                                       ident[:])
                        last.then_inc(t2_ready, 1)

            def middle(i):
                project(i, 0)
                n = i - 2
                if live(n, nblk):
                    pe.wait_ge(t2_done, 4 * n + 4)
                    after(pe, zp_done, n)
                    for c in range(kchunks):
                        last = mm(ps[c * HD:(c + 1) * HD, B_ZP, :], projT[:, c, :], x2T[:, :, c, :], start=True, stop=True)
                    last.then_inc(zp_ready, 1)
                project(i, 1)
                if live(n, nblk):
                    pe.wait_ge(zp_done, n + 1)
                    after(pe, used_done, n)
                    for t in range(4):
                        last = mm(ps[:, B_Z, t * EXPERTS:(t + 1) * EXPERTS], zpart[:, t * P:(t + 1) * P], fold[:],
                                  start=True, stop=True)
                    last.then_inc(z_ready, 1)
                project(i, 2)
                rows_transposed(i - 1, (0, 1))
                project(i, 3)
                rows_transposed(i - 1, (2, 3))
                if live(n, nblk):
                    pe.wait_ge(sel_done, n + 1)
                    mm(ps[:, B_Z, PL0:PL0 + 5 * EXPERTS], allones[:], selc[:].rearrange("p t e -> p (t e)"),
                       start=True, stop=False)
                    mm(ps[:, B_Z, PL0:PL0 + 4 * EXPERTS], earlier[:], sel[:].rearrange("p t e -> p (t e)"),
                       start=False, stop=True).then_inc(pl_ready, 1)

            middle_loop(pe, middle)

            pe.wait_ge(wL_done, 2 * EXPERTS)
            pe.wait_ge(tab_done, 2)
            w1h, w1l = (w[:].rearrange("p e k h -> p (e k h)") for w in (w1H, w1L))
            w2h, w2l = (w[:].rearrange("p e j d -> p (e j d)") for w in (w2H, w2L))

            col_regs = [pe.alloc_register(f"col{k}") for k in range(TPI + L_DN - L_UP)]
            ncols = len(col_regs)

            def experts(i, combine=True):
                pe.load(col_regs, tab_col[0:1, TPI * i:TPI * i + ncols] if isinstance(i, int) else
                        tab_col[0:1, bass.ds(TPI * i, ncols)])
                col = [pe.snap(r, min_val=0, max_val=wexp * (EXPERTS - 1)) for r in col_regs]
                for k in range(TPI):
                    w, p, n = tl(i, k, L_T)
                    if live(w, tiles):
                        _, r, fetched = tl(i, k, L_T, 4)
                        pe.wait_ge(xg_in[r], 16 * (fetched + 1))
                        after(pe, xl_done, w - 1)
                        for c in range(kchunks):
                            last = nc.tensor.transpose(ps[:, B_X + p, c * P:(c + 1) * P], xg[:, r, c * P:(c + 1) * P], ident[:])
                        last.then_inc(xt_ready, 1)
                    w, p, n = tl(i, k, L_UP)
                    if live(w, tiles):
                        pe.wait_ge(xl_done, w + 1)
                        after(pe, gel_done, w - 1)
                        e = col[k + L_DN - L_UP]
                        o = ps[:, B_UP + p, 0:HID]
                        for c in range(kchunks):
                            cols = bass.ds(e + c * HID, HID)
                            mm(o, xgH[:, p, c, :], w1h[:, cols], start=(c == 0), stop=False)
                            mm(o, xgL[:, p, c, :], w1h[:, cols], start=False, stop=False)
                            last = mm(o, xgH[:, p, c, :], w1l[:, cols], start=False, stop=(c == kchunks - 1))
                        last.then_inc(up_ready, 1)
                    w, p, n = tl(i, k, L_HT)
                    if live(w, tiles):
                        pe.wait_ge(gel_done, w + 1)
                        after(pe, hl_done, w - 1)
                        for c in range(halves):
                            last = nc.tensor.transpose(ps[:, B_H + p, c * P:(c + 1) * P], gel[:, p, c * P:(c + 1) * P], ident[:])
                        last.then_inc(ht_ready, 1)
                    w, p, n = tl(i, k, L_DN)
                    if live(w, tiles):
                        pe.wait_ge(hl_done, w + 1)
                        after(pe, yc_done, w - 1)
                        e = col[k]
                        o = ps[:, B_Y + p, :]
                        for c in range(halves):
                            cols = bass.ds(e + c * emb, emb)
                            mm(o, hH[:, p, c, :], w2h[:, cols], start=(c == 0), stop=False)
                            mm(o, hL[:, p, c, :], w2h[:, cols], start=False, stop=False)
                            last = mm(o, hH[:, p, c, :], w2l[:, cols], start=False, stop=(c == halves - 1))
                        last.then_inc(y_ready, 1)

            expert_loop(pe, experts)


_INS = ["x", "ctx_1024", "mask_Bx1x1xS2_ik0", "L0_xattn_W_out", "L0_ffn_proj_w", "L0_ffn_anchors",
        "L0_ffn_routing_temp", "L0_ffn_w1", "L0_ffn_w2"]


def kernel(**inputs):
    import numpy as np
    import concourse.bacc as bacc
    from concourse.bass_utils import run_bass_kernel_spmd

    nc = bacc.Bacc("TRN2", target_bir_lowering=False, num_devices=1)
    arrays, args = {}, []
    for name in _INS:
        a = np.ascontiguousarray(inputs[name])
        arrays[f"in_{name}"] = a
        args.append(nc.dram_tensor(f"in_{name}", a.shape, mybir.dt.from_np(a.dtype), kind="ExternalInput").ap())
    shape = arrays["in_x"].shape
    args.append(nc.dram_tensor("out_x", shape, F32, kind="ExternalOutput").ap())
    xattn_moe(nc, *args)
    r = run_bass_kernel_spmd(nc, [arrays], core_ids=[0])
    return r.results[0]["out_x"]
```

```python
from contextlib import ExitStack

import concourse.bass as bass
from concourse import mybir

ALU = mybir.AluOpType
ACT = mybir.ActivationFunctionType
AX = mybir.AxisListType
F32 = mybir.dt.float32
F32R = mybir.dt.float32r
U32 = mybir.dt.uint32
I32 = mybir.dt.int32

P = 128
HEADS, HD = 16, 32
EXPERTS, HID = 6, 256
LN_EPS = 1e-5
QUANT_TEMP = 0.3
MASKED = 1e20


def xattn_moe(nc, x, ctx_in, mask, w_out, proj_w, anchors, routing_temp, w1, w2, out):
    batches, seq, emb = x.shape
    keys = ctx_in.shape[1]
    kchunks = emb // P
    hpg = P // HD
    blk = 4 * P
    nblk = batches * seq // blk
    ntile = nblk * 4
    blk_per_batch = seq // blk
    scale = float(emb) ** -0.5
    halves = HID // P
    btiles = seq // P
    region = seq
    NT = (2 * seq + EXPERTS * (P - 1)) // P
    TPI = 4
    CPI = 2
    TAIL = 4
    rows = (EXPERTS - 1) * region + NT * P
    wexp = kchunks * HID
    L_IDX, L_T, L_UP, L_HT, L_DN, L_YW = -2, 2, 3, 4, 5, 6
    tiles = batches * NT
    n_iter = -(-(tiles + L_YW) // TPI)
    NCOL = (n_iter - 1) * TPI + L_DN + 1
    assert NCOL >= L_DN + tiles
    R_BIAS = 3 * HD
    R_MAX = R_BIAS + 2
    ROWS = R_MAX + 2

    x_t = x.rearrange("b (n t p) d -> (b n) t p d", t=4, p=P)
    out_rows = out.rearrange("b (n p) d -> (b n) p d", p=P)

    def dram(name, shape, dt):
        return nc.dram_tensor(name, shape, dt, kind="Internal").ap()

    qhi_d = dram("qhi_d", [nblk, kchunks, P, blk], F32)
    qlo_d = dram("qlo_d", [nblk, kchunks, P, blk], F32)
    att_d = dram("att_d", [nblk, kchunks, P, 4 * P], F32)
    x2_d = dram("x2_d", [nblk, 4, P, emb], F32)
    xn_d = [dram(f"xn{b}_d", [seq, emb], F32) for b in range(batches)]
    perm_d = dram("perm_d", [batches * rows, 1], I32)
    xn_t = [xn_d[b].rearrange("(n t p) d -> n t p d", t=4, p=P) for b in range(batches)]
    x2_rows = x2_d.rearrange("n t p d -> (n t) p d")
    y_d = [dram(f"y{b}_d", [NT * P, emb], F32) for b in range(batches)]

    ctx = ExitStack()
    with ctx:
        ctx.enter_context(nc.allow_non_contiguous_dma(reason="one mask value to a partition"))
        base = -(-nc.sbuf_base // 64) * 64
        cursor = [base]

        def size_of(shape):
            n = 4
            for s in shape[1:]:
                n *= s
            return -(-n // 64) * 64

        def sb(name, shape, dt=F32):
            at = cursor[0]
            cursor[0] += size_of(shape)
            return nc.alloc_sbuf_tensor_at(name, shape, dt, offset=at)

        ident = sb("ident", [P, P])
        vals = sb("vals", [P, batches * kchunks, P])
        ones = sb("ones", [P, HD])
        fold = sb("fold", [P, EXPERTS])
        projT = sb("projT", [P, kchunks, HD])
        anc = sb("anc", [P, EXPERTS, 6])
        tri = sb("tri", [P, EXPERTS, EXPERTS])
        earlier = sb("earlier", [P, P])
        allones = sb("allones", [P, P])
        steps = sb("steps", [P, btiles])
        tileno = sb("tileno", [P, NT])
        expno = sb("expno", [P, EXPERTS])
        rank01 = sb("rank01", [P, 2])
        before = sb("before", [P, 5, 4])
        token = sb("token", [P, blk_per_batch, 4])
        used = sb("used", [P, batches, blk_per_batch + 1, EXPERTS])
        place = sb("place", [P, nblk * 4, 2])
        out_row = sb("out_row", [P, nblk * 4, 2], U32)
        share = sb("share", [P, nblk * 4, 2])
        tab_row = sb("tab_row", [P, tiles - L_IDX], I32)
        tab_col = sb("tab_col", [P, NCOL], I32)
        temp = sb("temp", [P, 1])
        tclip = sb("tclip", [P, 1])
        tinv = sb("tinv", [P, 1])
        nhalf = sb("nhalf", [P, 4, 1])
        att_base = cursor[0]
        xin = sb("xin", [P, 4, emb])
        xhi = sb("xhi", [P, 2, emb])
        xlo = sb("xlo", [P, 2, emb])
        xn = sb("xn", [P, 2, emb])
        qth = sb("qth", [P, 2, kchunks, P])
        qtl = sb("qtl", [P, 2, kchunks, P])
        qst = sb("qst", [P, 4, hpg, blk], F32R)
        prob = sb("prob", [P, 2, hpg, blk])
        lnden = sb("lnden", [P, blk])
        rden = sb("rden", [P, 2, blk])
        newton = sb("newton", [P, blk])
        atT = sb("atT", [P, 2, blk])
        mhl = sb("mhl", [2 * hpg, 2, blk])
        st1 = sb("st1", [P, 4, 6])
        mv1 = sb("mv1", [P, 4, 2])
        vare1 = sb("vare1", [P, 4, 1])
        rstd1 = sb("rstd1", [P, 4, 1])
        nmr1 = sb("nmr1", [P, 4, 1])
        nmax = sb("nmax", [P, 2, 4, hpg])
        nmhl = sb("nmhl", [P, 2, 4, 2 * hpg])
        cursor[0] = max(cursor[0], att_base + 4 * 2 * (EXPERTS * kchunks * HID + EXPERTS * halves * emb))
        att_end = cursor[0]
        attf = sb("attf", [P, kchunks, blk])
        atH = sb("atH", [P, kchunks, blk], F32R)
        atL = sb("atL", [P, kchunks, blk], F32R)
        xres = sb("xres", [P, 4, emb])
        mid_base = cursor[0]
        x2 = sb("x2", [P, 4, emb])
        xn2 = sb("xn2", [P, 4, emb])
        x2T = sb("x2T", [P, 4, kchunks, P])
        mid_end = cursor[0]
        woH = sb("woH", [P, kchunks, emb], F32R)
        woL = sb("woL", [P, kchunks, emb], F32R)
        wraw = sb("wraw", [P, 2, kchunks * HID])
        exp_end = cursor[0]
        st2 = sb("st2", [P, 4, 6])
        mv2 = sb("mv2", [P, 4, 2])
        vare2 = sb("vare2", [P, 4, 1])
        rstd2 = sb("rstd2", [P, 4, 1])
        mrs2 = sb("mrs2", [P, 4, 1])
        nmr2 = sb("nmr2", [P, 4, 1])
        zpart = sb("zpart", [P, blk])
        qr = sb("qr", [P, 4, 6])
        qa = sb("qa", [P, 4, EXPERTS, 6])
        dot = sb("dot", [P, 4, EXPERTS])
        lgs = sb("lgs", [P, 4, EXPERTS])
        gt = sb("gt", [P, 4, EXPERTS, EXPERTS])
        eq = sb("eq", [P, 4, EXPERTS, EXPERTS])
        rank = sb("rank", [P, 4, EXPERTS])
        lmax = sb("lmax", [P, 4])
        ldif = sb("ldif", [P, 4, EXPERTS])
        lexp = sb("lexp", [P, 4, EXPERTS])
        wsel = sb("wsel", [P, 4, EXPERTS])
        wsum = sb("wsum", [P, 4])
        winv = sb("winv", [P, 4])
        wgt = sb("wgt", [P, 4, EXPERTS])
        sel = sb("sel", [P, 4, EXPERTS])
        pick = sb("pick", [P, 2, 4, EXPERTS])
        selb = sb("selb", [P, 5, EXPERTS, 4])
        selc = sb("selc", [P, 5, EXPERTS])
        slot = sb("slot", [P, 4, EXPERTS])
        pslot = sb("pslot", [P, 2, 4, EXPERTS])
        pwgt = sb("pwgt", [P, 2, 4, EXPERTS])
        slot01 = sb("slot01", [P, 2, 4])
        place_now = sb("place_now", [P, 2, 2, 4], U32)
        token_now = sb("token_now", [P, 2, 4], I32)
        spare = cursor[0]
        maski = sb("maski", [P, batches, 1], I32)
        m01 = sb("m01", [P, batches, 1])
        bias = sb("bias", [P, batches, 1])
        bhi = sb("bhi", [P, batches, 1])
        blo = sb("blo", [P, batches, 1])
        pjraw = sb("pjraw", [EXPERTS, emb])
        zeros = sb("zeros", [P, batches * rows // P])
        cursor[0] = att_end
        ctok = sb("ctok", [P, batches, emb])
        kmask = sb("kmask", [P, batches, emb])
        ktok = sb("ktok", [P, batches, HEADS, P])
        woraw = sb("woraw", [P, kchunks, emb])
        assert cursor[0] <= mid_base
        cursor[0] = mid_base
        kss = sb("kss", [P, batches * kchunks, 6 * keys], F32R)
        assert cursor[0] <= mid_end
        cursor[0] = att_base
        w1H = sb("w1H", [P, EXPERTS, kchunks, HID], F32R)
        w1L = sb("w1L", [P, EXPERTS, kchunks, HID], F32R)
        w2H = sb("w2H", [P, EXPERTS, halves, emb], F32R)
        w2L = sb("w2L", [P, EXPERTS, halves, emb], F32R)
        assert cursor[0] <= att_end
        cursor[0] = spare
        cnt = sb("cnt", [P, EXPERTS])
        ncmp = sb("ncmp", [P, EXPERTS, btiles])
        ntil = sb("ntil", [P, EXPERTS])
        nbef = sb("nbef", [P, EXPERTS, EXPERTS])
        first = sb("first", [P, EXPERTS])
        tcmp = sb("tcmp", [P, NT, EXPERTS])
        tsel = sb("tsel", [P, NT, EXPERTS])
        texp = sb("texp", [P, NT])
        tfirst = sb("tfirst", [P, NT])
        trow = sb("trow", [P, NT])
        offset = sb("offset", [P, EXPERTS])
        shift = sb("shift", [P, EXPERTS])
        bounds = sb("bounds", [P, EXPERTS])
        within = sb("within", [P, 2 * btiles, EXPERTS])
        moved = sb("moved", [P, 2 * btiles])
        assert cursor[0] <= nc.sbuf_usable_end
        cursor[0] = att_end
        pidx = sb("pidx", [P, 4, 1], U32)
        xg = sb("xg", [P, 4, emb])
        sidx = sb("sidx", [P, TAIL, 2], U32)
        wst = sb("wst", [P, TAIL, 2])
        xgH = sb("xgH", [P, 2, kchunks, P], F32R)
        xgL = sb("xgL", [P, 2, kchunks, P], F32R)
        gel = sb("gel", [P, 2, HID])
        hH = sb("hH", [P, 2, halves, P], F32R)
        hL = sb("hL", [P, 2, halves, P], F32R)
        ysb = sb("ysb", [P, 2, emb])
        yg = sb("yg", [P, TAIL, 2, emb])
        x2c = sb("x2c", [P, CPI, emb])
        x2t = sb("x2t", [P, btiles, emb])
        assert cursor[0] <= exp_end

        ps = ctx.enter_context(nc.psum_tensor("ps", [P, 8, 512], F32))
        B_TH, B_TL, B_MX, B_SC, B_NUM, B_DEN = 0, 1, 2, 4, 6, 7
        B_KT, B_WT = 2, 5
        B_OUT, B_T2, B_Z, B_ZP = 0, 4, 6, 7
        PL0 = P
        B_X, B_UP, B_H, B_Y = 0, 2, 4, 6

        def sem(name):
            return ctx.enter_context(nc.semaphore(name))

        def sems(name, n):
            return [sem(f"{name}{k}") for k in range(n)]

        s_key, s_load = sem("s_key"), sem("s_load")
        s_ident, s_const, s_ktok0, s_row1 = sem("s_ident"), sem("s_const"), sem("s_ktok0"), sem("s_row1")
        s_set = sem("s_set")
        s_ktok = sem("s_ktok")
        s_kT, s_kss, s_vals, s_gap = sem("s_kT"), sem("s_kss"), sem("s_vals"), sem("s_gap")
        s_woT, s_woH, s_woL = sem("s_woT"), sem("s_woH"), sem("s_woL")
        s_pjT, s_pj = sem("s_pjT"), sem("s_pj")
        s_pool, s_dve, s_sync = sem("s_pool"), sem("s_dve"), sem("s_sync")
        x_in = sems("x_in", 4)
        st_done, mv_done = sem("st_done"), sem("mv_done")
        rstd_done, nmr_done = sem("rstd_done"), sem("nmr_done")
        xhi_done, xn_done, xlo_done = sem("xhi_done"), sem("xn_done"), sem("xlo_done")
        th_ready, tl_ready = sem("th_ready"), sem("tl_ready")
        qth_done, qtl_done = sem("qth_done"), sem("qtl_done")
        q_out = sems("q_out", 4)
        q_in = sems("q_in", 4)
        mx_ready, mx_done = sem("mx_ready"), sem("mx_done")
        nmh_done, nml_done = sem("nmh_done"), sem("nml_done")
        mt_ready, mt_done = sem("mt_ready"), sem("mt_done")
        m_in = sems("m_in", 4)
        sc_ready, exp_done = sem("sc_ready"), sem("exp_done")
        pv_done, sums_ready, den_done, rec_done, newton_done, at_done = (
            sem("pv_done"), sem("sums_ready"), sem("den_done"), sem("rec_done"), sem("newton_done"), sem("at_done"))
        at_out = sems("at_out", 4)
        att_in = sems("att_in", 4)
        xr_in, atH_done, atL_done = sem("xr_in"), sem("atH_done"), sem("atL_done")
        wo_done, out_ready, add_done = sem("wo_done"), sem("out_ready"), sem("add_done")
        st2_done, mv2_done, rs2_done, xn2_done = sem("st2_done"), sem("mv2_done"), sem("rs2_done"), sem("xn2_done")
        nmr2_done, zp_ready, zp_done = sem("nmr2_done"), sem("zp_ready"), sem("zp_done")
        t2_ready, t2_done = sem("t2_ready"), sem("t2_done")
        x2_out, xn_out = sem("x2_out"), sem("xn_out")
        z_ready, q_done, rt, rw, ldif_done, lexp_done, w_done = (
            sem("z_ready"), sem("q_done"), sem("rt"), sem("rw"), sem("ldif_done"), sem("lexp_done"), sem("w_done"))
        sel_done, pl, pl_ready, used_done, place_done, share_done, token_done, scattered = (
            sem("sel_done"), sem("pl"), sem("pl_ready"), sem("used_done"), sem("place_done"), sem("share_done"),
            sem("token_done"), sem("scattered"))
        s_zero, perm_zero, s_pos, tb, tab_done = sem("s_zero"), sem("perm_zero"), sem("s_pos"), sem("tb"), sem("tab_done")
        wr_in, wH_done, wL_done = sem("wr_in"), sem("wH_done"), sem("wL_done")
        pidx_in, xg_in = sems("pidx_in", 4), sems("xg_in", 4)
        xt_ready, xh_done, xl_done = sem("xt_ready"), sem("xh_done"), sem("xl_done")
        up_ready, gel_done, ht_ready, hh_done, hl_done = (
            sem("up_ready"), sem("gel_done"), sem("ht_ready"), sem("hh_done"), sem("hl_done"))
        y_ready, yc_done, y_out = sem("y_ready"), sem("yc_done"), sems("y_out", 2)
        sidx_done, yg_in = sems("sidx_done", TAIL), sems("yg_in", TAIL)
        x2c_in, x2t_in = sems("x2c_in", CPI), sem("x2t_in")
        half_done, cmb_done, o_out, o2_out = sems("half_done", TAIL), sems("cmb_done", TAIL), sems("o_out", CPI), sem("o2_out")

        block = ctx.enter_context(nc.Block())

        def after(eng, semaphore, count):
            if not isinstance(count, int) or count > 0:
                eng.wait_ge(semaphore, count)

        def apart(eng, tick):
            eng.sem_inc(tick, 1)

        def live(v, n):
            return not isinstance(v, int) or 0 <= v < n

        def at(i, s, lag):
            return 4 * batches * i + (s - lag), batches * i + (s - lag) // 4, (s - lag) % 4

        def batch_of(s, lag):
            return (s - lag) // 4 % batches

        def block_of(i, s, lag):
            return batch_of(s, lag) * blk_per_batch + i + (s - lag) // (4 * batches)

        L_LOAD, L_STAT, L_NORM, L_TR = -2, 0, 1, 2
        L_UNIT, L_MAX, L_MT, L_SC, L_PV, L_DIV, L_STORE = 6, 8, 9, 10, 11, 12, 13
        SP_AHEAD = 2

        def attention_loop(eng, step, last, setup):
            def iteration(i):
                for s in range(4 * batches):
                    step(i, s)
            for s in range(4 * batches):
                step(0, s)
                setup(s)
            iteration(1)
            with eng.Fori(2, blk_per_batch) as i:
                iteration(i)
            for i in range(blk_per_batch, blk_per_batch + -(-last // (4 * batches)) + 1):
                iteration(i)

        def middle_loop(eng, body):
            for i in range(3):
                body(i)
            with eng.Fori(3, blk_per_batch + 2) as i:
                body(i)
            for i in range(blk_per_batch + 2, nblk + 3):
                body(i)

        def tl(i, k, lag, places=2):
            w = TPI * i + (k - lag)
            return w, (k - lag) % places, (TPI // places) * i + (k - lag) // places

        def in_batch(n):
            return (n // blk_per_batch, n % blk_per_batch) if isinstance(n, int) else (0, n)

        def at1(v):
            return slice(v, v + 1) if isinstance(v, int) else bass.ds(v, 1)

        C0 = -(-(NT + L_YW) // TPI)
        C1 = C0 + btiles // CPI
        LEAD = C0 - btiles // 2
        assert C1 <= n_iter - 1 and TPI * LEAD >= L_YW

        def expert_loop(eng, body):
            for i in range(LEAD):
                body(i)
            with eng.Fori(LEAD, NT // TPI) as i:
                body(i, combine=False)
            for i in range(NT // TPI, C0):
                body(i, combine=False)
            for i in range(C0, C0 + 2):
                body(i)
            with eng.Fori(C0 + 2, tiles // TPI - 1) as i:
                body(i)
            for i in range(tiles // TPI - 1, n_iter):
                body(i)

        combined = [btiles // CPI if k < CPI else 0 for k in range(TAIL)]

        def combine_loop(eng, body):
            body(0)
            with eng.Fori(1, btiles // TAIL) as j:
                body(j)
            body(btiles // TAIL)

        N_SETUP_LOADS = 4
        WT0 = 4
        assert batches * kchunks == 4 * batches and WT0 + kchunks == 4 * batches

        @block.sync
        def _(sp):
            sp.dma_start(ctok[:], ctx_in.rearrange("b k d -> k b d")).then_inc(s_key, 16)
            for b in range(batches):
                sp.dma_start(maski[:, b, :], mask[b, 0, :, :].rearrange("a k -> k a")).then_inc(s_key, 16)

            def setup(s):
                if s == 0:
                    sp.dma_start(woraw[:], w_out.rearrange("(c p) d -> p c d", p=P)).then_inc(s_load, 16)
                    sp.dma_start(pjraw[:], proj_w).then_inc(s_load, 16)
                    sp.dma_start(anc[:], anchors.partition_broadcast(P)).then_inc(s_load, 16)
                    sp.dma_start(temp[:], routing_temp.partition_broadcast(P)).then_inc(s_load, 16)
                if s == 7:
                    sp.wait_ge(s_zero, 1)
                    sp.dma_start(perm_d.rearrange("(p a) c -> p (a c)", p=P), zeros[:].bitcast(I32)).then_inc(perm_zero, 16)

            def load_attention(i, groups):
                if isinstance(i, int) and i == 1 and 0 in groups:
                    for g in range(4):
                        sp.wait_ge(at_out[g], 16 * nblk)
                if live(i, nblk):
                    for g in groups:
                        after(sp, atL_done, 4 * (i - 1) + g + 1)
                        sp.dma_start(attf[:, g, :], att_d[i, g, :, :]).then_inc(att_in[g], 16)

            def step(i, s):
                w, n, t = at(i, s, 0)
                if live(w, ntile):
                    after(sp, xhi_done, w - 3)
                    after(sp, xn_done, w - 3)
                    sp.dma_start(xin[:, t, :], x_t[block_of(i, s, 0), t, :, :]).then_inc(x_in[t], 16)
                m, n, g = at(i, s, L_MT + SP_AHEAD)
                if live(m, ntile):
                    sp.wait_ge(mt_done, m + 1)
                    sp.dma_start(qst[R_MAX:R_MAX + 2, g, :, :].bitcast(F32), mhl[:, g % 2, :]).then_inc(m_in[g], 16)
                v, n, g = at(i, s, L_STORE + SP_AHEAD)
                if live(v, ntile):
                    sp.wait_ge(at_done, v + 1)
                    sp.dma_start(att_d[block_of(i, s, L_STORE + SP_AHEAD), g, :, :], atT[:, g % 2, :]).then_inc(at_out[g], 16)
                u, n, g = at(i, s, L_UNIT + SP_AHEAD)
                if live(u, ntile):
                    if isinstance(u, int) and u == 0:
                        sp.wait_ge(s_row1, 2)
                    for k in range(4):
                        sp.wait_ge(q_out[k], 32 * (n + 1))
                    apart(sp, s_sync)
                    after(sp, sc_ready, hpg * (u - 3))
                    q3 = qhi_d[n, g, :, :].rearrange("(h r) t -> r h t", r=HD)
                    sp.dma_start(qst[0:HD, g, :, :].bitcast(F32), q3).then_inc(q_in[g], 16)
                    sp.dma_start(qst[2 * HD:3 * HD, g, :, :].bitcast(F32), q3).then_inc(q_in[g], 16)
                    sp.dma_start(qst[HD:2 * HD, g, :, :].bitcast(F32),
                                 qlo_d[n, g, :, :].rearrange("(h r) t -> r h t", r=HD)).then_inc(q_in[g], 16)
                if isinstance(i, int) and (i, s) == (blk_per_batch + 1, 0):
                    for g in range(4):
                        sp.wait_ge(at_out[g], 16)
                    load_attention(0, range(4))
                    sp.dma_start(xres[:], x_t[0, :, :, :].rearrange("t p d -> p t d")).then_inc(xr_in, 16)
                w, n, t = at(i, s, L_TR + SP_AHEAD)
                if live(w, ntile):
                    sp.wait_ge(qth_done, w + 1)
                    sp.dma_start(qhi_d[n, :, :, t * P:(t + 1) * P].rearrange("k p t -> p k t"), qth[:, t % 2, :, :])\
                      .then_inc(q_out[t], 16)
                    sp.wait_ge(qtl_done, w + 1)
                    sp.dma_start(qlo_d[n, :, :, t * P:(t + 1) * P].rearrange("k p t -> p k t"), qtl[:, t % 2, :, :])\
                      .then_inc(q_out[t], 16)

            attention_loop(sp, step, L_STORE + SP_AHEAD, setup)

            def middle(i):
                n = i - 2
                if live(n, nblk):
                    sp.wait_ge(xn2_done, 4 * n + 4)
                    b, m = in_batch(n)
                    sp.dma_start(xn_t[b][m, :, :, :].rearrange("t p d -> p t d"), xn2[:]).then_inc(xn_out, 16)
                load_attention(i + 1, (0, 1, 2))
                if live(i, nblk) and not (isinstance(i, int) and i == 0):
                    sp.wait_ge(add_done, 4 * i)
                    sp.dma_start(xres[:], x_t[i, :, :, :].rearrange("t p d -> p t d")).then_inc(xr_in, 16)
                n = i - 1
                if live(n, nblk):
                    sp.wait_ge(add_done, 4 * n + 4)
                    sp.dma_start(x2_d[n, :, :, :].rearrange("t p d -> p t d"), x2[:]).then_inc(x2_out, 16)
                load_attention(i + 1, (3,))
                if not isinstance(i, int) or 1 <= i <= EXPERTS:
                    e = i - 1
                    sp.wait_ge(add_done, 4)
                    after(sp, wL_done, 2 * e)
                    sp.dma_start(wraw[:, 0, :].rearrange("p (k h) -> p k h", k=kchunks),
                                 w1[e, :, :].rearrange("(k p) h -> p k h", p=P)).then_inc(wr_in, 16)
                    sp.dma_start(wraw[:, 1, :].rearrange("p (j d) -> p j d", j=halves),
                                 w2[e, :, :].rearrange("(j p) d -> p j d", p=P)).then_inc(wr_in, 16)

            sp.wait_ge(perm_zero, 16)
            middle_loop(sp, middle)

            sp.wait_ge(xn_out, 16 * blk_per_batch)
            sp.wait_ge(scattered, 16 * 8 * blk_per_batch)
            sp.wait_ge(tab_done, 3)
            row_regs = [sp.alloc_register(f"row{k}") for k in range(TPI)]

            def rows_from(w):
                sp.load(row_regs, tab_row[0:1, w:w + TPI] if isinstance(w, int) else tab_row[0:1, bass.ds(w, TPI)])
                return [sp.snap(r, min_val=0, max_val=batches * rows - P) for r in row_regs]

            def load_tokens(row, p, n):
                after(sp, xg_in[p], 16 * n)
                apart(sp, s_sync)
                sp.dma_start(pidx[:, p, :].bitcast(I32), perm_d[bass.ds(row, P), :]).then_inc(pidx_in[p], 16)

            row = rows_from(0)
            for k in range(-L_IDX):
                load_tokens(row[k], k, 0)

            def experts(i, combine=True):
                if isinstance(i, int) and i == 1:
                    sp.wait_ge(x2_out, 16 * nblk)
                    sp.wait_ge(xn_out, 16 * nblk)
                if isinstance(i, int) and i == NT // TPI:
                    sp.wait_ge(scattered, 16 * 8 * nblk)
                    sp.wait_ge(tab_done, 6)
                if live(TPI * i - L_IDX, tiles):
                    row = rows_from(TPI * i - L_IDX)
                for k in range(TPI):
                    w, p, n = tl(i, k, L_IDX, 4)
                    if live(w, tiles):
                        load_tokens(row[k], p, n)
                    w, p, n = tl(i, k, L_YW)
                    if live(w, tiles):
                        sp.wait_ge(yc_done, w + 1)
                        if isinstance(w, int):
                            y = y_d[w // NT].rearrange("(t p) d -> t p d", p=P)[w % NT, :, :]
                        else:
                            y = y_d[int(combine)].rearrange("(t p) d -> t p d", p=P)[w - NT * int(combine), :, :]
                        sp.dma_start(y, ysb[:, p, :]).then_inc(y_out[p], 16)
                    if not combine and k % 2:
                        c = 2 * (i - LEAD) + k // 2
                        sp.dma_start(x2t[:, at1(c), :].squeeze(1), x2_rows[btiles + c, :, :]).then_inc(x2t_in, 16)
                    j = i - C0 - 1
                    q = k - (TPI - CPI)
                    if combine and q >= 0 and live(j, btiles // CPI):
                        sp.wait_ge(cmb_done[q], j + 1)
                        sp.dma_start(out_rows[CPI * j + q, :, :], x2c[:, q, :]).then_inc(o_out[q], 16)
                    j, q = (i - C0 - 1, 1) if k == 0 else (i - C0, 0)
                    if combine and k in (0, TPI - 1) and live(j, btiles // CPI):
                        after(sp, o_out[q], 16 * j)
                        sp.dma_start(x2c[:, q, :], x2_rows[CPI * j + q, :, :]).then_inc(x2c_in[q], 16)

            expert_loop(sp, experts)

            def put_together(j):
                for k in range(TAIL):
                    if live(j - 1, btiles // TAIL):
                        c = TAIL * (j - 1) + k
                        sp.wait_ge(cmb_done[k], combined[k] + j)
                        sp.dma_start(out_rows[btiles + c, :, :], x2t[:, at1(c), :].squeeze(1)).then_inc(o2_out, 16)

            combine_loop(sp, put_together)
            for q in range(CPI):
                sp.wait_ge(o_out[q], 16 * (btiles // CPI))
            sp.wait_ge(o2_out, 16 * btiles)

        @block.gpsimd
        def _(pool):
            nc.gpsimd.memset(ident[:], 0.0).then_inc(s_ident, 1)
            pool.wait_ge(s_ident, 1)
            nc.gpsimd.affine_select(out=ident[:], in_=ident[:], compare_op=ALU.not_equal, fill=1.0, base=0,
                                    pattern=[[-1, P]], channel_multiplier=1).then_inc(s_ident, 1)
            nc.gpsimd.memset(ktok[:, :, :, R_MAX:P], 1.0).then_inc(s_ktok0, 1)
            nc.gpsimd.memset(nhalf[:], -0.5).then_inc(s_const, 1)
            pool.wait_ge(s_ident, 2)
            pool.wait_ge(s_ktok0, 1)
            pool.wait_ge(s_const, 1)
            nc.gpsimd.memset(qst[R_BIAS:R_BIAS + 2, 2:4, :, :].bitcast(F32), 1.0).then_inc(s_row1, 1)
            pool.wait_ge(s_row1, 2)

            def setup(s):
                if s == 1:
                    nc.gpsimd.memset(ones[:], 1.0).then_inc(s_gap, 1)
                    nc.gpsimd.memset(projT[:], 0.0).then_inc(s_gap, 1)
                    nc.gpsimd.memset(fold[:], 0.0).then_inc(s_gap, 1)
                    pool.wait_ge(s_gap, 4)
                    for c in range(kchunks):
                        nc.gpsimd.affine_select(out=fold[:], in_=fold[:], compare_op=ALU.not_equal, fill=1.0, base=-HD * c,
                                                pattern=[[-1, EXPERTS]], channel_multiplier=1).then_inc(s_gap, 1)
                        pool.wait_ge(s_gap, 5 + c)
                if s == 2:
                    nc.gpsimd.memset(tri[:], 0.0).then_inc(s_const, 1)
                    pool.wait_ge(s_const, 2)
                    nc.gpsimd.affine_select(out=tri[:], in_=tri[:], compare_op=ALU.is_ge, fill=1.0, base=0,
                                            pattern=[[-1, EXPERTS], [1, EXPERTS]], channel_multiplier=0).then_inc(s_const, 1)
                    nc.gpsimd.memset(zeros[:], 0.0).then_inc(s_zero, 1)
                if s == 3:
                    nc.gpsimd.memset(allones[:], 1.0).then_inc(s_pos, 1)
                    nc.gpsimd.memset(earlier[:], 1.0).then_inc(s_pos, 1)
                    nc.gpsimd.memset(before[:], 1.0).then_inc(s_pos, 1)
                    nc.gpsimd.iota(steps[:], pattern=[[P, btiles]], base=0, channel_multiplier=0,
                                   allow_small_or_imprecise_dtypes=True).then_inc(s_pos, 1)
                    nc.gpsimd.iota(tileno[:], pattern=[[1, NT]], base=0, channel_multiplier=0,
                                   allow_small_or_imprecise_dtypes=True).then_inc(s_pos, 1)
                    nc.gpsimd.iota(expno[:], pattern=[[1, EXPERTS]], base=0, channel_multiplier=0,
                                   allow_small_or_imprecise_dtypes=True).then_inc(s_pos, 1)
                    nc.gpsimd.iota(rank01[:], pattern=[[1, 2]], base=0, channel_multiplier=0,
                                   allow_small_or_imprecise_dtypes=True).then_inc(s_pos, 1)
                    nc.gpsimd.iota(token[:], pattern=[[blk, blk_per_batch], [P, 4]], base=0, channel_multiplier=1,
                                   allow_small_or_imprecise_dtypes=True).then_inc(s_pos, 1)
                    for b in range(batches):
                        nc.gpsimd.iota(used[:, b, 0, :], pattern=[[region, EXPERTS]], base=b * rows, channel_multiplier=0,
                                       allow_small_or_imprecise_dtypes=True).then_inc(s_pos, 1)
                if s == 4:
                    pool.wait_ge(s_pos, 8 + batches)
                    nc.gpsimd.affine_select(out=earlier[:], in_=earlier[:], compare_op=ALU.is_gt, fill=0.0, base=0,
                                            pattern=[[1, P]], channel_multiplier=-1).then_inc(s_pos, 1)
                    nc.gpsimd.affine_select(out=before[:], in_=before[:], compare_op=ALU.is_gt, fill=0.0, base=0,
                                            pattern=[[1, 5], [-1, 4]], channel_multiplier=0).then_inc(s_pos, 1)
            def step(i, s):
                w, n, t = at(i, s, L_STAT)
                if live(w, ntile):
                    pool.wait_ge(mv_done, w + 1)
                    after(pool, xhi_done, w - 3)
                    apart(pool, s_pool)
                    nc.gpsimd.tensor_scalar(vare1[:, t, :], mv1[:, t, 1:2], LN_EPS, None, ALU.add).then_inc(rstd_done, 1)
                    pool.wait_ge(rstd_done, 2 * w + 1)
                    nc.gpsimd.tensor_tensor(rstd1[:, t, :], vare1[:, t, :], nhalf[:, 0, :], ALU.pow).then_inc(rstd_done, 1)
                    pool.wait_ge(rstd_done, 2 * w + 2)
                    apart(pool, s_pool)
                    nc.gpsimd.tensor_scalar(nmr1[:, t, :], mv1[:, t, 0:1], rstd1[:, t, :], -1.0, ALU.mult, ALU.mult)\
                      .then_inc(nmr_done, 1)
                v, n, g = at(i, s, L_MAX)
                if live(v, ntile):
                    pool.wait_ge(mx_done, 4 * v + 4)
                    after(pool, mt_ready, v - 1)
                    apart(pool, s_pool)
                    nc.gpsimd.tensor_scalar(nmhl[:, g % 2, :, 0:hpg].bitcast(F32R), nmax[:, g % 2, :, :], 1.0, None,
                                            ALU.mult).then_inc(nmh_done, 1)
                    pool.wait_ge(nmh_done, v + 1)
                    nc.gpsimd.tensor_tensor(nmhl[:, g % 2, :, hpg:2 * hpg].bitcast(F32R), nmax[:, g % 2, :, :],
                                            nmhl[:, g % 2, :, 0:hpg], ALU.subtract).then_inc(nml_done, 1)
                w, n, t = at(i, s, L_NORM)
                if live(w, ntile):
                    pool.wait_ge(xn_done, w + 1)
                    pool.wait_ge(xhi_done, w + 1)
                    after(pool, tl_ready, w - 1)
                    nc.gpsimd.tensor_tensor(xlo[:, t % 2, :].bitcast(F32R), xn[:, t % 2, :], xhi[:, t % 2, :], ALU.subtract)\
                      .then_inc(xlo_done, 1)

            attention_loop(pool, step, L_MAX, setup)

            def gather(i, k, combine=True):
                w, p, n = tl(i, k, 0, 4)
                if live(w, tiles):
                    pool.wait_ge(pidx_in[p], 16 * (n + 1))
                    after(pool, xt_ready, w - 3)
                    apart(pool, s_pool)
                    b = w // NT if isinstance(w, int) else int(combine)
                    nc.gpsimd.indirect_dma_start(xg[:, p, :], None, xn_d[b],
                                                 bass.IndirectOffsetOnAxis(ap=pidx[:, p, :], axis=0)).then_inc(xg_in[p], 16)

            def middle(i):
                n = i - 1
                if live(n, nblk):
                    pool.wait_ge(mv2_done, 4 * n + 4)
                    after(pool, xn2_done, 4 * n)
                    apart(pool, s_pool)
                    nc.gpsimd.tensor_scalar(vare2[:], mv2[:, :, 1:2], LN_EPS, None, ALU.add).then_inc(rs2_done, 1)
                    pool.wait_ge(rs2_done, 3 * n + 1)
                    nc.gpsimd.tensor_tensor(rstd2[:], vare2[:], nhalf[:], ALU.pow).then_inc(rs2_done, 1)
                    pool.wait_ge(rs2_done, 3 * n + 2)
                    nc.gpsimd.tensor_tensor(mrs2[:], mv2[:, :, 0:1], rstd2[:], ALU.mult).then_inc(rs2_done, 1)
                    pool.wait_ge(rs2_done, 3 * n + 3)
                    apart(pool, s_pool)
                    nc.gpsimd.tensor_scalar(nmr2[:], mrs2[:], -1.0, None, ALU.mult).then_inc(nmr2_done, 1)
                if isinstance(i, int) and i > nblk:
                    for k in range(TPI):
                        gather(i - nblk - 1, k)
                n = i - 3
                if live(n, nblk):
                    last = int(isinstance(n, int) and n == nblk - 1)
                    pool.wait_ge(token_done, n + 1)
                    pool.wait_ge(place_done, 2 * n + 1)
                    if isinstance(n, int) and n == 0:
                        pool.wait_ge(perm_zero, 16)
                    apart(pool, s_pool)
                    for k in range(2):
                        for t in range(4):
                            nc.gpsimd.indirect_dma_start(
                                perm_d, bass.IndirectOffsetOnAxis(ap=place_now[:, last, k, t:t + 1], axis=0),
                                token_now[:, last, t:t + 1], None).then_inc(scattered, 16)
                if not isinstance(i, int) or 2 <= i <= EXPERTS + 1:
                    e = i - 2
                    pool.wait_ge(wH_done, 2 * e + 1)
                    apart(pool, s_pool)
                    nc.gpsimd.tensor_tensor(w1L[:, e, :, :], wraw[:, 0, :].rearrange("p (k h) -> p k h", k=kchunks),
                                            w1H[:, e, :, :], ALU.subtract).then_inc(wL_done, 1)
                    pool.wait_ge(wH_done, 2 * e + 2)
                    apart(pool, s_pool)
                    nc.gpsimd.tensor_tensor(w2L[:, e, :, :], wraw[:, 1, :].rearrange("p (j d) -> p j d", j=halves),
                                            w2H[:, e, :, :], ALU.subtract).then_inc(wL_done, 1)

            middle_loop(pool, middle)

            def fetch_outputs(b, q):
                k, n = q
                pool.wait_ge(sidx_done[k], 2 * n + 2)
                after(pool, cmb_done[k], n)
                apart(pool, s_pool)
                for z in range(2):
                    nc.gpsimd.indirect_dma_start(yg[:, k, z, :], None, y_d[b],
                                                 bass.IndirectOffsetOnAxis(ap=sidx[:, k, z:z + 1], axis=0))\
                        .then_inc(yg_in[k], 16)

            def experts(i, combine=True):
                for k in range(TPI):
                    if not isinstance(i, int) or i > 1:
                        gather(i, k, combine)
                    j, q = (i - C0 - 1, 1) if k == 0 else (i - C0, 0)
                    if combine and k in (0, TPI - 1) and live(j, btiles // CPI):
                        if isinstance(j, int) and j == 0 and q == 0:
                            for p in range(2):
                                pool.wait_ge(y_out[p], 16 * ((NT + 1 - p) // 2))
                        fetch_outputs(0, (q, j))

            expert_loop(pool, experts)
            for p in range(2):
                pool.wait_ge(y_out[p], 16 * ((tiles + 1 - p) // 2))

            def put_together(j):
                for k in range(TAIL):
                    if live(j, btiles // TAIL):
                        fetch_outputs(1, (k, combined[k] + j))

            combine_loop(pool, put_together)

        @block.scalar
        def _(act):
            nc.scalar.preload_act_table_set("natural_log_exp_and_others")
            act.wait_ge(s_ident, 2)
            gaps = [P, batches * kchunks, 2, keys]
            nc.scalar.activation(kss[:].rearrange("p s (a c k) -> p s a c k", a=2, c=3)[:, :, :, 1, :],
                                 ident[:].unsqueeze(1).unsqueeze(2).to_broadcast(gaps), ACT.Copy, scale=0.0).then_inc(s_gap, 1)

            def setup(s):
                act.wait_ge(s_kT, s + 1)
                nc.scalar.activation(kss[:, s, :].rearrange("p (a c k) -> p a c k", a=2, c=3)[:, :, 0:3:2, :],
                                     ps[:, B_KT + s % 3, :].rearrange("p (a h k) -> p a h k", a=2, h=2), ACT.Copy).then_inc(s_kss, 1)
                c = s - WT0
                if c >= 0:
                    act.wait_ge(s_woT, c + 1)
                    nc.scalar.activation(woH[:, c, :], ps[:, B_WT + c % 3, :], ACT.Copy).then_inc(s_woH, 1)
                if c == kchunks - 1:
                    act.wait_ge(s_pjT, 1)
                    act.wait_ge(s_gap, 3)
                    nc.scalar.activation(projT[:, :, 0:EXPERTS],
                                         ps[:, B_WT + 1, 0:kchunks * EXPERTS].rearrange("p (k e) -> p k e", k=kchunks),
                                         ACT.Copy).then_inc(s_pj, 1)

            def exps(v, g, heads):
                for h in heads:
                    act.wait_ge(sc_ready, hpg * v + h + 1)
                    after(act, pv_done, v - 1)
                    nc.scalar.activation(prob[:, g % 2, h, :], ps[:, B_SC + h % 2, :], ACT.Exp, scale=scale)\
                      .then_inc(exp_done, 1)

            def step(i, s):
                v, n, g = at(i, s, L_SC)
                if live(v, ntile):
                    exps(v, g, (0, 1))
                m, mn, mg = at(i, s, L_MT)
                if live(m, ntile):
                    _, pn, pg = at(i, s, L_MT + 2)
                    act.wait_ge(mt_ready, m + 1)
                    after(act, m_in[pg], 16 * (pn + 1))
                    nc.scalar.activation(mhl[:, mg % 2, :], ps[0:2 * hpg, B_TL, :], ACT.Copy).then_inc(mt_done, 1)
                if live(v, ntile):
                    exps(v, g, (2, 3))
                f, fn, ft = at(i, s, L_NORM)
                if live(f, ntile):
                    act.wait_ge(nmr_done, f + 1)
                    act.wait_ge(x_in[ft], 16 * (fn + 1))
                    after(act, th_ready, f - 1)
                    after(act, xlo_done, f - 1)
                    nc.scalar.activation(xhi[:, ft % 2, :].bitcast(F32R), xin[:, ft, :], ACT.Identity,
                                         bias=nmr1[:, ft, :], scale=rstd1[:, ft, :]).then_inc(xhi_done, 1)
                w, wn, wt = at(i, s, L_TR)
                if live(w, ntile):
                    _, pn, pt = at(i, s, L_TR + 2)
                    act.wait_ge(th_ready, w + 1)
                    after(act, q_out[pt], 32 * (pn + 1))
                    nc.scalar.activation(qth[:, wt % 2, :, :], ps[:, B_TH, :].rearrange("p (k t) -> p k t", k=kchunks),
                                         ACT.Copy).then_inc(qth_done, 1)
                    act.wait_ge(tl_ready, w + 1)
                    nc.scalar.activation(qtl[:, wt % 2, :, :], ps[:, B_TL, :].rearrange("p (k t) -> p k t", k=kchunks),
                                         ACT.Copy).then_inc(qtl_done, 1)
                d, dn, dg = at(i, s, L_PV)
                if live(d, ntile):
                    act.wait_ge(sums_ready, d + 1)
                    after(act, rec_done, d)
                    nc.scalar.activation(lnden[:], ps[:, B_DEN, :], ACT.Ln).then_inc(den_done, 1)
                    act.wait_ge(den_done, d + 1)
                    after(act, newton_done, 2 * (d - 1))
                    nc.scalar.activation(rden[:, dg % 2, :], lnden[:], ACT.Exp, scale=-1.0).then_inc(rec_done, 1)

            attention_loop(act, step, L_PV, setup)

            def split(i, g):
                if live(i, nblk):
                    act.wait_ge(att_in[g], 16 * (i + 1))
                    if g < 3:
                        after(act, wo_done, 3 * (i - 1) + g + 1)
                    else:
                        after(act, out_ready, 4 * i)
                    nc.scalar.activation(atH[:, g, :], attf[:, g, :], ACT.Copy).then_inc(atH_done, 1)

            def normalise(n, t):
                if live(n, nblk):
                    act.wait_ge(nmr2_done, n + 1)
                    after(act, t2_ready, 4 * (n - 1) + t + 1)
                    after(act, xn_out, 16 * n)
                    nc.scalar.activation(xn2[:, t, :], x2[:, t, :], ACT.Identity, bias=nmr2[:, t, :], scale=rstd2[:, t, :])\
                      .then_inc(xn2_done, 1)

            def rows_out(n, t):
                if live(n, nblk):
                    act.wait_ge(t2_ready, 4 * n + t + 1)
                    after(act, zp_ready, n)
                    nc.scalar.activation(x2T[:, t, :, :],
                                         ps[:, B_T2 + t % 2, :].rearrange("p (k t) -> p k t", k=kchunks), ACT.Copy)\
                      .then_inc(t2_done, 1)

            def middle(i):
                n = i - 2
                if live(n, nblk):
                    act.wait_ge(zp_ready, n + 1)
                    after(act, z_ready, n)
                    nc.scalar.activation(zpart[:], ps[:, B_ZP, :], ACT.Copy).then_inc(zp_done, 1)
                    act.wait_ge(z_ready, n + 1)
                    after(act, w_done, n)
                    nc.scalar.activation(qr[:], ps[:, B_Z, 0:4 * 6].rearrange("p (t d) -> p t d", t=4), ACT.Tanh,
                                         scale=1.0 / QUANT_TEMP).then_inc(q_done, 1)
                normalise(i - 1, 0)
                normalise(i - 1, 1)
                if not isinstance(i, int) or 2 <= i <= EXPERTS + 1:
                    e = i - 2
                    act.wait_ge(wr_in, 32 * e + 32)
                    nc.scalar.activation(w1H[:, e, :, :], wraw[:, 0, :].rearrange("p (k h) -> p k h", k=kchunks), ACT.Copy)\
                      .then_inc(wH_done, 1)
                    nc.scalar.activation(w2H[:, e, :, :], wraw[:, 1, :].rearrange("p (j d) -> p j d", j=halves), ACT.Copy)\
                      .then_inc(wH_done, 1)
                split(i + 1, 0)
                if live(n, nblk):
                    act.wait_ge(ldif_done, n + 1)
                    nc.scalar.activation(lexp[:], ldif[:], ACT.Exp).then_inc(lexp_done, 1)
                split(i + 1, 1)
                rows_out(i - 1, 0)
                normalise(i - 1, 2)
                rows_out(i - 1, 1)
                normalise(i - 1, 3)
                split(i + 1, 2)
                rows_out(i - 1, 2)
                rows_out(i - 1, 3)
                split(i + 1, 3)

            for g in range(4):
                split(0, g)
            middle_loop(act, middle)

            def experts(i, combine=True):
                for k in range(TPI):
                    w, p, n = tl(i, k, L_T)
                    if live(w, tiles):
                        act.wait_ge(xt_ready, w + 1)
                        after(act, up_ready, w - 1)
                        nc.scalar.activation(xgH[:, p, :, :], ps[:, B_X + p, :].rearrange("p (k t) -> p k t", k=kchunks),
                                             ACT.Copy).then_inc(xh_done, 1)
                    w, p, n = tl(i, k, L_UP)
                    if live(w, tiles):
                        act.wait_ge(up_ready, w + 1)
                        after(act, ht_ready, w - 1)
                        nc.scalar.activation(gel[:, p, :], ps[:, B_UP + p, 0:HID], ACT.Gelu_apprx_tanh).then_inc(gel_done, 1)
                    w, p, n = tl(i, k, L_HT)
                    if live(w, tiles):
                        act.wait_ge(ht_ready, w + 1)
                        after(act, y_ready, w - 1)
                        nc.scalar.activation(hH[:, p, :, :], ps[:, B_H + p, 0:HID].rearrange("p (j t) -> p j t", j=halves),
                                             ACT.Copy).then_inc(hh_done, 1)

            expert_loop(act, experts)

        @block.vector
        def _(dve):
            nc.vector.memset(qst[R_BIAS:R_BIAS + 2, 0:2, :, :].bitcast(F32), 1.0).then_inc(s_row1, 1)
            dve.wait_ge(s_key, 16 * (1 + batches))
            chain = [0]

            def link(ins):
                chain[0] += 1
                ins.then_inc(s_set, 1)
                dve.wait_ge(s_set, chain[0])

            link(nc.vector.tensor_scalar(m01[:], maski[:], 0.0, None, ALU.not_equal))
            link(nc.vector.tensor_scalar(bias[:], m01[:], -1.0, MASKED, ALU.add, ALU.mult))
            link(nc.vector.tensor_copy(bhi[:].bitcast(F32R), bias[:]))
            link(nc.vector.tensor_tensor(blo[:].bitcast(F32R), bias[:], bhi[:], ALU.subtract))
            dve.wait_ge(s_ktok0, 1)

            def stack_keys(b):
                link(nc.vector.tensor_scalar(kmask[:, b, :], ctok[:, b, :], m01[:, b, :], None, ALU.mult))
                km = kmask[:, b, :].rearrange("k (h d) -> k h d", h=HEADS)
                nc.vector.tensor_copy(ktok[:, b, :, HD:2 * HD].bitcast(F32R), km).then_inc(s_ktok, 1)
                link(nc.vector.tensor_copy(ktok[:, b, :, 0:HD].bitcast(F32R), km))
                nc.vector.tensor_tensor(ktok[:, b, :, 2 * HD:3 * HD].bitcast(F32R), km, ktok[:, b, :, 0:HD], ALU.subtract)\
                  .then_inc(s_ktok, 1)
                nc.vector.tensor_copy(ktok[:, b, :, R_BIAS:R_BIAS + 1], bhi[:, b, :].unsqueeze(1).to_broadcast([P, HEADS, 1]))\
                  .then_inc(s_ktok, 1)
                nc.vector.tensor_copy(ktok[:, b, :, R_BIAS + 1:R_BIAS + 2],
                                      blo[:, b, :].unsqueeze(1).to_broadcast([P, HEADS, 1])).then_inc(s_ktok, 1)

            stack_keys(0)

            def setup(s):
                if 0 < s < batches:
                    stack_keys(s)
                if s == batches:
                    nc.vector.tensor_copy(vals[:], ctok[:].rearrange("k b (g c) -> k (b g) c", g=kchunks)).then_inc(s_vals, 1)
                if s == WT0 - 1:
                    dve.wait_ge(s_load, 16 * N_SETUP_LOADS)
                    link(nc.vector.tensor_scalar(tclip[:], temp[:], 0.1, None, ALU.max))
                    link(nc.vector.reciprocal(tinv[:], tclip[:]))
                c = s - WT0
                if c >= 0:
                    dve.wait_ge(s_woH, c + 1)
                    nc.vector.tensor_tensor(woL[:, c, :], ps[:, B_WT + c % 3, :], woH[:, c, :], ALU.subtract).then_inc(s_woL, 1)

            def maxima(v, g, tiles):
                for t in tiles:
                    dve.wait_ge(mx_ready, 4 * v + t + 1)
                    after(dve, nml_done, v - 1)
                    nc.vector.tensor_reduce(nmax[:, g % 2, t, :],
                                            ps[:, B_MX + t % 2, :].rearrange("p (h k) -> p h k", h=hpg),
                                            axis=AX.X, op=ALU.max, negate=True).then_inc(mx_done, 1)

            def step(i, s):
                d, dn, dg = at(i, s, L_DIV)
                v, n, g = at(i, s, L_MAX)
                if live(d, ntile):
                    dve.wait_ge(rec_done, d + 1)
                    after(dve, at_done, d)
                    nc.vector.tensor_tensor(newton[:], ps[:, B_DEN, :], rden[:, dg % 2, :], ALU.mult).then_inc(newton_done, 1)
                    dve.wait_ge(newton_done, 2 * d + 1)
                    nc.vector.scalar_tensor_tensor(newton[:], newton[:], 2.0, rden[:, dg % 2, :], ALU.subtract, ALU.mult)\
                      .then_inc(newton_done, 1)
                if live(v, ntile):
                    maxima(v, g, (0,))
                if live(d, ntile):
                    _, pn, pg = at(i, s, L_DIV + 2)
                    dve.wait_ge(newton_done, 2 * d + 2)
                    dve.wait_ge(pv_done, d + 1)
                    after(dve, at_out[pg], 16 * (pn + 1))
                    nc.vector.scalar_tensor_tensor(atT[:, dg % 2, :], ps[:, B_NUM, :], -1.0, newton[:], ALU.mult, ALU.mult)\
                      .then_inc(at_done, 1)
                if live(v, ntile):
                    maxima(v, g, (1,))
                w, wn, t = at(i, s, L_STAT)
                if live(w, ntile):
                    dve.wait_ge(x_in[t], 16 * (wn + 1))
                    after(dve, mv_done, w - 3)
                    nc.vector.bn_stats(st1[:, t, :], xin[:, t, :]).then_inc(st_done, 1)
                f, fn, ft = at(i, s, L_NORM)
                if live(f, ntile):
                    dve.wait_ge(rstd_done, 2 * f + 2)
                    after(dve, xlo_done, f - 1)
                    nc.vector.tensor_scalar(xn[:, ft % 2, :], xin[:, ft, :], mv1[:, ft, 0:1], rstd1[:, ft, :],
                                            ALU.subtract, ALU.mult).then_inc(xn_done, 1)
                if live(w, ntile):
                    dve.wait_ge(st_done, w + 1)
                    after(dve, xn_done, w - 3)
                    apart(dve, s_dve)
                    nc.vector.bn_aggr(mv1[:, t, :], st1[:, t, :]).then_inc(mv_done, 1)
                if live(v, ntile):
                    maxima(v, g, (2, 3))

            attention_loop(dve, step, L_DIV, setup)

            RT = 9

            def router_logits(n):
                def link(ins, k):
                    ins.then_inc(rt, 1)
                    dve.wait_ge(rt, RT * n + k)
                dve.wait_ge(q_done, n + 1)
                after(dve, share_done, n)
                link(nc.vector.tensor_tensor(qa[:], qr[:].unsqueeze(2).to_broadcast([P, 4, EXPERTS, 6]),
                                             anc[:].unsqueeze(1).to_broadcast([P, 4, EXPERTS, 6]), ALU.mult), 1)
                link(nc.vector.tensor_reduce(dot[:], qa[:], axis=AX.X, op=ALU.add), 2)
                link(nc.vector.tensor_scalar(dot[:], dot[:], 6.0, 0.5, ALU.subtract, ALU.mult), 3)
                link(nc.vector.tensor_scalar(lgs[:], dot[:], tinv[:], None, ALU.mult), 4)
                link(nc.vector.tensor_reduce(lmax[:], lgs[:], axis=AX.X, op=ALU.max), 5)
                after(dve, lexp_done, n)
                nc.vector.tensor_tensor(ldif[:], lgs[:], lmax[:].unsqueeze(2).to_broadcast([P, 4, EXPERTS]),
                                        ALU.subtract).then_inc(ldif_done, 1)
                mine = lgs[:].unsqueeze(3).to_broadcast([P, 4, EXPERTS, EXPERTS])
                other = lgs[:].unsqueeze(2).to_broadcast([P, 4, EXPERTS, EXPERTS])
                nc.vector.tensor_tensor(gt[:], other, mine, ALU.is_gt).then_inc(rt, 1)
                link(nc.vector.tensor_tensor(eq[:], other, mine, ALU.is_equal), 7)
                link(nc.vector.tensor_tensor(eq[:], eq[:], tri[:].unsqueeze(1).to_broadcast([P, 4, EXPERTS, EXPERTS]),
                                             ALU.mult), 8)
                link(nc.vector.tensor_tensor(gt[:], gt[:], eq[:], ALU.add), 9)

            RW = 4

            def router_weights(n):
                def link(ins, k):
                    ins.then_inc(rw, 1)
                    dve.wait_ge(rw, RW * n + k)
                link(nc.vector.tensor_reduce(rank[:], gt[:], axis=AX.X, op=ALU.add), 1)
                dve.wait_ge(lexp_done, n + 1)
                link(nc.vector.scalar_tensor_tensor(wsel[:], rank[:], 2.0, lexp[:], ALU.is_lt, ALU.mult), 2)
                link(nc.vector.tensor_reduce(wsum[:], wsel[:], axis=AX.X, op=ALU.add), 3)
                link(nc.vector.reciprocal(winv[:], wsum[:]), 4)
                nc.vector.tensor_tensor(wgt[:], wsel[:], winv[:].unsqueeze(2).to_broadcast([P, 4, EXPERTS]), ALU.mult)\
                  .then_inc(w_done, 1)

                link2(nc.vector.tensor_scalar(sel[:], rank[:], 2.0, None, ALU.is_lt), n, 1)
                nc.vector.tensor_tensor(pick[:], rank[:].unsqueeze(1).to_broadcast([P, 2, 4, EXPERTS]),
                                        rank01[:].unsqueeze(2).unsqueeze(3).to_broadcast([P, 2, 4, EXPERTS]),
                                        ALU.is_equal).then_inc(pl, 1)
                link2(nc.vector.tensor_tensor(selb[:], sel[:].rearrange("p t e -> p e t").unsqueeze(1)
                                              .to_broadcast([P, 5, EXPERTS, 4]),
                                              before[:].unsqueeze(2).to_broadcast([P, 5, EXPERTS, 4]), ALU.mult), n, 3)
                nc.vector.tensor_reduce(selc[:], selb[:], axis=AX.X, op=ALU.add).then_inc(sel_done, 1)

            RP = 7

            def link2(ins, n, k):
                ins.then_inc(pl, 1)
                dve.wait_ge(pl, RP * n + k)

            def places(n):
                b, m = in_batch(n)
                dve.wait_ge(pl_ready, n + 1)
                apart(dve, s_dve)
                link2(nc.vector.tensor_tensor(slot[:], ps[:, B_Z, PL0:PL0 + 4 * EXPERTS].rearrange("p (t e) -> p t e", t=4),
                                              used[:, b, at1(m), :].to_broadcast([P, 4, EXPERTS]), ALU.add), n, 4)
                apart(dve, s_dve)
                nc.vector.tensor_tensor(used[:, b, at1(m + 1), :],
                                        ps[:, B_Z, PL0 + 4 * EXPERTS:PL0 + 5 * EXPERTS].unsqueeze(1),
                                        used[:, b, at1(m), :], ALU.add).then_inc(used_done, 1)
                link2(nc.vector.tensor_tensor(pslot[:], pick[:], slot[:].unsqueeze(1).to_broadcast([P, 2, 4, EXPERTS]),
                                              ALU.mult), n, 5)
                link2(nc.vector.tensor_reduce(slot01[:], pslot[:], axis=AX.X, op=ALU.add), n, 6)
                last = int(isinstance(n, int) and n == nblk - 1)
                if not last:
                    after(dve, scattered, 16 * 8 * n)
                nc.vector.tensor_scalar(place_now[:, last, :, :], slot01[:], 0.0, float(batches * rows - 1), ALU.max, ALU.min).then_inc(place_done, 1)
                apart(dve, s_dve)
                nc.vector.tensor_copy(token_now[:, last, :], token[:, at1(m), :].squeeze(1)).then_inc(token_done, 1)
                nc.vector.tensor_tensor(pwgt[:], pick[:], wgt[:].unsqueeze(1).to_broadcast([P, 2, 4, EXPERTS]), ALU.mult)\
                  .then_inc(pl, 1)
                apart(dve, s_dve)
                nc.vector.tensor_copy(place[:, bass.ds(4 * n, 4), :] if not isinstance(n, int) else place[:, 4 * n:4 * n + 4, :],
                                      slot01[:].rearrange("p k t -> p t k")).then_inc(place_done, 1)
                dve.wait_ge(pl, RP * n + 7)
                apart(dve, s_dve)
                nc.vector.tensor_reduce(share[:, bass.ds(4 * n, 4), :] if not isinstance(n, int) else share[:, 4 * n:4 * n + 4, :],
                                        pwgt[:].rearrange("p k t e -> p t k e"), axis=AX.X, op=ALU.add).then_inc(share_done, 1)

            def split(i, g):
                if live(i, nblk):
                    dve.wait_ge(atH_done, 4 * i + g + 1)
                    nc.vector.tensor_tensor(atL[:, g, :], attf[:, g, :], atH[:, g, :], ALU.subtract).then_inc(atL_done, 1)

            def middle(i):
                n = i - 2
                if live(n, nblk):
                    router_logits(n)
                split(i + 1, 0)
                if live(n, nblk):
                    router_weights(n)
                split(i + 1, 1)
                split(i + 1, 2)
                n = i
                if live(n, nblk):
                    dve.wait_ge(xr_in, 16 * (n + 1))
                    after(dve, x2_out, 16 * n)
                    after(dve, xn2_done, 4 * n)
                    for t in range(4):
                        dve.wait_ge(out_ready, 4 * n + t + 1)
                        nc.vector.tensor_tensor(x2[:, t, :], ps[:, B_OUT + t, :], xres[:, t, :], ALU.add).then_inc(add_done, 1)
                    for t in range(4):
                        dve.wait_ge(add_done, 4 * n + t + 1)
                        after(dve, mv2_done, 4 * n)
                        nc.vector.bn_stats(st2[:, t, :], x2[:, t, :]).then_inc(st2_done, 1)
                    for t in range(4):
                        dve.wait_ge(st2_done, 4 * n + t + 1)
                        apart(dve, s_dve)
                        nc.vector.bn_aggr(mv2[:, t, :], st2[:, t, :]).then_inc(mv2_done, 1)
                split(i + 1, 3)
                n = i - 2
                if live(n, nblk):
                    places(n)
                if isinstance(i, int) and i == blk_per_batch + 2:
                    tiles_of_experts(0)
                    experts_of_tiles(0)
                if isinstance(i, int) and i == blk_per_batch + 3:
                    rows_of_tiles(0)
                    table(0)
                if isinstance(i, int) and i == blk_per_batch + 4:
                    rows_of_tokens(0)

            tabs = [0]

            def link(ins):
                tabs[0] += 1
                ins.then_inc(tb, 1)
                dve.wait_ge(tb, tabs[0])

            full = [P, NT, EXPERTS]

            def tiles_of_experts(b):
                dve.wait_ge(used_done, (b + 1) * blk_per_batch)
                link(nc.vector.tensor_tensor(cnt[:], used[:, b, blk_per_batch, :], used[:, b, 0, :], ALU.subtract))
                link(nc.vector.tensor_tensor(ncmp[:], cnt[:].unsqueeze(2).to_broadcast([P, EXPERTS, btiles]),
                                             steps[:].unsqueeze(1).to_broadcast([P, EXPERTS, btiles]), ALU.is_gt))
                link(nc.vector.tensor_reduce(ntil[:], ncmp[:], axis=AX.X, op=ALU.add))
                link(nc.vector.tensor_tensor(nbef[:], ntil[:].unsqueeze(1).to_broadcast([P, EXPERTS, EXPERTS]), tri[:], ALU.mult))
                link(nc.vector.tensor_reduce(first[:], nbef[:], axis=AX.X, op=ALU.add))

            def experts_of_tiles(b):
                firsts = first[:].unsqueeze(1).to_broadcast(full)
                link(nc.vector.tensor_tensor(tcmp[:], firsts, tileno[:].unsqueeze(2).to_broadcast(full), ALU.is_le))
                link(nc.vector.tensor_reduce(texp[:], tcmp[:], axis=AX.X, op=ALU.add))
                link(nc.vector.tensor_tensor(tsel[:], tcmp[:], firsts, ALU.mult))
                link(nc.vector.tensor_reduce(tfirst[:], tsel[:], axis=AX.X, op=ALU.max))
                link(nc.vector.tensor_scalar(texp[:], texp[:], 1.0, None, ALU.subtract))

            def rows_of_tiles(b):
                link(nc.vector.tensor_tensor(tcmp[:], expno[:].unsqueeze(1).to_broadcast(full),
                                             texp[:].unsqueeze(2).to_broadcast(full), ALU.is_equal))
                link(nc.vector.tensor_tensor(tsel[:], tcmp[:], used[:, b, 0:1, :].to_broadcast(full), ALU.mult))
                link(nc.vector.tensor_reduce(trow[:], tsel[:], axis=AX.X, op=ALU.add))
                link(nc.vector.tensor_tensor(tfirst[:], tileno[:], tfirst[:], ALU.subtract))
                link(nc.vector.scalar_tensor_tensor(trow[:], tfirst[:], float(P), trow[:], ALU.mult, ALU.add))

            def table(b):
                if b == 0:
                    link(nc.vector.memset(tab_row[:, tiles:].bitcast(F32), 0.0))
                    link(nc.vector.memset(tab_col[:].bitcast(F32), 0.0))
                nc.vector.tensor_copy(tab_row[:, b * NT:(b + 1) * NT], trow[:]).then_inc(tab_done, 1)
                nc.vector.tensor_scalar(tab_col[:, L_DN + b * NT:L_DN + (b + 1) * NT], texp[:], float(wexp), None, ALU.mult)\
                  .then_inc(tab_done, 1)
                link(nc.vector.scalar_tensor_tensor(offset[:], first[:], float(P), used[:, b, 0, :], ALU.mult, ALU.subtract))
                link(nc.vector.tensor_copy(shift[:, 0:1], offset[:, 0:1]))
                link(nc.vector.tensor_tensor(shift[:, 1:EXPERTS], offset[:, 1:EXPERTS], offset[:, 0:EXPERTS - 1], ALU.subtract))
                link(nc.vector.tensor_scalar(bounds[:], expno[:], float(region), float(b * rows), ALU.mult, ALU.add))

            def rows_of_tokens(b):
                dve.wait_ge(place_done, 2 * (b + 1) * blk_per_batch)
                mine = place[:, b * btiles:(b + 1) * btiles, :].rearrange("p t k -> p (t k)")
                each = [P, 2 * btiles, EXPERTS]
                link(nc.vector.tensor_tensor(within[:], mine.unsqueeze(2).to_broadcast(each),
                                             bounds[:].unsqueeze(1).to_broadcast(each), ALU.is_ge))
                link(nc.vector.tensor_tensor(within[:], within[:], shift[:].unsqueeze(1).to_broadcast(each), ALU.mult))
                link(nc.vector.tensor_reduce(moved[:], within[:], axis=AX.X, op=ALU.add))
                nc.vector.tensor_tensor(out_row[:, b * btiles:(b + 1) * btiles, :].rearrange("p t k -> p (t k)"),
                                        mine, moved[:], ALU.add).then_inc(tab_done, 1)

            for g in range(4):
                split(0, g)
            middle_loop(dve, middle)

            def stage(c, q):
                k, n = q
                after(dve, yg_in[k], 32 * n)
                apart(dve, s_dve)
                nc.vector.tensor_copy(sidx[:, k, :], out_row[:, at1(c), :].squeeze(1)).then_inc(sidx_done[k], 1)
                after(dve, cmb_done[k], n)
                apart(dve, s_dve)
                nc.vector.tensor_copy(wst[:, k, :], share[:, at1(c), :].squeeze(1)).then_inc(sidx_done[k], 1)

            def add(x, q):
                k, n = q
                dve.wait_ge(yg_in[k], 32 * (n + 1))
                dve.wait_ge(sidx_done[k], 2 * n + 2)
                apart(dve, s_dve)
                nc.vector.scalar_tensor_tensor(x, yg[:, k, 0, :], wst[:, k, 0:1], x, ALU.mult, ALU.add)\
                  .then_inc(half_done[k], 1)
                dve.wait_ge(half_done[k], n + 1)
                apart(dve, s_dve)
                nc.vector.scalar_tensor_tensor(x, yg[:, k, 1, :], wst[:, k, 1:2], x, ALU.mult, ALU.add)\
                  .then_inc(cmb_done[k], 1)

            def experts(i, combine=True):
                for k in range(TPI):
                    w, p, n = tl(i, k, L_T)
                    if live(w, tiles):
                        dve.wait_ge(xh_done, w + 1)
                        nc.vector.tensor_tensor(xgL[:, p, :, :], ps[:, B_X + p, :].rearrange("p (k t) -> p k t", k=kchunks),
                                                xgH[:, p, :, :], ALU.subtract).then_inc(xl_done, 1)
                    w, p, n = tl(i, k, L_HT)
                    if live(w, tiles):
                        dve.wait_ge(hh_done, w + 1)
                        nc.vector.tensor_tensor(hL[:, p, :, :], ps[:, B_H + p, 0:HID].rearrange("p (j t) -> p j t", j=halves),
                                                hH[:, p, :, :], ALU.subtract).then_inc(hl_done, 1)
                    w, p, n = tl(i, k, L_DN)
                    if live(w, tiles):
                        dve.wait_ge(y_ready, w + 1)
                        after(dve, y_out[p], 16 * n)
                        nc.vector.tensor_copy(ysb[:, p, :], ps[:, B_Y + p, :]).then_inc(yc_done, 1)
                    if isinstance(i, int) and (i, k) == (1, 0):
                        tiles_of_experts(1)
                    if isinstance(i, int) and (i, k) == (1, 1):
                        experts_of_tiles(1)
                    if isinstance(i, int) and (i, k) == (1, 2):
                        rows_of_tiles(1)
                    if isinstance(i, int) and (i, k) == (1, 3):
                        table(1)
                    if isinstance(i, int) and (i, k) == (2, 0):
                        rows_of_tokens(1)
                    q = k - 1
                    if combine and 0 <= q < CPI:
                        j = i - C0 - 1
                        if live(j, btiles // CPI):
                            dve.wait_ge(x2c_in[q], 16 * (j + 1))
                            add(x2c[:, q, :], (q, j))
                        j = i - C0
                        if live(j, btiles // CPI):
                            stage(CPI * j + q, (q, j))

            dve.wait_ge(share_done, nblk)
            expert_loop(dve, experts)

            dve.wait_ge(x2t_in, 16 * btiles)

            def put_together(j):
                for k in range(TAIL):
                    c = TAIL * (j - 1) + k
                    if live(j - 1, btiles // TAIL):
                        add(x2t[:, at1(c), :].squeeze(1), (k, combined[k] + j - 1))
                    c = TAIL * j + k
                    if live(j, btiles // TAIL):
                        stage(btiles + c, (k, combined[k] + j))

            combine_loop(dve, put_together)

        @block.tensor
        def _(pe):
            mm = nc.tensor.matmul
            pe.wait_ge(s_ident, 2)

            def setup(s):
                b, g = s // kchunks, s % kchunks
                pe.wait_ge(s_ktok, 4 * (b + 1))
                pe.wait_ge(s_set, 4 + 2 * (b + 1))
                after(pe, s_kss, s - 2)
                for h in range(hpg):
                    last = nc.tensor.transpose(ps[:, B_KT + s % 3, h * keys:(h + 1) * keys], ktok[:, b, g * hpg + h, :], ident[:])
                last.then_inc(s_kT, 1)
                c = s - WT0
                if c >= 0:
                    if c == 0:
                        pe.wait_ge(s_load, 16 * N_SETUP_LOADS)
                    after(pe, s_woL, c - 2)
                    for r in range(kchunks):
                        last = nc.tensor.transpose(ps[:, B_WT + c % 3, r * P:(r + 1) * P], woraw[:, r, c * P:(c + 1) * P], ident[:])
                    last.then_inc(s_woT, 1)
                if c == kchunks - 1:
                    pe.wait_ge(s_woL, 2)
                    for r in range(kchunks):
                        last = nc.tensor.transpose(ps[:, B_WT + 1, r * EXPERTS:(r + 1) * EXPERTS], pjraw[:, r * P:(r + 1) * P],
                                                   ident[0:EXPERTS, 0:EXPERTS])
                    last.then_inc(s_pjT, 1)
                    pe.wait_ge(s_kss, batches * kchunks)
                    pe.wait_ge(s_woL, kchunks)
                    pe.wait_ge(s_pj, 1)
                    pe.wait_ge(s_const, 3)
                    pe.wait_ge(s_pos, 10 + batches)
                    pe.wait_ge(s_gap, 4 + kchunks)
                    pe.wait_ge(s_vals, 1)

            def scores_by_token(v, stack, g, tiles):
                for t in tiles:
                    after(pe, mx_done, 4 * v + t - 1)
                    for h in range(hpg):
                        o, c = h // 2 * 2 * keys, (h // 2 * 3 + h % 2) * keys
                        last = mm(ps[:, B_MX + t % 2, o:o + 2 * keys], qst[0:R_MAX, g, h, t * P:(t + 1) * P],
                                  kss[0:R_MAX, stack, c:c + 2 * keys], start=(h % 2 == 0), stop=(h % 2 == 1))
                    last.then_inc(mx_ready, 1)

            def scores_by_key(v, stack, g, heads):
                for h in heads:
                    after(pe, exp_done, hpg * v + h - 1)
                    c = (h // 2 * 3 + h % 2 * 2) * keys
                    mm(ps[:, B_SC + h % 2, :], kss[0:ROWS, stack, c:c + keys], qst[0:ROWS, g, h, :], start=True, stop=True)\
                        .then_inc(sc_ready, 1)

            def step(i, s):
                v, n, g = at(i, s, L_SC)
                stack = batch_of(s, L_SC) * kchunks + g
                if live(v, ntile):
                    pe.wait_ge(m_in[g], 16 * (n + 1))
                    scores_by_key(v, stack, g, (0, 1))
                a, an, ag = at(i, s, L_MAX)
                astack = batch_of(s, L_MAX) * kchunks + ag
                if live(a, ntile):
                    pe.wait_ge(q_in[ag], 48 * (an + 1))
                    scores_by_token(a, astack, ag, (0, 1))
                m, mn, mg = at(i, s, L_MT)
                if live(m, ntile):
                    w = at(i, s, L_TR + 1)[0]
                    pe.wait_ge(nml_done, m + 1)
                    pe.wait_ge(qtl_done, min(w + 1, ntile) if isinstance(w, int) else w + 1)
                    for t in range(4):
                        last = nc.tensor.transpose(ps[0:2 * hpg, B_TL, t * P:(t + 1) * P], nmhl[:, mg % 2, t, :], ident[:])
                    last.then_inc(mt_ready, 1)
                if live(v, ntile):
                    scores_by_key(v, stack, g, (2, 3))
                w, n, t = at(i, s, L_TR)
                if live(w, ntile):
                    pe.wait_ge(xhi_done, w + 1)
                    after(pe, qth_done, w)
                    for c in range(kchunks):
                        last = nc.tensor.transpose(ps[:, B_TH, c * P:(c + 1) * P], xhi[:, t % 2, c * P:(c + 1) * P], ident[:])
                    last.then_inc(th_ready, 1)
                    pe.wait_ge(xlo_done, w + 1)
                    after(pe, qtl_done, w)
                    if live(m, ntile):
                        pe.wait_ge(mt_done, m + 1)
                    for c in range(kchunks):
                        last = nc.tensor.transpose(ps[:, B_TL, c * P:(c + 1) * P], xlo[:, t % 2, c * P:(c + 1) * P], ident[:])
                    last.then_inc(tl_ready, 1)
                if live(a, ntile):
                    scores_by_token(a, astack, ag, (2, 3))
                v, n, g = at(i, s, L_PV)
                stack = batch_of(s, L_PV) * kchunks + g
                if live(v, ntile):
                    pe.wait_ge(exp_done, hpg * v + hpg)
                    after(pe, newton_done, 2 * v - 1)
                    for h in range(hpg):
                        last = mm(ps[h * HD:(h + 1) * HD, B_DEN, :], ones[:], prob[:, g % 2, h, :], start=True, stop=True)
                    last.then_inc(sums_ready, 1)
                    after(pe, at_done, v)
                    for h in range(hpg):
                        last = mm(ps[h * HD:(h + 1) * HD, B_NUM, :], vals[:, stack, h * HD:(h + 1) * HD], prob[:, g % 2, h, :],
                                  start=True, stop=True)
                    last.then_inc(pv_done, 1)

            attention_loop(pe, step, L_PV, setup)

            def project(n, g):
                if live(n, nblk):
                    pe.wait_ge(atH_done, 4 * n + g + 1)
                    pe.wait_ge(atL_done, 4 * n + g + 1)
                    for t in range(4):
                        if g == 0:
                            after(pe, add_done, 4 * (n - 1) + t + 1)
                        o = ps[:, B_OUT + t, :]
                        mm(o, atH[:, g, t * P:(t + 1) * P], woH[:, g, :], start=(g == 0), stop=False)
                        mm(o, atH[:, g, t * P:(t + 1) * P], woL[:, g, :], start=False, stop=False)
                        last = mm(o, atL[:, g, t * P:(t + 1) * P], woH[:, g, :], start=False, stop=(g == 3))
                        if g == 3:
                            last.then_inc(out_ready, 1)
                    if g < 3:
                        last.then_inc(wo_done, 1)

            def rows_transposed(n, tiles):
                if live(n, nblk):
                    for t in tiles:
                        pe.wait_ge(xn2_done, 4 * n + t + 1)
                        after(pe, t2_done, 4 * n + t - 1)
                        for c in range(kchunks):
                            last = nc.tensor.transpose(ps[:, B_T2 + t % 2, c * P:(c + 1) * P], xn2[:, t, c * P:(c + 1) * P],
                                                       ident[:])
                        last.then_inc(t2_ready, 1)

            def middle(i):
                project(i, 0)
                n = i - 2
                if live(n, nblk):
                    pe.wait_ge(t2_done, 4 * n + 4)
                    after(pe, zp_done, n)
                    for c in range(kchunks):
                        last = mm(ps[c * HD:(c + 1) * HD, B_ZP, :], projT[:, c, :], x2T[:, :, c, :], start=True, stop=True)
                    last.then_inc(zp_ready, 1)
                project(i, 1)
                if live(n, nblk):
                    pe.wait_ge(zp_done, n + 1)
                    after(pe, used_done, n)
                    for t in range(4):
                        last = mm(ps[:, B_Z, t * EXPERTS:(t + 1) * EXPERTS], zpart[:, t * P:(t + 1) * P], fold[:],
                                  start=True, stop=True)
                    last.then_inc(z_ready, 1)
                project(i, 2)
                rows_transposed(i - 1, (0, 1))
                project(i, 3)
                rows_transposed(i - 1, (2, 3))
                if live(n, nblk):
                    pe.wait_ge(sel_done, n + 1)
                    mm(ps[:, B_Z, PL0:PL0 + 5 * EXPERTS], allones[:], selc[:].rearrange("p t e -> p (t e)"),
                       start=True, stop=False)
                    mm(ps[:, B_Z, PL0:PL0 + 4 * EXPERTS], earlier[:], sel[:].rearrange("p t e -> p (t e)"),
                       start=False, stop=True).then_inc(pl_ready, 1)

            middle_loop(pe, middle)

            pe.wait_ge(wL_done, 2 * EXPERTS)
            pe.wait_ge(tab_done, 3)
            w1h, w1l = (w[:].rearrange("p e k h -> p (e k h)") for w in (w1H, w1L))
            w2h, w2l = (w[:].rearrange("p e j d -> p (e j d)") for w in (w2H, w2L))

            col_regs = [pe.alloc_register(f"col{k}") for k in range(TPI + L_DN - L_UP)]
            ncols = len(col_regs)

            def experts(i, combine=True):
                if isinstance(i, int) and i == NT // TPI:
                    pe.wait_ge(tab_done, 6)
                pe.load(col_regs, tab_col[0:1, TPI * i:TPI * i + ncols] if isinstance(i, int) else
                        tab_col[0:1, bass.ds(TPI * i, ncols)])
                col = [pe.snap(r, min_val=0, max_val=wexp * (EXPERTS - 1)) for r in col_regs]
                for k in range(TPI):
                    w, p, n = tl(i, k, L_T)
                    if live(w, tiles):
                        _, r, fetched = tl(i, k, L_T, 4)
                        pe.wait_ge(xg_in[r], 16 * (fetched + 1))
                        after(pe, xl_done, w - 1)
                        for c in range(kchunks):
                            last = nc.tensor.transpose(ps[:, B_X + p, c * P:(c + 1) * P], xg[:, r, c * P:(c + 1) * P], ident[:])
                        last.then_inc(xt_ready, 1)
                    w, p, n = tl(i, k, L_UP)
                    if live(w, tiles):
                        pe.wait_ge(xl_done, w + 1)
                        after(pe, gel_done, w - 1)
                        e = col[k + L_DN - L_UP]
                        o = ps[:, B_UP + p, 0:HID]
                        for c in range(kchunks):
                            cols = bass.ds(e + c * HID, HID)
                            mm(o, xgH[:, p, c, :], w1h[:, cols], start=(c == 0), stop=False)
                            mm(o, xgL[:, p, c, :], w1h[:, cols], start=False, stop=False)
                            last = mm(o, xgH[:, p, c, :], w1l[:, cols], start=False, stop=(c == kchunks - 1))
                        last.then_inc(up_ready, 1)
                    w, p, n = tl(i, k, L_HT)
                    if live(w, tiles):
                        pe.wait_ge(gel_done, w + 1)
                        after(pe, hl_done, w - 1)
                        for c in range(halves):
                            last = nc.tensor.transpose(ps[:, B_H + p, c * P:(c + 1) * P], gel[:, p, c * P:(c + 1) * P], ident[:])
                        last.then_inc(ht_ready, 1)
                    w, p, n = tl(i, k, L_DN)
                    if live(w, tiles):
                        pe.wait_ge(hl_done, w + 1)
                        after(pe, yc_done, w - 1)
                        e = col[k]
                        o = ps[:, B_Y + p, :]
                        for c in range(halves):
                            cols = bass.ds(e + c * emb, emb)
                            mm(o, hH[:, p, c, :], w2h[:, cols], start=(c == 0), stop=False)
                            mm(o, hL[:, p, c, :], w2h[:, cols], start=False, stop=False)
                            last = mm(o, hH[:, p, c, :], w2l[:, cols], start=False, stop=(c == halves - 1))
                        last.then_inc(y_ready, 1)

            expert_loop(pe, experts)


_INS = ["x", "ctx_1024", "mask_Bx1x1xS2_ik0", "L0_xattn_W_out", "L0_ffn_proj_w", "L0_ffn_anchors",
        "L0_ffn_routing_temp", "L0_ffn_w1", "L0_ffn_w2"]


def kernel(**inputs):
    import numpy as np
    import concourse.bacc as bacc
    from concourse.bass_utils import run_bass_kernel_spmd

    nc = bacc.Bacc("TRN2", target_bir_lowering=False, num_devices=1)
    arrays, args = {}, []
    for name in _INS:
        a = np.ascontiguousarray(inputs[name])
        arrays[f"in_{name}"] = a
        args.append(nc.dram_tensor(f"in_{name}", a.shape, mybir.dt.from_np(a.dtype), kind="ExternalInput").ap())
    shape = arrays["in_x"].shape
    args.append(nc.dram_tensor("out_x", shape, F32, kind="ExternalOutput").ap())
    xattn_moe(nc, *args)
    r = run_bass_kernel_spmd(nc, [arrays], core_ids=[0])
    return r.results[0]["out_x"]
```
